# Optimizing a Trainium2 kernel written in Bass

```python
import numpy as np
import jax
import jax.numpy as jnp

def _softmax(x, axis=-1):
    return jax.nn.softmax(x, axis=axis)

def _gelu(x):
    return jax.nn.gelu(x, approximate=True)

def _silu(x):
    return jax.nn.silu(x)

def _sigmoid(x):
    return jax.nn.sigmoid(x)

def _layernorm(x, axis=-1, eps=1e-05):
    m = jnp.mean(x, axis=axis, keepdims=True)
    v = jnp.var(x, axis=axis, keepdims=True)
    return (x - m) / jnp.sqrt(v + eps)

def _scatter_add(tgt, idx, src, axis=0):
    return tgt.at[idx].add(src)

def _segment_sum(src, seg, n):
    return jax.ops.segment_sum(src, seg, n)
kernel_name = 'mk_vit_tower_d1_tok_img1024_r4_81ce07'

def setup_inputs(seed: int=0):
    np.random.seed(seed)
    _w = jnp.asarray

    def _rec_inputs():
        import jax
        import jax.numpy as jnp
        _rk = jax.random.key(seed)
        x = -0.000125008 + 0.999885 * jax.random.normal(jax.random.fold_in(_rk, 1), (8, 64, 64, 64), jnp.float32)
        return x
    x = _rec_inputs()

    def _L0_tok_setup():
        import jax, jax.numpy as jnp
        import numpy as np
        C_IN = 64
        HIDDEN = 1024
        OUT = 256
        R = 2
        EPS = 1e-05

        def _xavier(key, fan_in, fan_out):
            limit = float(np.sqrt(6.0 / (fan_in + fan_out)))
            return jax.random.uniform(key, (fan_in, fan_out), jnp.float32, -limit, limit)

        def _pixel_unshuffle_tokens(x):
            B, C, H, W = x.shape
            h_pad, w_pad = ((R - H % R) % R, (R - W % R) % R)
            if h_pad or w_pad:
                x = jnp.pad(x, ((0, 0), (0, 0), (0, h_pad), (0, w_pad)))
                H, W = (H + h_pad, W + w_pad)
            Hr, Wr = (H // R, W // R)
            x = x.reshape(B, C, Hr, R, Wr, R)
            x = x.transpose(0, 2, 4, 1, 3, 5)
            return x.reshape(B, Hr * Wr, C * R * R)
        key = jax.random.key(seed)
        kx, k1, k2 = jax.random.split(key, 3)
        shuf = C_IN * R * R
        x = jax.random.normal(kx, (32, C_IN, 64, 64), jnp.float32)
        w1 = _xavier(k1, shuf, HIDDEN)
        b1 = jnp.zeros((HIDDEN,), jnp.float32)
        w2 = _xavier(k2, HIDDEN, OUT)
        b2 = jnp.zeros((OUT,), jnp.float32)
        gamma = jnp.ones((OUT,), jnp.float32)
        beta = jnp.zeros((OUT,), jnp.float32)
        return {'x': x, 'w1': w1, 'b1': b1, 'w2': w2, 'b2': b2, 'gamma': gamma, 'beta': beta}
    _L0_tok_all = _L0_tok_setup()
    _L0_tok_in = {k: v for k, v in _L0_tok_all.items() if k in ('w1', 'b1', 'w2', 'b2', 'gamma', 'beta')}
    del _L0_tok_all

    def _L0_attn_setup():
        import jax, jax.numpy as jnp
        import numpy as np
        from jax import lax
        D_MODEL = 256
        D_STATE = 128
        D_CONV = 4
        EXPAND = 2
        HEADDIM = 64
        D_INNER = EXPAND * D_MODEL
        NHEADS = D_INNER // HEADDIM
        CONV_DIM = D_INNER + 2 * D_STATE
        D_IN_PROJ = 2 * D_INNER + 2 * D_STATE + NHEADS
        EPS = 1e-05

        def _ssm_forward(x, in_proj_w, conv_w, conv_b, norm_w, out_proj_w, dt_bias, A_log, D_param):
            B, L, _ = x.shape
            zxbcdt = jnp.einsum('bld,ed->ble', x, in_proj_w)
            z = zxbcdt[..., :D_INNER]
            xBC = zxbcdt[..., D_INNER:D_INNER + CONV_DIM]
            dt = zxbcdt[..., D_INNER + CONV_DIM:]
            xBC_c = lax.conv_general_dilated(xBC.transpose(0, 2, 1), conv_w, window_strides=(1,), padding=[(D_CONV - 1, 0)], feature_group_count=CONV_DIM, dimension_numbers=('NCH', 'OIH', 'NCH'))
            xBC = jax.nn.silu((xBC_c + conv_b[None, :, None]).transpose(0, 2, 1))
            x_part = xBC[..., :D_INNER]
            B_part = xBC[..., D_INNER:D_INNER + D_STATE]
            C_part = xBC[..., D_INNER + D_STATE:]
            x_heads = x_part.reshape(B, L, NHEADS, HEADDIM)
            dt = jax.nn.softplus(dt + dt_bias)
            A = -jnp.exp(A_log)

            def step(state, inp):
                x_t, B_t, C_t, dt_t = inp
                decay = jnp.exp(A[None, :] * dt_t)
                state = state * decay[:, :, None, None] + (x_t * dt_t[:, :, None])[..., None] * B_t[:, None, None, :]
                y_t = jnp.einsum('bhpn,bn->bhp', state, C_t)
                return (state, y_t)
            state0 = jnp.zeros((B, NHEADS, HEADDIM, D_STATE), dtype=x.dtype)
            inputs = (jnp.moveaxis(x_heads, 1, 0), jnp.moveaxis(B_part, 1, 0), jnp.moveaxis(C_part, 1, 0), jnp.moveaxis(dt, 1, 0))
            _, y_seq = lax.scan(step, state0, inputs)
            y = jnp.moveaxis(y_seq, 0, 1).reshape(B, L, D_INNER)
            D_full = jnp.repeat(D_param, HEADDIM)
            y = y + x_part * D_full
            y = y * jax.nn.silu(z)
            y = y * jax.lax.rsqrt(jnp.mean(y * y, axis=-1, keepdims=True) + EPS) * norm_w
            return jnp.einsum('ble,de->bld', y, out_proj_w)
        key = jax.random.key(seed)
        ks = jax.random.split(key, 8)
        B, L = (2, 512)
        x = jax.random.normal(ks[0], (B, L, D_MODEL), dtype=jnp.float32)
        in_proj_w = jax.random.normal(ks[1], (D_IN_PROJ, D_MODEL), dtype=jnp.float32) * 0.02
        conv_w = jax.random.normal(ks[2], (CONV_DIM, 1, D_CONV), dtype=jnp.float32) * 0.2
        conv_b = jax.random.normal(ks[3], (CONV_DIM,), dtype=jnp.float32) * 0.02
        norm_w = jnp.ones((D_INNER,), dtype=jnp.float32)
        out_proj_w = jax.random.normal(ks[4], (D_MODEL, D_INNER), dtype=jnp.float32) * 0.02
        dt_bias = jax.random.normal(ks[5], (NHEADS,), dtype=jnp.float32) * 0.1
        A_log = jax.random.normal(ks[6], (NHEADS,), dtype=jnp.float32) * 0.1
        D_param = jnp.ones((NHEADS,), dtype=jnp.float32)
        return {'x': x, 'in_proj_w': in_proj_w, 'conv_w': conv_w, 'conv_b': conv_b, 'norm_w': norm_w, 'out_proj_w': out_proj_w, 'dt_bias': dt_bias, 'A_log': A_log, 'D_param': D_param}
    _L0_attn_all = _L0_attn_setup()
    _L0_attn_in = {k: v for k, v in _L0_attn_all.items() if k in ('in_proj_w', 'conv_w', 'conv_b', 'norm_w', 'out_proj_w', 'dt_bias', 'A_log', 'D_param')}
    del _L0_attn_all

    def _L0_ffn_setup():
        import jax, jax.numpy as jnp
        import numpy as np
        B, S, H, F, G = (8, 512, 256, 1024, 128)
        EPS = 1e-05

        def _dequant(q, scales, g):
            K, N = q.shape
            w = (q.astype(jnp.float32) - 128.0).reshape(K // g, g, N) * scales[:, None, :]
            return w.reshape(K, N)
        key = jax.random.key(seed)
        ks = jax.random.split(key, 8)
        x = jax.random.normal(ks[0], (B, S, H), dtype=jnp.float32)
        ln_gamma = jnp.ones((H,), jnp.float32)
        ln_beta = jnp.zeros((H,), jnp.float32)
        fc1_q = jax.random.randint(ks[1], (H, F), 0, 64, dtype=jnp.int32)
        fc2_q = jax.random.randint(ks[2], (F, H), 0, 64, dtype=jnp.int32)
        fc1_scales = jax.random.uniform(ks[3], (H // G, F), jnp.float32) * 0.02 + 0.001
        fc2_scales = jax.random.uniform(ks[4], (F // G, H), jnp.float32) * 0.02 + 0.001
        fc1_bias = jax.random.normal(ks[5], (F,), jnp.float32) * 0.02
        fc2_bias = jax.random.normal(ks[6], (H,), jnp.float32) * 0.02
        return {'x': x, 'ln_gamma': ln_gamma, 'ln_beta': ln_beta, 'fc1_q': fc1_q, 'fc1_scales': fc1_scales, 'fc1_bias': fc1_bias, 'fc2_q': fc2_q, 'fc2_scales': fc2_scales, 'fc2_bias': fc2_bias}
    _L0_ffn_all = _L0_ffn_setup()
    _L0_ffn_in = {k: v for k, v in _L0_ffn_all.items() if k in ('ln_gamma', 'ln_beta', 'fc1_q', 'fc1_scales', 'fc1_bias', 'fc2_q', 'fc2_scales', 'fc2_bias')}
    del _L0_ffn_all
    return {'x': x, 'L0_tok_w1': _L0_tok_in['w1'], 'L0_tok_b1': _L0_tok_in['b1'], 'L0_tok_w2': _L0_tok_in['w2'], 'L0_tok_b2': _L0_tok_in['b2'], 'L0_tok_gamma': _L0_tok_in['gamma'], 'L0_tok_beta': _L0_tok_in['beta'], 'L0_attn_in_proj_w': _L0_attn_in['in_proj_w'], 'L0_attn_conv_w': _L0_attn_in['conv_w'], 'L0_attn_conv_b': _L0_attn_in['conv_b'], 'L0_attn_norm_w': _L0_attn_in['norm_w'], 'L0_attn_out_proj_w': _L0_attn_in['out_proj_w'], 'L0_attn_dt_bias': _L0_attn_in['dt_bias'], 'L0_attn_A_log': _L0_attn_in['A_log'], 'L0_attn_D_param': _L0_attn_in['D_param'], 'L0_ffn_ln_gamma': _L0_ffn_in['ln_gamma'], 'L0_ffn_ln_beta': _L0_ffn_in['ln_beta'], 'L0_ffn_fc1_q': _L0_ffn_in['fc1_q'], 'L0_ffn_fc1_scales': _L0_ffn_in['fc1_scales'], 'L0_ffn_fc1_bias': _L0_ffn_in['fc1_bias'], 'L0_ffn_fc2_q': _L0_ffn_in['fc2_q'], 'L0_ffn_fc2_scales': _L0_ffn_in['fc2_scales'], 'L0_ffn_fc2_bias': _L0_ffn_in['fc2_bias']}

def reference(x, L0_tok_w1, L0_tok_b1, L0_tok_w2, L0_tok_b2, L0_tok_gamma, L0_tok_beta, L0_attn_in_proj_w, L0_attn_conv_w, L0_attn_conv_b, L0_attn_norm_w, L0_attn_out_proj_w, L0_attn_dt_bias, L0_attn_A_log, L0_attn_D_param, L0_ffn_ln_gamma, L0_ffn_ln_beta, L0_ffn_fc1_q, L0_ffn_fc1_scales, L0_ffn_fc1_bias, L0_ffn_fc2_q, L0_ffn_fc2_scales, L0_ffn_fc2_bias):
    import jax
    import jax.numpy as jnp

    def _L0_tok_ref(x, w1, b1, w2, b2, gamma, beta):
        import jax, jax.numpy as jnp
        import numpy as np
        C_IN = 64
        HIDDEN = 1024
        OUT = 256
        R = 2
        EPS = 1e-05

        def _xavier(key, fan_in, fan_out):
            limit = float(np.sqrt(6.0 / (fan_in + fan_out)))
            return jax.random.uniform(key, (fan_in, fan_out), jnp.float32, -limit, limit)

        def _pixel_unshuffle_tokens(x):
            B, C, H, W = x.shape
            h_pad, w_pad = ((R - H % R) % R, (R - W % R) % R)
            if h_pad or w_pad:
                x = jnp.pad(x, ((0, 0), (0, 0), (0, h_pad), (0, w_pad)))
                H, W = (H + h_pad, W + w_pad)
            Hr, Wr = (H // R, W // R)
            x = x.reshape(B, C, Hr, R, Wr, R)
            x = x.transpose(0, 2, 4, 1, 3, 5)
            return x.reshape(B, Hr * Wr, C * R * R)
        t = _pixel_unshuffle_tokens(x)
        h = jax.nn.gelu(jnp.einsum('btc,ch->bth', t, w1) + b1, approximate=False)
        y = jnp.einsum('bth,ho->bto', h, w2) + b2
        mu = jnp.mean(y, axis=-1, keepdims=True)
        var = jnp.mean(jnp.square(y - mu), axis=-1, keepdims=True)
        return (y - mu) * jax.lax.rsqrt(var + EPS) * gamma + beta

    def _L0_attn_ref(x, in_proj_w, conv_w, conv_b, norm_w, out_proj_w, dt_bias, A_log, D_param):
        import jax, jax.numpy as jnp
        import numpy as np
        from jax import lax
        D_MODEL = 256
        D_STATE = 128
        D_CONV = 4
        EXPAND = 2
        HEADDIM = 64
        D_INNER = EXPAND * D_MODEL
        NHEADS = D_INNER // HEADDIM
        CONV_DIM = D_INNER + 2 * D_STATE
        D_IN_PROJ = 2 * D_INNER + 2 * D_STATE + NHEADS
        EPS = 1e-05

        def _ssm_forward(x, in_proj_w, conv_w, conv_b, norm_w, out_proj_w, dt_bias, A_log, D_param):
            B, L, _ = x.shape
            zxbcdt = jnp.einsum('bld,ed->ble', x, in_proj_w)
            z = zxbcdt[..., :D_INNER]
            xBC = zxbcdt[..., D_INNER:D_INNER + CONV_DIM]
            dt = zxbcdt[..., D_INNER + CONV_DIM:]
            xBC_c = lax.conv_general_dilated(xBC.transpose(0, 2, 1), conv_w, window_strides=(1,), padding=[(D_CONV - 1, 0)], feature_group_count=CONV_DIM, dimension_numbers=('NCH', 'OIH', 'NCH'))
            xBC = jax.nn.silu((xBC_c + conv_b[None, :, None]).transpose(0, 2, 1))
            x_part = xBC[..., :D_INNER]
            B_part = xBC[..., D_INNER:D_INNER + D_STATE]
            C_part = xBC[..., D_INNER + D_STATE:]
            x_heads = x_part.reshape(B, L, NHEADS, HEADDIM)
            dt = jax.nn.softplus(dt + dt_bias)
            A = -jnp.exp(A_log)

            def step(state, inp):
                x_t, B_t, C_t, dt_t = inp
                decay = jnp.exp(A[None, :] * dt_t)
                state = state * decay[:, :, None, None] + (x_t * dt_t[:, :, None])[..., None] * B_t[:, None, None, :]
                y_t = jnp.einsum('bhpn,bn->bhp', state, C_t)
                return (state, y_t)
            state0 = jnp.zeros((B, NHEADS, HEADDIM, D_STATE), dtype=x.dtype)
            inputs = (jnp.moveaxis(x_heads, 1, 0), jnp.moveaxis(B_part, 1, 0), jnp.moveaxis(C_part, 1, 0), jnp.moveaxis(dt, 1, 0))
            _, y_seq = lax.scan(step, state0, inputs)
            y = jnp.moveaxis(y_seq, 0, 1).reshape(B, L, D_INNER)
            D_full = jnp.repeat(D_param, HEADDIM)
            y = y + x_part * D_full
            y = y * jax.nn.silu(z)
            y = y * jax.lax.rsqrt(jnp.mean(y * y, axis=-1, keepdims=True) + EPS) * norm_w
            return jnp.einsum('ble,de->bld', y, out_proj_w)
        return _ssm_forward(x, in_proj_w, conv_w, conv_b, norm_w, out_proj_w, dt_bias, A_log, D_param)

    def _L0_ffn_ref(x, ln_gamma, ln_beta, fc1_q, fc1_scales, fc1_bias, fc2_q, fc2_scales, fc2_bias):
        import jax, jax.numpy as jnp
        import numpy as np
        B, S, H, F, G = (8, 512, 256, 1024, 128)
        EPS = 1e-05

        def _dequant(q, scales, g):
            K, N = q.shape
            w = (q.astype(jnp.float32) - 128.0).reshape(K // g, g, N) * scales[:, None, :]
            return w.reshape(K, N)
        residual = x
        mu = jnp.mean(x, axis=-1, keepdims=True)
        var = jnp.mean(jnp.square(x - mu), axis=-1, keepdims=True)
        h = (x - mu) * jax.lax.rsqrt(var + EPS) * ln_gamma + ln_beta
        hf = h.reshape(-1, H)
        w1 = _dequant(fc1_q, fc1_scales, G)
        y = hf @ w1 + fc1_bias
        y = jax.nn.silu(y)
        w2 = _dequant(fc2_q, fc2_scales, G)
        z = y @ w2 + fc2_bias
        return residual + 0.5 * z.reshape(residual.shape)
    h = _L0_tok_ref(x, L0_tok_w1, L0_tok_b1, L0_tok_w2, L0_tok_b2, L0_tok_gamma, L0_tok_beta)
    h = h + _L0_attn_ref(_layernorm(h, axis=-1), L0_attn_in_proj_w, L0_attn_conv_w, L0_attn_conv_b, L0_attn_norm_w, L0_attn_out_proj_w, L0_attn_dt_bias, L0_attn_A_log, L0_attn_D_param)
    h = h + _L0_ffn_ref(_layernorm(h, axis=-1), L0_ffn_ln_gamma, L0_ffn_ln_beta, L0_ffn_fc1_q, L0_ffn_fc1_scales, L0_ffn_fc1_bias, L0_ffn_fc2_q, L0_ffn_fc2_scales, L0_ffn_fc2_bias)
    return h

_drawn_inputs = setup_inputs


def setup_inputs(seed=0):
    import zlib

    import numpy as np

    out = dict(_drawn_inputs(seed))
    spreads = {'L0_tok_b1': (0.0, 0.1),
     'L0_tok_b2': (0.0, 0.1),
     'L0_tok_gamma': (1.0, 0.2),
     'L0_tok_beta': (0.0, 0.1),
     'L0_attn_norm_w': (1.0, 0.2),
     'L0_attn_D_param': (1.0, 0.2),
     'L0_ffn_ln_gamma': (1.0, 0.2),
     'L0_ffn_ln_beta': (0.0, 0.1)}
    factors = {'L0_attn_dt_bias': 64.0,
     'L0_attn_A_log': 64.0,
     'L0_ffn_fc1_bias': 64.0,
     'L0_ffn_fc2_bias': 64.0}
    for name, (base, spread) in spreads.items():
        noise = np.random.default_rng([zlib.crc32(name.encode()), seed]).standard_normal(out[name].shape)
        drawn = base * np.exp(spread * noise) if base else spread * noise
        out[name] = jnp.asarray(drawn.astype(out[name].dtype))
    for name, factor in factors.items():
        out[name] = (out[name] * factor).astype(out[name].dtype)
    return out
```

```python
from contextlib import ExitStack

import concourse.bass as bass
from concourse import mybir

ALU = mybir.AluOpType
ACT = mybir.ActivationFunctionType
F32 = mybir.dt.float32
F32R = mybir.dt.float32r
I32 = mybir.dt.int32

P = 128
EPS = 1e-5


class Count:

    def __init__(self, loop, per, extra):
        self.loop, self.per, self.extra = loop, per, extra

    def __add__(self, n):
        return Count(self.loop, self.per, self.extra + n)

    def __sub__(self, n):
        return Count(self.loop, self.per, self.extra - n)

    def __mul__(self, n):
        return Count(self.loop, self.per * n, self.extra * n)

    __radd__, __rmul__ = __add__, __mul__


class Loop:

    def __init__(self, eng, image, registers):
        self.eng, self.image, self.used = eng, image, 0
        self.product, *self.registers = registers

    def register(self, count):
        r = self.registers[self.used % len(self.registers)]
        self.used += 1
        self.eng.reg_mul(self.product, self.image, count.per)
        self.eng.reg_add(r, self.product, count.extra)
        return r


def at(value):
    return value.loop.register(value) if isinstance(value, Count) else value


def vit_tower(nc, x, tok_w1, tok_b1, tok_w2, tok_b2, tok_gamma, tok_beta, in_proj_w, conv_w, conv_b,
              norm_w, out_proj_w, dt_bias, A_log, D_param, ln_gamma, ln_beta, fc1_q, fc1_scales,
              fc1_bias, fc2_q, fc2_scales, fc2_bias, out):
    B, CIN, HH, WW = x.shape
    HR, WR = HH // 2, WW // 2
    L = HR * WR
    HID = tok_w1.shape[1]
    DM = tok_w2.shape[1]
    NH = dt_bias.shape[0]
    DI = out_proj_w.shape[1]
    HD = DI // NH
    NS = (conv_w.shape[0] - DI) // 2
    TAPS = conv_w.shape[2]
    HALO = TAPS - 1
    E_ALL = in_proj_w.shape[0]
    T = 2 * P
    TILES = B * L // T
    PER_B = L // T
    ROWS = T // WR
    NT = HID // P
    KM = DM // P
    KI = DI // P
    NCV = conv_w.shape[0] // P
    QG = P
    assert CIN * 4 == 2 * P and KM == 2 and NS == P and PER_B == 4 and fc1_q.shape[1] == HID

    ctx = ExitStack()
    with ctx:
        def sb(name, shape, dt=F32):
            return ctx.enter_context(nc.sbuf_tensor(name, shape, dt))

        def sem(name):
            return ctx.enter_context(nc.semaphore(name))

        w1 = [sb(f"w1_{p}", [P, KM, HID], F32R) for p in ("hi", "lo")]
        w2 = [sb(f"w2_{p}", [P, NT, DM], F32R) for p in ("hi", "lo")]
        win = [sb(f"win_{p}", [P, KM, E_ALL], F32R) for p in ("hi", "lo")]
        wout = [sb(f"wout_{p}", [P, KI, DM], F32R) for p in ("hi", "lo")]
        f1 = [sb(f"f1_{p}", [P, KM, HID], F32R) for p in ("hi", "lo")]
        f2 = [sb(f"f2_{p}", [P, NT, DM], F32R) for p in ("hi", "lo")]
        ident = sb("ident", [P, P])
        ident4 = sb("ident4", [P, 4, P])
        zeros = sb("zeros", [P, P])
        notfirst = sb("notfirst", [P, 1])
        b1c = sb("b1c", [P, NT])
        fcb = sb("fcb", [P, NT])
        fcb_raw = sb("fcb_raw", [P, NT])
        fcb_part = sb("fcb_part", [P, NT])
        cw = sb("cw", [P, NCV, TAPS])
        cb = sb("cb", [P, NCV])
        nw = sb("nw", [P, KI])
        lng = sb("lng", [P, KM])
        lnb = sb("lnb", [P, KM])
        gam = sb("gam", [P, DM])
        bet = sb("bet", [P, DM])
        b2r = sb("b2r", [P, DM])
        fb2 = sb("fb2", [P, DM])
        dpar = sb("dpar", [P, NH])
        dtb = sb("dtb", [P, 2, NH])
        alog = sb("alog", [P, 2, NH])
        expa = sb("expa", [P, 2, NH])
        xin = [sb(f"xin{i}", [P, ROWS * WW]) for i in range(2)]
        xs = [sb(f"xs_{p}", [P, 2, T], F32R) for p in ("hi", "lo")]
        hfull = sb("hfull", [P, 2, T])
        ffull = sb("ffull", [P, 2, T])
        hid = [sb(f"hid_{p}", [P, NT, T], F32R) for p in ("hi", "lo")]
        ytok = sb("ytok", [P, 2, DM])
        h1 = sb("h1", [P, 2, 2, DM])
        u = sb("u", [P, 2, DM])
        uT = [sb(f"uT_{p}", [P, KM, T], F32R) for p in ("hi", "lo")]
        raw = sb("raw", [P, NCV, HALO + T])
        acc = sb("acc", [P, 3, T])
        xc = sb("xc", [P, NCV, T])
        sz = sb("sz", [P, 2, DI])
        dtr = sb("dtr", [P, 2, NH])
        dab = sb("dab", [P, 2, NH])
        dex = sb("dex", [P, 2, NH])
        dln = sb("dln", [P, 2, NH])
        dtt = sb("dtt", [P, 2, 2, NH])
        da = sb("da", [P, 2, NH])
        dec = sb("dec", [P, 2, NH])
        decz = sb("decz", [P, 2, 2, NH])
        pT = sb("pT", [2 * NH, P])
        pp = sb("pp", [P, 2, 2, 2, NH])
        xtm = sb("xtm", [P, DI])
        xdt = sb("xdt", [P, DI])
        xw = sb("xw", [P, DI])
        btm = sb("btm", [P, NS])
        dmat = sb("dmat", [P, NH, P])
        dlast = sb("dlast", [P, NH])
        S = sb("S", [P, DI])
        yb = sb("yb", [P, 2, DI])
        sq = sb("sq", [P, DI])
        ssum = sb("ssum", [P, 2])
        yr = sb("yr", [P, 2])
        yT = [sb(f"yT_{p}", [P, KI, P], F32R) for p in ("hi", "lo")]
        h2 = sb("h2", [P, 2, DM])
        x3 = sb("x3", [P, 2, DM])
        res = sb("res", [P, 2, 2, DM])
        f = sb("f", [P, 2, DM])
        fT = [sb(f"fT_{p}", [P, KM, T], F32R) for p in ("hi", "lo")]
        ob = sb("ob", [P, 2, DM])
        st = sb("st", [P, 4, 6])
        mv = sb("mv", [P, 4, 2, 2])
        veps = sb("veps", [P, 4, 2])
        negm = sb("negm", [P, 4, 2])
        mhalf = sb("mhalf", [P, 1])
        msq = sb("msq", [P, 2])
        rstd = sb("rstd", [P, 4, 2])
        nb = sb("nb", [P, 4, 2])

        def bank(name):
            return ctx.enter_context(nc.psum_tensor(name, [P, 512], F32))

        wide = [bank("wide0"), bank("wide1")]
        tmb = bank("tmb")
        trb = bank("trb")
        bcb = bank("bcb")
        yib = bank("yib")
        yxb = bank("yxb")
        dsb = bank("dsb")

        waits_passed = sem("waits_passed")
        x_loaded = [sem("x_loaded0"), sem("x_loaded1")]
        const_loaded = sem("const_loaded")
        w_loaded = [sem("w_loaded0"), sem("w_loaded1")]
        scale_loaded = [sem("scale_loaded0"), sem("scale_loaded1")]
        ident_ready = sem("ident_ready")
        const_ready = sem("const_ready")
        expa_ready = sem("expa_ready")
        dequant = sem("dequant")
        w_turned = sem("w_turned")
        w_hi = sem("w_hi")
        w_lo = sem("w_lo")
        beta_product = sem("beta_product")
        fcb_ready = sem("fcb_ready")
        xs_hi = sem("xs_hi")
        xs_lo = sem("xs_lo")
        tok1_done = sem("tok1_done")
        gelu_done = sem("gelu_done")
        tok_hi = sem("tok_hi")
        tok_lo = sem("tok_lo")
        tok2_done = sem("tok2_done")
        ln12 = sem("ln12")
        norm1_done = sem("norm1_done")
        h1_steps = sem("h1_steps")
        u_done = sem("u_done")
        uT_done = sem("uT_done")
        uT_hi = sem("uT_hi")
        uT_lo = sem("uT_lo")
        xbc_done = sem("xbc_done")
        halo_ready = sem("halo_ready")
        raw_done = sem("raw_done")
        tap0_done = sem("tap0_done")
        taps = sem("taps")
        xc_done = sem("xc_done")
        z_done = sem("z_done")
        sz_done = sem("sz_done")
        dt_done = sem("dt_done")
        dt_act = sem("dt_act")
        dt_vec = sem("dt_vec")
        decT_done = sem("decT_done")
        pT_done = sem("pT_done")
        ppT_done = sem("ppT_done")
        pp_done = sem("pp_done")
        xT_done = sem("xT_done")
        bT_done = sem("bT_done")
        bc_done = sem("bc_done")
        bcast_done = sem("bcast_done")
        xtm_done = sem("xtm_done")
        btm_done = sem("btm_done")
        scan_done = sem("scan_done")
        dlast_done = sem("dlast_done")
        mask_done = sem("mask_done")
        xdt_done = sem("xdt_done")
        xd_done = sem("xd_done")
        xw_done = sem("xw_done")
        yinter_done = sem("yinter_done")
        yintra_done = sem("yintra_done")
        ds_done = sem("ds_done")
        s_decayed = sem("s_decayed")
        s_done = sem("s_done")
        ya_done = sem("ya_done")
        yb_done = sem("yb_done")
        y_steps = sem("y_steps")
        sq_done = sem("sq_done")
        msq_done = sem("msq_done")
        yr_done = sem("yr_done")
        pow12 = sem("pow12")
        pow34 = sem("pow34")
        yT_done = sem("yT_done")
        yT_hi = sem("yT_hi")
        yT_lo = sem("yT_lo")
        outp_done = sem("outp_done")
        ln34 = sem("ln34")
        x3_done = sem("x3_done")
        f_done = sem("f_done")
        res_steps = sem("res_steps")
        fT_done = sem("fT_done")
        fT_hi = sem("fT_hi")
        fT_lo = sem("fT_lo")
        fc1_done = sem("fc1_done")
        silu_done = sem("silu_done")
        fc_hi = sem("fc_hi")
        fc_lo = sem("fc_lo")
        fc2_done = sem("fc2_done")
        out_ready = sem("out_ready")
        out_stored = [sem("out_stored0"), sem("out_stored1")]

        def wait(eng, s, value):
            if not (isinstance(value, int) and value <= 0):
                eng.wait_ge(s, at(value))

        def passed(eng):
            eng.sem_inc(waits_passed, 1)

        def steps(eng, step):
            step(-1, PER_B - 1)
            for q in range(PER_B):
                step(q, q)
            registers = [eng.alloc_register(f"count{i}") for i in range(5)]
            with eng.Fori(0, B - 2) as b:
                loop = Loop(eng, b, registers)
                for q in range(PER_B):
                    step(Count(loop, PER_B, PER_B + q), q)
            for q in range(PER_B):
                step(TILES - PER_B + q, q)
            step(TILES, 0)

        def known(k, test):
            return test(k) if isinstance(k, int) else True

        def has_next(k):
            return known(k, lambda i: i + 1 < TILES)

        def has_scan(k):
            return known(k, lambda i: 0 <= i < TILES)

        def has_prev(k):
            return known(k, lambda i: i >= 1)

        def heads(ap):
            return ap.rearrange("p (h d) -> p h d", h=NH)

        def per_head(ap):
            return ap.unsqueeze(2).to_broadcast([P, NH, HD])

        stage = [dmat[:, :, :].rearrange("p h t -> p (h t)"), yb[:, :, :].rearrange("p c n -> p (c n)")]
        scale_stage = [h1[:, :, :, :].rearrange("p a c n -> p (a c n)"),
                       res[:, :, :, :].rearrange("p a c n -> p (a c n)")]
        W1ROWS = tok_w1.rearrange("(c a b) n -> a c b n", a=2, b=2)
        LOADS = []
        LOADS += [("w1", k) for k in range(KM)] + [("w2", k) for k in range(2)]
        LOADS += [("win", k) for k in range(3)] + [("wout", 0)]
        LOADS += [("f1", k) for k in range(KM)] + [("f2", k) for k in range(2)]
        HALF = NT // 2

        def parts(kind, i):
            if kind == "w1":
                return [[w[:, i, :] for w in w1]]
            if kind == "w2":
                return [[w[:, i * HALF:(i + 1) * HALF, :].rearrange("p k n -> p (k n)") for w in w2]]
            if kind == "win":
                e0, e1 = i * 4 * P, min((i + 1) * 4 * P, E_ALL)
                return [[w[:, k, e0:e1] for w in win] for k in range(KM)]
            if kind == "wout":
                return [[w[:, k, :] for w in wout] for k in range(KI)]
            if kind == "f1":
                return [[w[:, i, :] for w in f1]]
            return [[w[:, i * HALF:(i + 1) * HALF, :].rearrange("p k n -> p (k n)") for w in f2]]

        FIRST_PART, n_parts = [], 0
        for kind, i in LOADS:
            FIRST_PART.append(n_parts)
            n_parts += len(parts(kind, i))
        FIRST_PART.append(n_parts)
        IN_FC = [n for n, (kind, _) in enumerate(LOADS) if kind in ("f1", "f2")]
        TURNED = [n for n, (kind, _) in enumerate(LOADS) if kind in ("win", "wout")]

        def part_source(n, p):
            kind, i = LOADS[n]
            if kind == "win":
                width = min(4 * P, E_ALL - i * 4 * P)
                return wide[p][:, 0:width]
            if kind == "wout":
                return wide[p % 2][:, (p // 2) * DM:(p // 2 + 1) * DM]
            return stage[n % 2]

        def load_count(n):
            return 16 * sum(2 if LOADS[m][0] == "w1" or LOADS[m] == ("win", 2) else 1 for m in range(n % 2, n + 1, 2))

        def part_scale(n, p):
            kind, i = LOADS[n]
            if kind == "wout":
                return nw[:, p:p + 1]
            if kind == "f1":
                return lng[:, i:i + 1]
            return 0.5 if kind == "f2" else 1.0

        block = ctx.enter_context(nc.Block())

        CONSTS = [
            (b1c[:, :], tok_b1.rearrange("(n p) -> p n", p=P)),
            (fcb_raw[:, :], fc1_bias.rearrange("(n p) -> p n", p=P)),
            (cw[:, :, :], conv_w.rearrange("(n p) o k -> p n (o k)", p=P)),
            (cb[:, :], conv_b.rearrange("(n p) -> p n", p=P)),
            (nw[:, :], norm_w.rearrange("(n p) -> p n", p=P)),
            (lng[:, :], ln_gamma.rearrange("(n p) -> p n", p=P)),
            (lnb[:, :], ln_beta.rearrange("(n p) -> p n", p=P)),
            (gam[:, :], tok_gamma.partition_broadcast(P)),
            (bet[:, :], tok_beta.partition_broadcast(P)),
            (b2r[:, :], tok_b2.partition_broadcast(P)),
            (fb2[:, :], fc2_bias.partition_broadcast(P)),
            (dpar[:, :], D_param.partition_broadcast(P)),
            (dtb[:, 0, :], dt_bias.partition_broadcast(P)),
            (dtb[:, 1, :], dt_bias.partition_broadcast(P)),
            (alog[:, 0, :], A_log.partition_broadcast(P)),
            (alog[:, 1, :], A_log.partition_broadcast(P)),
        ]
        x_rows = x.rearrange("i c (t r a) w -> a i t c r w", a=2, r=ROWS)
        out_rows = out.rearrange("i (t p) n -> (i t) p n", p=P)

        @block.sync
        def _(sp):
            def load_x(j, q):
                if not (isinstance(j, int) and j >= TILES):
                    wait(sp, xs_hi, j - 1)
                    wait(sp, xs_lo, j - 1)
                    if isinstance(j, int):
                        img = j // PER_B
                    else:
                        img = (j - q % PER_B) // PER_B
                    for a in range(2):
                        sp.dma_start(xin[q % 2][a * CIN:(a + 1) * CIN, :].rearrange("c (r w) -> c r w", w=WW),
                                     x_rows[a, img, q % PER_B]).then_inc(x_loaded[q % 2], 16)

            def step(k, q):
                if isinstance(k, int):
                    load_x(k + 4, q)
                else:
                    wait(sp, xs_hi, k + 3)
                    wait(sp, xs_lo, k + 3)
                    for a in range(2):
                        sp.dma_start(xin[q % 2][a * CIN:(a + 1) * CIN, :].rearrange("c (r w) -> c r w", w=WW),
                                     x_rows[a, bass.ds(k.loop.image + 2, 1), q][0]).then_inc(x_loaded[q % 2], 16)
                if has_prev(k):
                    for c in range(2):
                        g = 2 * (k - 1) + c
                        sp.wait_ge(out_ready, at(g + 1))
                        dst = out_rows[g] if isinstance(k, int) else out_rows[bass.ds(g.loop.image * g.per + g.extra, 1)][0]
                        sp.dma_start(dst, ob[:, c, :]).then_inc(out_stored[c], 16)

            for j in range(2):
                load_x(j, j)
            for n, (kind, i) in enumerate(LOADS):
                if n >= 2:
                    sp.wait_ge(w_lo, at(FIRST_PART[n - 1]))
                if n - 2 in IN_FC and LOADS[n - 2][0] == "f1":
                    sp.wait_ge(beta_product, at(IN_FC.index(n - 2) + 1))
                dst, s = stage[n % 2], w_loaded[n % 2]
                if kind == "w1":
                    for a in range(2):
                        sp.dma_start(dst[a * CIN:(a + 1) * CIN, :], W1ROWS[a, :, i, :]).then_inc(s, 16)
                elif kind == "w2":
                    sp.dma_start(dst.rearrange("p (k n) -> p k n", n=DM),
                                 tok_w2[i * HALF * P:(i + 1) * HALF * P, :].rearrange("(k p) n -> p k n", p=P)).then_inc(s, 16)
                elif kind == "win":
                    rows = min(4 * P, E_ALL - i * 4 * P)
                    full = rows // P
                    sp.dma_start(dst[:, 0:full * DM].rearrange("p (k n) -> p k n", n=DM),
                                 in_proj_w[i * 4 * P:(i * 4 + full) * P, :].rearrange("(k p) n -> p k n", p=P)).then_inc(s, 16)
                    if rows % P:
                        sp.dma_start(dst[0:NH, full * DM:(full + 1) * DM], in_proj_w[E_ALL - NH:E_ALL, :]).then_inc(s, 16)
                elif kind == "wout":
                    sp.dma_start(dst.rearrange("p (k n) -> p k n", n=DI),
                                 out_proj_w.rearrange("(k p) n -> p k n", p=P)).then_inc(s, 16)
                else:
                    o = IN_FC.index(n)
                    if o >= 2:
                        sp.wait_ge(dequant, at(o - 1))
                    sdst = scale_stage[o % 2]
                    if kind == "f1":
                        sp.dma_start(dst.bitcast(I32), fc1_q[i * P:(i + 1) * P, :]).then_inc(s, 16)
                        sp.dma_start(sdst, fc1_scales[i].partition_broadcast(P)).then_inc(scale_loaded[o % 2], 16)
                    else:
                        sp.dma_start(dst.bitcast(I32).rearrange("p (k n) -> p k n", n=DM),
                                     fc2_q[i * HALF * P:(i + 1) * HALF * P, :].rearrange("(k p) n -> p k n", p=P)).then_inc(s, 16)
                        sp.dma_start(sdst.rearrange("p (k n) -> p k n", n=DM),
                                     fc2_scales[i * HALF:(i + 1) * HALF, :].partition_broadcast(P)).then_inc(scale_loaded[o % 2], 16)
                if n == 0:
                    for dst, src in CONSTS:
                        sp.dma_start(dst, src, allow_slow_non_contiguous=True).then_inc(const_loaded, 16)
            load_x(2, 2)
            steps(sp, step)
            for c in range(2):
                sp.wait_ge(out_stored[c], at(16 * TILES))

        @block.gpsimd
        def _(pool):
            pool.memset(ident[:, :], 0.0).then_inc(ident_ready, 1)
            pool.memset(ident4[:, :, :], 0.0).then_inc(ident_ready, 1)
            pool.memset(notfirst[:, :], 1.0).then_inc(ident_ready, 1)
            pool.memset(zeros[:, :], 0.0).then_inc(ident_ready, 1)
            pool.memset(S[:, :], 0.0).then_inc(ident_ready, 1)
            pool.memset(mhalf[:, :], -0.5).then_inc(ident_ready, 1)
            pool.wait_ge(ident_ready, 6)
            pool.affine_select(out=ident[:, :], in_=ident[:, :], compare_op=ALU.not_equal, fill=1.0, base=0,
                               pattern=[[-1, P]], channel_multiplier=1).then_inc(ident_ready, 1)
            pool.affine_select(out=ident4[:, :, :], in_=ident4[:, :, :], compare_op=ALU.not_equal, fill=1.0,
                               base=0, pattern=[[0, 4], [-1, P]], channel_multiplier=1).then_inc(ident_ready, 1)
            pool.affine_select(out=notfirst[:, :], in_=notfirst[:, :], compare_op=ALU.not_equal, fill=0.0,
                               base=0, pattern=[[0, 1]], channel_multiplier=1).then_inc(ident_ready, 1)

            def chunk(k, q, c):
                g, par = 2 * k + c, q % 2
                pool.wait_ge(xtm_done, at(g + 1))
                wait(pool, yintra_done, g)
                pool.tensor_tensor(heads(xdt[:, :]), heads(xtm[:, :]), per_head(dtt[:, par, c, :]),
                                   ALU.mult).then_inc(xdt_done, 1)
                pool.wait_ge(xdt_done, at(g + 1))
                pool.tensor_tensor(heads(xtm[:, :]), heads(xtm[:, :]), per_head(dpar[:, :]),
                                   ALU.mult).then_inc(xd_done, 1)
                pool.wait_ge(dlast_done, at(2 * g + 2))
                wait(pool, ds_done, g)
                pool.tensor_tensor(heads(xw[:, :]), heads(xdt[:, :]), per_head(dlast[:, :]),
                                   ALU.mult).then_inc(xw_done, 1)
                pool.wait_ge(yinter_done, at(g + 1))
                wait(pool, s_done, g)
                pool.tensor_tensor(heads(S[:, :]), heads(S[:, :]), per_head(pp[:, par, 1, c, :]),
                                   ALU.mult).then_inc(s_decayed, 1)

            def gate(k, c):
                g = 2 * k + c
                pool.wait_ge(yb_done, at(g + 1))
                pool.wait_ge(xd_done, at(g + 1))
                pool.tensor_tensor(yb[:, c, :], yb[:, c, :], xtm[:, :], ALU.add).then_inc(y_steps, 1)
                pool.wait_ge(y_steps, at(2 * g + 1))
                pool.wait_ge(sz_done, at(g + 1))
                pool.tensor_tensor(yb[:, c, :], yb[:, c, :], sz[:, c, :], ALU.mult).then_inc(y_steps, 1)

            def inverse_rms(k, c):
                g = 2 * k + c
                pool.wait_ge(msq_done, at(g + 1))
                pool.tensor_tensor(yr[:, c:c + 1], msq[:, c:c + 1], mhalf[:, :], ALU.pow).then_inc(yr_done, 1)

            def inverse_std(which, c, stats, stats_count, powers, base):
                pool.wait_ge(stats, at(stats_count))
                pool.tensor_tensor(rstd[:, which, c:c + 1], veps[:, which, c:c + 1], mhalf[:, :],
                                   ALU.pow).then_inc(powers, 1)
                pool.wait_ge(powers, at(base + 1))
                pool.tensor_tensor(nb[:, which, c:c + 1], negm[:, which, c:c + 1], rstd[:, which, c:c + 1],
                                   ALU.mult).then_inc(powers, 1)

            def norms34(k, q, c):
                g = 2 * k + c
                inverse_rms(k, c)
                inverse_std(2, c, ln34, 9 * g + 5, pow34, 4 * g)
                inverse_std(3, c, ln34, 9 * g + 9, pow34, 4 * g + 2)
                residual(k, q, c)

            def norms12(j, q, c):
                g = 2 * j + c
                inverse_std(0, c, ln12, 9 * g + 5, pow12, 4 * g)
                affine(j, q, c)
                inverse_std(1, c, ln12, 9 * g + 9, pow12, 4 * g + 2)

            def residual(k, q, c):
                g, par = 2 * k + c, q % 2
                pool.wait_ge(x3_done, at(g + 1))
                wait(pool, out_ready, g - 3)
                pool.tensor_tensor(res[:, par, c, :], h2[:, c, :], x3[:, c, :], ALU.add).then_inc(res_steps, 1)
                pool.wait_ge(res_steps, at(2 * g + 1))
                pool.tensor_tensor(res[:, par, c, :], res[:, par, c, :], fb2[:, :], ALU.add).then_inc(res_steps, 1)

            def affine(j, q, c):
                g, par = 2 * j + c, q % 2
                pool.wait_ge(norm1_done, at(g + 1))
                wait(pool, ln34, 9 * (g - 4) + 1)
                pool.tensor_tensor(h1[:, par, c, :], ytok[:, c, :], gam[:, :], ALU.mult).then_inc(h1_steps, 1)
                pool.wait_ge(h1_steps, at(2 * g + 1))
                pool.tensor_tensor(h1[:, par, c, :], h1[:, par, c, :], bet[:, :], ALU.add).then_inc(h1_steps, 1)

            def halo(j, q):
                wait(pool, taps, 3 * NCV * j)
                passed(pool)
                if q % PER_B == 0:
                    pool.memset(raw[:, :, 0:HALO], 0.0).then_inc(halo_ready, 1)
                else:
                    pool.tensor_copy(raw[:, :, 0:HALO], raw[:, :, T:T + HALO]).then_inc(halo_ready, 1)

            def step(k, q):
                if has_scan(k):
                    chunk(k, q, 0)
                    gate(k, 0)
                if has_prev(k):
                    norms34(k - 1, q - 1, 1)
                if has_next(k):
                    for c in range(2):
                        norms12(k + 1, q + 1, c)
                    halo(k + 1, q + 1)
                if has_scan(k):
                    chunk(k, q, 1)
                    gate(k, 1)
                    norms34(k, q, 0)

            pool.wait_ge(const_ready, at(1))
            pool.wait_ge(dequant, at(len(IN_FC)))
            steps(pool, step)

        @block.scalar
        def _(act):
            act.wait_ge(const_loaded, at(16 * len(CONSTS)))
            act.activation(expa[:, :, :], alog[:, :, :], ACT.Exp).then_inc(expa_ready, 1)
            for n, (kind, i) in enumerate(LOADS):
                for p, (hi, lo) in enumerate(parts(kind, i)):
                    if n in TURNED:
                        act.wait_ge(w_turned, at(TURNED.index(n) + 1))
                        if p >= 2:
                            act.wait_ge(w_lo, FIRST_PART[n] + p - 1)
                    elif n in IN_FC:
                        act.wait_ge(dequant, at(IN_FC.index(n) + 1))
                    else:
                        act.wait_ge(w_loaded[n % 2], at(load_count(n)))
                    act.activation(hi, part_source(n, p), ACT.Copy, scale=part_scale(n, p)).then_inc(w_hi, 1)

            def split_x(j, q):
                act.wait_ge(x_loaded[q % 2], at(32 * count_pairs(j, q)))
                wait(act, tok1_done, NT * j)
                act.activation(xs[0][:, :, :], xin[q % 2][:, :].rearrange("p (t b) -> p b t", b=2),
                               ACT.Copy).then_inc(xs_hi, 1)

            def x_and_b(k, c):
                g = 2 * k + c
                act.wait_ge(xT_done, at(g + 1))
                wait(act, y_steps, 2 * g - 1)
                act.activation(xtm[:, :], trb[:, :], ACT.Copy).then_inc(xtm_done, 1)
                act.wait_ge(bT_done, at(g + 1))
                wait(act, ds_done, g)
                act.activation(btm[:, :], yib[:, 0:NS], ACT.Copy).then_inc(btm_done, 1)

            def y_turned(k, c):
                g = 2 * k + c
                act.wait_ge(yT_done, at(g + 1))
                wait(act, outp_done, g)
                act.activation(yT[0][:, :, :], trb[:, :].rearrange("p (k t) -> p k t", t=P),
                               ACT.Copy).then_inc(yT_hi, 1)

            def normalise(dst, src, which, c):
                return act.activation(dst, src, ACT.Identity, scale=rstd[:, which, c:c + 1],
                                      bias=nb[:, which, c:c + 1])

            def norms34(k, c):
                g = 2 * k + c
                act.wait_ge(pow34, at(4 * g + 2))
                wait(act, res_steps, 2 * g - 3)
                normalise(x3[:, c, :], h2[:, c, :], 2, c).then_inc(x3_done, 1)
                act.wait_ge(pow34, at(4 * g + 4))
                wait(act, fT_done, k)
                normalise(f[:, c, :], x3[:, c, :], 3, c).then_inc(f_done, 1)

            def norms12(j, c):
                g = 2 * j + c
                act.wait_ge(pow12, at(4 * g + 2))
                normalise(ytok[:, c, :], ytok[:, c, :], 0, c).then_inc(norm1_done, 1)
                act.wait_ge(pow12, at(4 * g + 4))
                wait(act, uT_done, j)
                normalise(u[:, c, :], h1[:, j_par[0], c, :], 1, c).then_inc(u_done, 1)

            j_par = [0]

            def square(k, c):
                g = 2 * k + c
                act.wait_ge(y_steps, at(2 * g + 2))
                wait(act, sq_done, g)
                wait(act, msq_done, g - 1)
                act.activation(sq[:, :], yb[:, c, :], ACT.Square, accum_out=ssum[:, c:c + 1]).then_inc(sq_done, 1)

            def step(k, q):
                j = k + 1
                j_par[0] = (q + 1) % 2
                if has_scan(k):
                    x_and_b(k, 0)
                if has_next(k):
                    for n in range(NT):
                        if n == 0:
                            wait(act, fc2_done, 2 * (j - 2))
                        act.wait_ge(tok1_done, at(NT * j + n + 1))
                        wait(act, tok_lo, NT * j + n - 1)
                        act.activation(hfull[:, n % 2, :], wide[n % 2][:, 0:T], ACT.Gelu,
                                       bias=b1c[:, n:n + 1]).then_inc(gelu_done, 1)
                        act.wait_ge(gelu_done, at(NT * j + n + 1))
                        act.activation(hid[0][:, n, :], hfull[:, n % 2, :], ACT.Copy).then_inc(tok_hi, 1)
                if has_prev(k):
                    y_turned(k - 1, 1)
                    norms34(k - 1, 1)
                if has_scan(k):
                    square(k, 0)
                if has_next(k):
                    norms12(j, 0)
                    norms12(j, 1)
                if has_scan(k):
                    x_and_b(k, 1)
                if has_prev(k):
                    i = k - 1
                    act.wait_ge(fT_done, at(i + 1))
                    wait(act, fc1_done, NT * i)
                    act.activation(fT[0][:, :, :], trb[:, :].rearrange("p (k t) -> p k t", t=T),
                                   ACT.Copy).then_inc(fT_hi, 1)
                    for n in range(NT):
                        if n == 0:
                            act.wait_ge(tok2_done, at(2 * (k + 2) if has_next(k) else 2 * TILES))
                            if not has_next(k):
                                wait(act, fc2_done, 2 * i)
                        act.wait_ge(fc1_done, at(NT * i + n + 1))
                        wait(act, fc_lo, NT * i + n - 1)
                        act.activation(ffull[:, n % 2, :], wide[n % 2][:, 0:T], ACT.Silu,
                                       bias=fcb[:, n:n + 1]).then_inc(silu_done, 1)
                        act.wait_ge(silu_done, at(NT * i + n + 1))
                        act.activation(hid[0][:, n, :], ffull[:, n % 2, :], ACT.Copy).then_inc(fc_hi, 1)
                if has_scan(k):
                    y_turned(k, 0)
                    norms34(k, 0)
                if has_next(k):
                    act.wait_ge(uT_done, at(j + 1))
                    wait(act, dt_done, j)
                    act.activation(uT[0][:, :, :], trb[:, :].rearrange("p (k t) -> p k t", t=T),
                                   ACT.Copy).then_inc(uT_hi, 1)
                    act.wait_ge(halo_ready, at(j + 1))
                    for n in range(NCV):
                        m = NCV * j + n
                        act.wait_ge(xbc_done, at(m + 1))
                        act.activation(raw[:, n, HALO:HALO + T], wide[n % 2][:, 0:T], ACT.Copy).then_inc(raw_done, 1)
                        wait(act, xc_done, m - 2)
                        act.activation(acc[:, n % 3, :], wide[n % 2][:, 0:T], ACT.Identity,
                                       scale=cw[:, n, HALO:TAPS], bias=cb[:, n:n + 1]).then_inc(tap0_done, 1)
                        if n >= 2:
                            conv_silu(k, j, n - 2)
                    for n in range(NCV - 2, NCV):
                        conv_silu(k, j, n)
                    for c in range(2):
                        act.wait_ge(z_done, at(2 * j + c + 1))
                        wait(act, y_steps, 4 * j - 2 + 2 * c)
                        act.activation(sz[:, c, :], wide[c][:, :], ACT.Silu).then_inc(sz_done, 1)
                    act.preload_act_table_set("natural_log_exp_and_others")
                    act.wait_ge(dt_vec, at(4 * j + 1))
                    act.activation(dab[:, :, :], dtr[:, :, :], ACT.Abs).then_inc(dt_act, 1)
                    act.wait_ge(dt_act, at(4 * j + 1))
                    act.activation(dex[:, :, :], dab[:, :, :], ACT.Exp, scale=-1.0).then_inc(dt_act, 1)
                    act.wait_ge(dt_act, at(4 * j + 2))
                    act.activation(dln[:, :, :], dex[:, :, :], ACT.Ln, bias=1.0).then_inc(dt_act, 1)
                    act.wait_ge(dt_vec, at(4 * j + 3))
                    act.activation(dec[:, :, :], da[:, :, :], ACT.Exp, scale=-1.0).then_inc(dt_act, 1)
                if has_scan(k):
                    square(k, 1)
                if known(k, lambda i: i + 2 < TILES):
                    split_x(k + 2, q + 2)

            def conv_silu(k, j, n):
                act.wait_ge(taps, at(3 * (NCV * j + n - n % 2) + 2 * HALO - 1 + n % 2))
                if n == 0:
                    wait(act, xT_done, 2 * j)
                    wait(act, bT_done, 2 * j)
                    wait(act, yinter_done, 2 * j)
                act.activation(xc[:, n, :], acc[:, n % 3, :], ACT.Silu).then_inc(xc_done, 1)

            def count_pairs(j, q):
                return j // 2 + 1 if isinstance(j, int) else Count(j.loop, j.per // 2, j.extra // 2 + 1)

            split_x(0, 0)
            steps(act, step)

        @block.tensor
        def _(pe):
            def product(dst, pairs):
                n = len(pairs)
                for m, (lhs, rhs) in enumerate(pairs):
                    pe.matmul(dst, lhs[0], rhs[0], start=(m == 0), stop=False)
                    pe.matmul(dst, lhs[0], rhs[1], start=False, stop=False)
                    last = pe.matmul(dst, lhs[1], rhs[0], start=False, stop=(m == n - 1))
                return last

            pe.wait_ge(ident_ready, 9)
            for n, (kind, i) in enumerate(LOADS):
                if n in TURNED:
                    pe.wait_ge(w_loaded[n % 2], at(load_count(n)))
                    if TURNED.index(n):
                        pe.wait_ge(w_lo, at(FIRST_PART[n]))
                    if kind == "win":
                        rows = min(4 * P, E_ALL - i * 4 * P)
                        src = stage[n % 2].rearrange("p (k n) -> p k n", n=DM)
                        for kt in range(KM):
                            for t in range(0, rows, P):
                                h = min(P, rows - t)
                                last = pe.transpose(wide[kt][:, t:t + h], src[0:h, t // P, kt * P:(kt + 1) * P],
                                                    ident[0:h, 0:h])
                    else:
                        src = stage[n % 2].rearrange("p (k n) -> p k n", n=DI)
                        for kt in range(KI):
                            for t in range(KM):
                                o = (kt // 2) * DM + t * P
                                last = pe.transpose(wide[kt % 2][:, o:o + P], src[:, t, kt * P:(kt + 1) * P],
                                                    ident[:, :])
                    last.then_inc(w_turned, 1)
                elif kind == "f1":
                    pe.wait_ge(dequant, at(IN_FC.index(n) + 1))
                    for t in range(NT):
                        last = pe.matmul(tmb[:, i * NT + t:i * NT + t + 1], stage[n % 2][:, t * P:(t + 1) * P],
                                         lnb[:, i:i + 1], start=True, stop=True)
                    last.then_inc(beta_product, 1)

            def prepare(k, q, c):
                g, par, t = 2 * k + c, q % 2, slice(c * P, (c + 1) * P)
                if c == 0:
                    pe.wait_ge(xc_done, at(NCV * (k + 1)))
                    pe.wait_ge(uT_lo, at(k + 1))
                else:
                    if has_prev(k):
                        pe.wait_ge(yT_lo, at(2 * k))
                    pe.wait_ge(xtm_done, at(g))
                for n in range(KI):
                    last = pe.transpose(trb[:, n * P:(n + 1) * P], xc[:, n, t], ident[:, :])
                last.then_inc(xT_done, 1)
                wait(pe, yb_done, g)
                pe.transpose(yib[:, 0:NS], xc[:, KI, t], ident[:, :]).then_inc(bT_done, 1)
                wait(pe, s_done, g)
                pe.matmul(dsb[:, 0:P], xc[:, KI, t], xc[:, KI + 1, t], start=True, stop=True).then_inc(bc_done, 1)
                if c == 0:
                    pe.wait_ge(pp_done, at(k + 1))
                spread(k, q, c, 0)

            def spread(k, q, c, half):
                g, par = 2 * k + c, q % 2
                wait(pe, scan_done, 2 * g + half)
                for h in range(4):
                    col = decz[:, par, c, half * 4 + h:half * 4 + h + 1]
                    last = pe.transpose(bcb[:, h * P:(h + 1) * P], col.to_broadcast([P, P]), ident[:, :])
                last.then_inc(bcast_done, 1)

            def scan_products(k, c):
                g, t = 2 * k + c, slice(c * P, (c + 1) * P)
                wait(pe, s_done, g)
                wait(pe, ya_done, g)
                pe.matmul(yxb[:, :], xc[:, KI + 1, t], S[:, :], start=True, stop=True).then_inc(yinter_done, 1)
                pe.wait_ge(xdt_done, at(g + 1))
                pe.wait_ge(btm_done, at(g + 1))
                for h in range(NH):
                    if h % 4 == 0:
                        pe.wait_ge(mask_done, at(2 * g + h // 4 + 1))
                    last = pe.matmul(yib[:, h * HD:(h + 1) * HD], dmat[:, h, :], xdt[:, h * HD:(h + 1) * HD],
                                     start=True, stop=True)
                last.then_inc(yintra_done, 1)
                pe.wait_ge(xw_done, at(g + 1))
                pe.matmul(dsb[:, :], btm[:, :], xw[:, :], start=True, stop=True).then_inc(ds_done, 1)

            def turn_y(k, c):
                g = 2 * k + c
                pe.wait_ge(y_steps, at(2 * g + 2))
                for n in range(KI):
                    last = pe.transpose(trb[:, n * P:(n + 1) * P], yb[:, c, n * P:(n + 1) * P], ident[:, :])
                last.then_inc(yT_done, 1)

            def out_proj(k, c):
                g = 2 * k + c
                pe.wait_ge(yT_lo, at(g + 1))
                product(tmb[:, 0:DM], [([w[:, n, :] for w in yT], [w[:, n, :] for w in wout])
                                       for n in range(KI)]).then_inc(outp_done, 1)

            def step(k, q):
                j, i = k + 1, k - 1
                if has_scan(k):
                    prepare(k, q, 0)
                if has_next(k):
                    pe.wait_ge(xs_lo, at(j + 1))
                for n in range(NT):
                    if has_next(k):
                        if n >= 2:
                            pe.wait_ge(gelu_done, at(NT * j + n - 1))
                        else:
                            wait(pe, sz_done, 2 * j + n - 1)
                        product(wide[n % 2][:, 0:T], [([w[:, m, n * P:(n + 1) * P] for w in w1], [v[:, m, :] for v in xs])
                                                      for m in range(KM)]).then_inc(tok1_done, 1)
                    if has_scan(k) and n == 3:
                        spread(k, q, 0, 1)
                if has_prev(k):
                    pe.wait_ge(xtm_done, at(2 * k + 1 if has_scan(k) else 2 * TILES))
                    pe.wait_ge(yT_lo, at(2 * i + 1))
                    turn_y(i, 1)
                if has_scan(k):
                    scan_products(k, 0)
                if has_prev(k):
                    wait(pe, out_ready, 2 * i)
                    wait(pe, ln34, 1)
                    out_proj(i, 1)
                if has_next(k):
                    for c in range(2):
                        if c == 1:
                            pe.wait_ge(ln12, at(18 * j + 1))
                        elif has_prev(k):
                            pe.wait_ge(ln34, at(18 * i + 10))
                        else:
                            wait(pe, ln12, 18 * j - 8)
                        for m in range(NT):
                            pe.wait_ge(tok_lo, at(NT * j + m + 1))
                            lhs = [v[:, m, c * P:(c + 1) * P] for v in hid]
                            for o, (a, b) in enumerate(((0, 0), (0, 1), (1, 0))):
                                last = pe.matmul(tmb[:, 0:DM], lhs[a], w2[b][:, m, :],
                                                 start=(m == 0 and o == 0), stop=(m == NT - 1 and o == 2))
                        last.then_inc(tok2_done, 1)
                if has_scan(k):
                    prepare(k, q, 1)
                if has_prev(k):
                    if has_scan(k):
                        pe.wait_ge(xtm_done, at(2 * k + 2))
                    else:
                        pe.wait_ge(yT_lo, at(2 * TILES))
                    pe.wait_ge(f_done, at(2 * i + 2))
                    for n in range(KM):
                        for c in range(2):
                            last = pe.transpose(trb[:, n * T + c * P:n * T + (c + 1) * P], f[:, c, n * P:(n + 1) * P],
                                                ident[:, :])
                    last.then_inc(fT_done, 1)
                    pe.wait_ge(fT_lo, at(i + 1))
                for n in range(NT):
                    if has_prev(k):
                        if n >= 2:
                            pe.wait_ge(silu_done, at(NT * i + n - 1))
                        elif has_next(k):
                            pe.wait_ge(gelu_done, at(NT * j + NT + n - 1))
                        elif has_scan(k):
                            pe.wait_ge(sz_done, 2 * k + n + 1)
                        else:
                            pe.wait_ge(silu_done, NT * i + n - 1)
                        product(wide[n % 2][:, 0:T], [([w[:, m, n * P:(n + 1) * P] for w in f1], [v[:, m, :] for v in fT])
                                                      for m in range(KM)]).then_inc(fc1_done, 1)
                    if has_scan(k) and n == 3:
                        spread(k, q, 1, 1)
                if has_scan(k):
                    if has_prev(k):
                        pe.wait_ge(fT_lo, at(i + 1))
                    else:
                        pe.wait_ge(xtm_done, at(2 * k + 2))
                    turn_y(k, 0)
                    scan_products(k, 1)
                    if has_next(k):
                        pe.wait_ge(ln12, at(18 * j + 10))
                    else:
                        pe.wait_ge(ln34, at(18 * i + 10))
                    out_proj(k, 0)
                if has_next(k):
                    pe.wait_ge(u_done, at(2 * j + 2))
                    if has_scan(k):
                        pe.wait_ge(yT_lo, at(2 * k + 1))
                    for n in range(KM):
                        for c in range(2):
                            last = pe.transpose(trb[:, n * T + c * P:n * T + (c + 1) * P], u[:, c, n * P:(n + 1) * P],
                                                ident[:, :])
                    last.then_inc(uT_done, 1)
                    pe.wait_ge(uT_lo, at(j + 1))
                    for n in range(NCV):
                        if n >= 2:
                            pe.wait_ge(tap0_done, at(NCV * j + n - 1))
                        elif has_prev(k):
                            pe.wait_ge(silu_done, at(NT * i + NT + n - 1))
                        else:
                            pe.wait_ge(gelu_done, at(NT * j + NT + n - 1))
                        e = DI + n * P
                        product(wide[n % 2][:, 0:T], [([w[:, m, e:e + P] for w in win], [v[:, m, :] for v in uT])
                                                      for m in range(KM)]).then_inc(xbc_done, 1)
                    for c in range(2):
                        pe.wait_ge(tap0_done, at(NCV * j + NCV + c - 1))
                        product(wide[c][:, :], [([v[:, m, c * P:(c + 1) * P] for v in uT], [w[:, m, 0:DI] for w in win])
                                                for m in range(KM)]).then_inc(z_done, 1)
                    wait(pe, scan_done, 4 * j)
                    for c in range(2):
                        last = product(bcb[:, c * NH:(c + 1) * NH],
                                       [([v[:, m, c * P:(c + 1) * P] for v in uT], [w[:, m, E_ALL - NH:E_ALL] for w in win])
                                        for m in range(KM)])
                    last.then_inc(dt_done, 1)
                if has_prev(k):
                    for c in range(2):
                        if c == 1:
                            pe.wait_ge(out_ready, at(2 * i + 1))
                        elif has_scan(k):
                            pe.wait_ge(ln34, at(18 * k + 1))
                        else:
                            pe.wait_ge(ln34, at(18 * i + 10))
                        for m in range(NT):
                            pe.wait_ge(fc_lo, at(NT * i + m + 1))
                            lhs = [v[:, m, c * P:(c + 1) * P] for v in hid]
                            for o, (a, b) in enumerate(((0, 0), (0, 1), (1, 0))):
                                last = pe.matmul(tmb[:, 0:DM], lhs[a], f2[b][:, m, :],
                                                 start=(m == 0 and o == 0), stop=(m == NT - 1 and o == 2))
                        last.then_inc(fc2_done, 1)
                if has_next(k):
                    pe.wait_ge(dt_act, at(4 * j + 4))
                    pe.transpose(bcb[0:2 * NH, P:2 * P], dec[:, :, :].rearrange("p c h -> p (c h)"),
                                 ident[:, :]).then_inc(decT_done, 1)
                    pe.wait_ge(pT_done, at(j + 1))
                    passed(pe)
                    pe.transpose(bcb[:, 2 * P:2 * P + 2 * NH], pT[:, :], ident[0:2 * NH, 0:2 * NH])
                    pe.transpose(bcb[:, 2 * P + 2 * NH:2 * P + 4 * NH], pT[:, P - 1:P].to_broadcast([2 * NH, P]),
                                 ident[0:2 * NH, 0:2 * NH]).then_inc(ppT_done, 1)

            pe.wait_ge(w_lo, at(FIRST_PART[-1]))
            pe.wait_ge(fcb_ready, at(2))
            steps(pe, step)

        @block.vector
        def _(dve):
            dve.wait_ge(const_loaded, at(16 * len(CONSTS)))
            dve.tensor_scalar(fb2[:, :], fb2[:, :], 0.5, None, ALU.mult).then_inc(const_ready, 1)
            dve.wait_ge(expa_ready, at(1))
            for n, (kind, i) in enumerate(LOADS):
                if n in IN_FC:
                    o = IN_FC.index(n)
                    dve.wait_ge(w_loaded[n % 2], at(load_count(n)))
                    dve.wait_ge(scale_loaded[o % 2], 16 * (o // 2 + 1))
                    dve.scalar_tensor_tensor(out=stage[n % 2], in0=stage[n % 2].bitcast(I32), scalar=-128.0,
                                             in1=scale_stage[o % 2], op0=ALU.add, op1=ALU.mult).then_inc(dequant, 1)
                for p, (hi, lo) in enumerate(parts(kind, i)):
                    dve.wait_ge(w_hi, at(FIRST_PART[n] + p + 1))
                    dve.scalar_tensor_tensor(out=lo, in0=part_source(n, p), scalar=part_scale(n, p), in1=hi,
                                             op0=ALU.mult, op1=ALU.subtract).then_inc(w_lo, 1)
            dve.wait_ge(beta_product, at(KM))
            dve.tensor_tensor(fcb_part[:, :], fcb_raw[:, :], tmb[:, 0:NT], ALU.add).then_inc(fcb_ready, 1)
            dve.wait_ge(fcb_ready, at(1))
            dve.tensor_tensor(fcb[:, :], fcb_part[:, :], tmb[:, NT:2 * NT], ALU.add).then_inc(fcb_ready, 1)

            def split_x(j, q):
                dve.wait_ge(xs_hi, at(j + 1))
                dve.tensor_tensor(xs[1][:, :, :], xin[q % 2][:, :].rearrange("p (t b) -> p b t", b=2),
                                  xs[0][:, :, :], ALU.subtract).then_inc(xs_lo, 1)

            def hidden_lo(j, n, full, hi_done, lo_done):
                dve.wait_ge(hi_done, at(NT * j + n + 1))
                dve.tensor_tensor(hid[1][:, n, :], full[:, n % 2, :], hid[0][:, n, :],
                                  ALU.subtract).then_inc(lo_done, 1)

            def scan(k, c, half):
                g, hs = 2 * k + c, slice(4 * half, 4 * half + 4)
                dve.wait_ge(bcast_done, at(2 * g + half + 1))
                if half == 0:
                    wait(dve, yintra_done, g)
                    wait(dve, xw_done, g)
                dve.tensor_tensor_scan(dmat[:, hs, :].rearrange("p h t -> p (h t)"), bcb[:, :],
                                       ident4[:, :, :].rearrange("p h t -> p (h t)"), 0.0,
                                       ALU.mult, ALU.add).then_inc(scan_done, 1)

            def mask(k, c, half):
                g, hs = 2 * k + c, slice(4 * half, 4 * half + 4)
                dve.wait_ge(scan_done, at(2 * g + half + 1))
                dve.tensor_copy(dlast[:, hs], dmat[:, hs, P - 1]).then_inc(dlast_done, 1)
                dve.wait_ge(dlast_done, at(2 * g + half + 1))
                dve.wait_ge(bc_done, at(g + 1))
                dve.tensor_tensor(dmat[:, hs, :], dmat[:, hs, :], dsb[:, 0:P].unsqueeze(1).to_broadcast([P, 4, P]),
                                  ALU.mult).then_inc(mask_done, 1)

            def y_lo(k, c):
                dve.wait_ge(yT_hi, at(2 * k + c + 1))
                dve.tensor_tensor(yT[1][:, :, :], trb[:, :].rearrange("p (k t) -> p k t", t=P), yT[0][:, :, :],
                                  ALU.subtract).then_inc(yT_lo, 1)

            def gather_y(k, q, c):
                g, par = 2 * k + c, q % 2
                dve.wait_ge(yinter_done, at(g + 1))
                wait(dve, yT_done, g - 1)
                wait(dve, sq_done, g - 1)
                dve.tensor_tensor(heads(yb[:, c, :]), heads(yxb[:, :]), per_head(pp[:, par, 0, c, :]),
                                  ALU.mult).then_inc(ya_done, 1)
                dve.wait_ge(ya_done, at(g + 1))
                dve.wait_ge(yintra_done, at(g + 1))
                dve.tensor_tensor(yb[:, c, :], yb[:, c, :], yib[:, :], ALU.add).then_inc(yb_done, 1)

            def state(k, q, c):
                g = 2 * k + c
                dve.wait_ge(s_decayed, at(g + 1))
                dve.wait_ge(ds_done, at(g + 1))
                if q == PER_B - 1 and c == 1:
                    dve.memset(S[:, :], 0.0).then_inc(s_done, 1)
                else:
                    dve.tensor_tensor(S[:, :], S[:, :], dsb[:, :], ALU.add).then_inc(s_done, 1)

            def moments(src, which, c, s, base):
                dve.bn_stats(st[:, which, :], src).then_inc(s, 1)
                dve.wait_ge(s, at(base + 1))
                passed(dve)
                dve.bn_aggr(mv[:, which, c, :], st[:, which, :]).then_inc(s, 1)
                dve.wait_ge(s, at(base + 2))
                dve.tensor_scalar(veps[:, which, c:c + 1], mv[:, which, c, 1:2], EPS, None, ALU.add).then_inc(s, 1)
                dve.tensor_scalar(negm[:, which, c:c + 1], mv[:, which, c, 0:1], -1.0, None, ALU.mult).then_inc(s, 1)

            def mean_square(k, c):
                g = 2 * k + c
                dve.wait_ge(sq_done, at(g + 1))
                dve.tensor_scalar(msq[:, c:c + 1], ssum[:, c:c + 1], 1.0 / DI, EPS, ALU.mult, ALU.add).then_inc(msq_done, 1)

            def norms34(k, q, c):
                g, par = 2 * k + c, q % 2
                dve.wait_ge(yr_done, at(g + 1))
                dve.wait_ge(outp_done, at(g + 1))
                wait(dve, res_steps, 2 * g - 3)
                dve.scalar_tensor_tensor(out=h2[:, c, :], in0=tmb[:, 0:DM], scalar=yr[:, c:c + 1],
                                         in1=h1[:, par, c, :], op0=ALU.mult, op1=ALU.add).then_inc(ln34, 1)
                dve.wait_ge(ln34, at(9 * g + 1))
                moments(h2[:, c, :], 2, c, ln34, 9 * g + 1)
                dve.wait_ge(x3_done, at(g + 1))
                moments(x3[:, c, :], 3, c, ln34, 9 * g + 5)

            def norms12(j, q, c):
                g, par = 2 * j + c, q % 2
                dve.wait_ge(tok2_done, at(g + 1))
                wait(dve, h1_steps, 2 * g - 3)
                dve.tensor_tensor(ytok[:, c, :], tmb[:, 0:DM], b2r[:, :], ALU.add).then_inc(ln12, 1)
                dve.wait_ge(ln12, at(9 * g + 1))
                moments(ytok[:, c, :], 0, c, ln12, 9 * g + 1)

            def norm2(j, q, c):
                g, par = 2 * j + c, q % 2
                dve.wait_ge(h1_steps, at(2 * g + 2))
                moments(h1[:, par, c, :], 1, c, ln12, 9 * g + 5)

            def step(k, q):
                j, i = k + 1, k - 1
                if has_scan(k):
                    scan(k, 0, 0)
                    mask(k, 0, 0)
                for n in range(NT):
                    if has_next(k):
                        hidden_lo(j, n, hfull, tok_hi, tok_lo)
                    if has_scan(k) and n == 3:
                        scan(k, 0, 1)
                        mask(k, 0, 1)
                if has_prev(k):
                    y_lo(i, 1)
                if has_scan(k):
                    gather_y(k, q, 0)
                if has_prev(k):
                    mean_square(i, 1)
                    norms34(i, q + 3, 1)
                if has_scan(k):
                    state(k, q, 0)
                if has_next(k):
                    for c in range(2):
                        norms12(j, q + 1, c)
                        norm2(j, q + 1, c)
                if has_scan(k):
                    scan(k, 1, 0)
                    mask(k, 1, 0)
                if has_prev(k):
                    dve.wait_ge(fT_hi, at(i + 1))
                    dve.tensor_tensor(fT[1][:, :, :], trb[:, :].rearrange("p (k t) -> p k t", t=T), fT[0][:, :, :],
                                      ALU.subtract).then_inc(fT_lo, 1)
                for n in range(NT):
                    if has_prev(k):
                        hidden_lo(i, n, ffull, fc_hi, fc_lo)
                    if has_scan(k) and n == 3:
                        scan(k, 1, 1)
                        mask(k, 1, 1)
                if has_scan(k):
                    y_lo(k, 0)
                    gather_y(k, q, 1)
                    state(k, q, 1)
                    mean_square(k, 0)
                    norms34(k, q, 0)
                if has_next(k):
                    dve.wait_ge(uT_hi, at(j + 1))
                    dve.tensor_tensor(uT[1][:, :, :], trb[:, :].rearrange("p (k t) -> p k t", t=T), uT[0][:, :, :],
                                      ALU.subtract).then_inc(uT_lo, 1)
                    convolve(j)
                    time_steps(j, q + 1)
                if has_prev(k):
                    for c in range(2):
                        g = 2 * i + c
                        dve.wait_ge(fc2_done, at(g + 1))
                        dve.wait_ge(res_steps, at(2 * g + 2))
                        if c == 0 or True:
                            wait(dve, out_stored[c], 16 * i)
                        dve.tensor_tensor(ob[:, c, :], tmb[:, 0:DM], res[:, (q + 3) % 2, c, :],
                                          ALU.add).then_inc(out_ready, 1)
                if has_next(k):
                    running_products(j, q + 1)
                if known(k, lambda m: m + 2 < TILES):
                    split_x(k + 2, q + 2)

            def convolve(j):
                for n in range(0, NCV, 2):
                    for t in range(1, TAPS):
                        for m in (n, n + 1):
                            seq = 3 * (NCV * j + n)
                            if t == 1:
                                dve.wait_ge(tap0_done, at(NCV * j + m + 1))
                                dve.wait_ge(raw_done, at(NCV * j + m + 1))
                            else:
                                dve.wait_ge(taps, at(seq + 2 * (t - 2) + (m - n) + 1))
                            o = HALO - t
                            dve.scalar_tensor_tensor(out=acc[:, m % 3, :], in0=raw[:, m, o:o + T],
                                                     scalar=cw[:, m, HALO - t:HALO - t + 1], in1=acc[:, m % 3, :],
                                                     op0=ALU.mult, op1=ALU.add).then_inc(taps, 1)

            def time_steps(j, q):
                par = q % 2
                dve.wait_ge(dt_done, at(j + 1))
                dve.tensor_tensor(dtr[:, :, :], bcb[:, 0:2 * NH].rearrange("p (c h) -> p c h", c=2), dtb[:, :, :],
                                  ALU.add).then_inc(dt_vec, 1)
                dve.wait_ge(dt_vec, at(4 * j + 1))
                dve.wait_ge(dt_act, at(4 * j + 3))
                dve.scalar_tensor_tensor(out=dtt[:, par, :, :], in0=dtr[:, :, :], scalar=0.0, in1=dln[:, :, :],
                                         op0=ALU.max, op1=ALU.add).then_inc(dt_vec, 1)
                dve.wait_ge(dt_vec, at(4 * j + 2))
                dve.tensor_tensor(da[:, :, :], dtt[:, par, :, :], expa[:, :, :], ALU.mult).then_inc(dt_vec, 1)
                dve.wait_ge(dt_act, at(4 * j + 4))
                dve.tensor_scalar(decz[:, par, :, :], dec[:, :, :], notfirst[:, 0:1], None,
                                  ALU.mult).then_inc(dt_vec, 1)

            def running_products(j, q):
                par = q % 2
                dve.wait_ge(decT_done, at(j + 1))
                dve.tensor_tensor_scan(pT[:, :], bcb[0:2 * NH, P:2 * P], zeros[0:2 * NH, :], 1.0, ALU.mult,
                                       ALU.add).then_inc(pT_done, 1)
                dve.wait_ge(ppT_done, at(j + 1))
                dve.tensor_copy(pp[:, par, :, :, :].rearrange("p a c h -> p (a c h)"),
                                bcb[:, 2 * P:2 * P + 4 * NH]).then_inc(pp_done, 1)

            split_x(0, 0)
            steps(dve, step)


_INS = ['x', 'L0_tok_w1', 'L0_tok_b1', 'L0_tok_w2', 'L0_tok_b2', 'L0_tok_gamma', 'L0_tok_beta',
        'L0_attn_in_proj_w', 'L0_attn_conv_w', 'L0_attn_conv_b', 'L0_attn_norm_w', 'L0_attn_out_proj_w',
        'L0_attn_dt_bias', 'L0_attn_A_log', 'L0_attn_D_param', 'L0_ffn_ln_gamma', 'L0_ffn_ln_beta',
        'L0_ffn_fc1_q', 'L0_ffn_fc1_scales', 'L0_ffn_fc1_bias', 'L0_ffn_fc2_q', 'L0_ffn_fc2_scales',
        'L0_ffn_fc2_bias']
_OUTS = [((8, 1024, 256), 'float32')]


def kernel(**inputs):
    import numpy as _np
    import concourse.bacc as _bacc
    from concourse import mybir as _mybir
    from concourse.bass_utils import run_bass_kernel_spmd as _run

    nc = _bacc.Bacc("TRN2", target_bir_lowering=False, num_devices=1)
    arrays, args = {}, []
    for name in _INS:
        a = _np.ascontiguousarray(inputs[name])
        arrays[f"in_{name}_dram"] = a
        args.append(nc.dram_tensor(f"in_{name}_dram", a.shape, _mybir.dt.from_np(a.dtype), kind="ExternalInput").ap())
    for i, (shape, dtype) in enumerate(_OUTS):
        dt = _mybir.dt.from_np(_np.dtype(dtype))
        args.append(nc.dram_tensor(f"out_{i}_dram", shape, dt, kind="ExternalOutput").ap())
    vit_tower(nc, *args)
    r = _run(nc, [arrays], core_ids=[0])
    got = tuple(r.results[0][f"out_{i}_dram"] for i in range(len(_OUTS)))
    return got[0]
```

```python
from contextlib import ExitStack

import concourse.bass as bass
from concourse import mybir

ALU = mybir.AluOpType
ACT = mybir.ActivationFunctionType
F32 = mybir.dt.float32
F32R = mybir.dt.float32r
I32 = mybir.dt.int32

P = 128
EPS = 1e-5


class Count:

    def __init__(self, loop, per, extra):
        self.loop, self.per, self.extra = loop, per, extra

    def __add__(self, n):
        return Count(self.loop, self.per, self.extra + n)

    def __sub__(self, n):
        return Count(self.loop, self.per, self.extra - n)

    def __mul__(self, n):
        return Count(self.loop, self.per * n, self.extra * n)

    __radd__, __rmul__ = __add__, __mul__


class Loop:

    def __init__(self, eng, image, registers):
        self.eng, self.image, self.used = eng, image, 0
        self.product, *self.registers = registers

    def register(self, count):
        r = self.registers[self.used % len(self.registers)]
        self.used += 1
        self.eng.reg_mul(self.product, self.image, count.per)
        self.eng.reg_add(r, self.product, count.extra)
        return r


def at(value):
    return value.loop.register(value) if isinstance(value, Count) else value


def vit_tower(nc, x, tok_w1, tok_b1, tok_w2, tok_b2, tok_gamma, tok_beta, in_proj_w, conv_w, conv_b,
              norm_w, out_proj_w, dt_bias, A_log, D_param, ln_gamma, ln_beta, fc1_q, fc1_scales,
              fc1_bias, fc2_q, fc2_scales, fc2_bias, out):
    B, CIN, HH, WW = x.shape
    HR, WR = HH // 2, WW // 2
    L = HR * WR
    HID = tok_w1.shape[1]
    DM = tok_w2.shape[1]
    NH = dt_bias.shape[0]
    DI = out_proj_w.shape[1]
    HD = DI // NH
    NS = (conv_w.shape[0] - DI) // 2
    TAPS = conv_w.shape[2]
    HALO = TAPS - 1
    E_ALL = in_proj_w.shape[0]
    T = 2 * P
    TILES = B * L // T
    PER_B = L // T
    ROWS = T // WR
    NT = HID // P
    KM = DM // P
    KI = DI // P
    NCV = conv_w.shape[0] // P
    RING = 4
    assert CIN * 4 == 2 * P and KM == 2 and NS == P and PER_B == 4 and fc1_q.shape[1] == HID

    ctx = ExitStack()
    with ctx:
        def sb(name, shape, dt=F32):
            return ctx.enter_context(nc.sbuf_tensor(name, shape, dt))

        def sem(name):
            return ctx.enter_context(nc.semaphore(name))

        w1 = [sb(f"w1_{p}", [P, KM, HID], F32R) for p in ("hi", "lo")]
        w2 = [sb(f"w2_{p}", [P, NT, DM], F32R) for p in ("hi", "lo")]
        win = [sb(f"win_{p}", [P, KM, E_ALL], F32R) for p in ("hi", "lo")]
        wout = [sb(f"wout_{p}", [P, KI, DM], F32R) for p in ("hi", "lo")]
        f1 = [sb(f"f1_{p}", [P, KM, HID], F32R) for p in ("hi", "lo")]
        f2 = [sb(f"f2_{p}", [P, NT, DM], F32R) for p in ("hi", "lo")]
        ident = sb("ident", [P, P])
        ident4 = sb("ident4", [P, 4, P])
        zeros = sb("zeros", [P, P])
        notfirst = sb("notfirst", [P, 1])
        b1c = sb("b1c", [P, NT])
        fcb = sb("fcb", [P, NT])
        fcb_raw = sb("fcb_raw", [P, NT])
        fcb_part = sb("fcb_part", [P, NT])
        cw = sb("cw", [P, NCV, TAPS])
        cb = sb("cb", [P, NCV])
        nw = sb("nw", [P, KI])
        lng = sb("lng", [P, KM])
        lnb = sb("lnb", [P, KM])
        gam = sb("gam", [P, DM])
        bet = sb("bet", [P, DM])
        b2r = sb("b2r", [P, DM])
        fb2 = sb("fb2", [P, DM])
        dpar = sb("dpar", [P, NH])
        dtb = sb("dtb", [P, 2, NH])
        alog = sb("alog", [P, 2, NH])
        expa = sb("expa", [P, 2, NH])
        xin = [sb(f"xin{i}", [P, ROWS * WW]) for i in range(2)]
        xs = [sb(f"xs_{p}", [P, 2, T], F32R) for p in ("hi", "lo")]
        hfull = sb("hfull", [P, RING, T])
        ffull = sb("ffull", [P, RING, T])
        hid = [sb(f"hid_{p}", [P, NT, T], F32R) for p in ("hi", "lo")]
        ytok = sb("ytok", [P, 2, DM])
        h1 = sb("h1", [P, 2, 2, DM])
        u = sb("u", [P, 2, DM])
        uT = [sb(f"uT_{p}", [P, KM, T], F32R) for p in ("hi", "lo")]
        raw = sb("raw", [P, NCV, HALO + T])
        acc = sb("acc", [P, 3, T])
        xc = sb("xc", [P, NCV, T])
        sz = sb("sz", [P, 2, DI])
        dtr = sb("dtr", [P, 2, NH])
        dab = sb("dab", [P, 2, NH])
        dex = sb("dex", [P, 2, NH])
        dln = sb("dln", [P, 2, NH])
        dtt = sb("dtt", [P, 2, 2, NH])
        da = sb("da", [P, 2, NH])
        dec = sb("dec", [P, 2, NH])
        decz = sb("decz", [P, 2, 2, NH])
        pT = sb("pT", [2 * NH, P])
        pp = sb("pp", [P, 2, 2, 2, NH])
        xtm = sb("xtm", [P, DI])
        xdt = sb("xdt", [P, DI])
        xw = sb("xw", [P, DI])
        btm = sb("btm", [P, NS])
        dmat = sb("dmat", [P, NH, P])
        dlast = sb("dlast", [P, NH])
        S = sb("S", [P, DI])
        yb = sb("yb", [P, 2, DI])
        sq = sb("sq", [P, DI])
        ssum = sb("ssum", [P, 2])
        yr = sb("yr", [P, 2])
        yT = [sb(f"yT_{p}", [P, KI, P], F32R) for p in ("hi", "lo")]
        h2 = sb("h2", [P, 2, DM])
        x3 = sb("x3", [P, 2, DM])
        res = sb("res", [P, 2, 2, DM])
        f = sb("f", [P, 2, DM])
        fT = [sb(f"fT_{p}", [P, KM, T], F32R) for p in ("hi", "lo")]
        ob = sb("ob", [P, 2, DM])
        st = sb("st", [P, 4, 6])
        mv = sb("mv", [P, 4, 2, 2])
        veps = sb("veps", [P, 4, 2])
        negm = sb("negm", [P, 4, 2])
        mhalf = sb("mhalf", [P, 1])
        msq = sb("msq", [P, 2])
        rstd = sb("rstd", [P, 4, 2])
        nb = sb("nb", [P, 4, 2])

        def bank(name):
            return ctx.enter_context(nc.psum_tensor(name, [P, 512], F32))

        wide = [bank("wide0"), bank("wide1")]
        tmb = bank("tmb")
        trb = bank("trb")
        bcb = bank("bcb")
        yib = bank("yib")
        yxb = bank("yxb")
        dsb = bank("dsb")

        waits_passed = sem("waits_passed")
        x_loaded = [sem("x_loaded0"), sem("x_loaded1")]
        const_loaded = sem("const_loaded")
        w_loaded = [sem("w_loaded0"), sem("w_loaded1")]
        scale_loaded = [sem("scale_loaded0"), sem("scale_loaded1")]
        ident_ready = sem("ident_ready")
        const_ready = sem("const_ready")
        expa_ready = sem("expa_ready")
        dequant = sem("dequant")
        w_turned = sem("w_turned")
        w_hi = sem("w_hi")
        w_lo = sem("w_lo")
        beta_product = sem("beta_product")
        fcb_ready = sem("fcb_ready")
        xs_hi = sem("xs_hi")
        xs_lo = sem("xs_lo")
        tok1_done = sem("tok1_done")
        gelu_done = sem("gelu_done")
        tok_hi = sem("tok_hi")
        tok_lo = sem("tok_lo")
        tok2_done = sem("tok2_done")
        y_stats = sem("y_stats")
        h1_stats = sem("h1_stats")
        norm1_done = sem("norm1_done")
        h1_steps = sem("h1_steps")
        u_done = sem("u_done")
        uT_done = sem("uT_done")
        uT_hi = sem("uT_hi")
        uT_lo = sem("uT_lo")
        xbc_done = sem("xbc_done")
        halo_ready = sem("halo_ready")
        raw_done = sem("raw_done")
        tap0_done = sem("tap0_done")
        taps = sem("taps")
        xc_done = sem("xc_done")
        z_done = sem("z_done")
        sz_done = sem("sz_done")
        dt_done = sem("dt_done")
        dt_act = sem("dt_act")
        dt_vec = sem("dt_vec")
        decT_done = sem("decT_done")
        pT_done = sem("pT_done")
        ppT_done = sem("ppT_done")
        pp_done = sem("pp_done")
        xT_done = sem("xT_done")
        bT_done = sem("bT_done")
        bc_done = sem("bc_done")
        bcast_done = sem("bcast_done")
        xtm_done = sem("xtm_done")
        btm_done = sem("btm_done")
        scan_done = sem("scan_done")
        dlast_done = sem("dlast_done")
        mask_done = sem("mask_done")
        xdt_done = sem("xdt_done")
        xd_done = sem("xd_done")
        xw_done = sem("xw_done")
        yinter_done = sem("yinter_done")
        yintra_done = sem("yintra_done")
        ds_done = sem("ds_done")
        s_decayed = sem("s_decayed")
        s_done = sem("s_done")
        ya_done = sem("ya_done")
        yb_done = sem("yb_done")
        y_steps = sem("y_steps")
        sq_done = sem("sq_done")
        msq_done = sem("msq_done")
        yr_done = sem("yr_done")
        pow_y = sem("pow_y")
        pow_h1 = sem("pow_h1")
        pow_h2 = sem("pow_h2")
        pow_x3 = sem("pow_x3")
        yT_done = sem("yT_done")
        yT_hi = sem("yT_hi")
        yT_lo = sem("yT_lo")
        outp_done = sem("outp_done")
        h2_stats = sem("h2_stats")
        x3_stats = sem("x3_stats")
        x3_done = sem("x3_done")
        f_done = sem("f_done")
        res_steps = sem("res_steps")
        fT_done = sem("fT_done")
        fT_hi = sem("fT_hi")
        fT_lo = sem("fT_lo")
        fc1_done = sem("fc1_done")
        silu_done = sem("silu_done")
        fc_hi = sem("fc_hi")
        fc_lo = sem("fc_lo")
        fc2_done = sem("fc2_done")
        out_ready = sem("out_ready")
        out_stored = [sem("out_stored0"), sem("out_stored1")]

        def wait(eng, s, value):
            if not (isinstance(value, int) and value <= 0):
                eng.wait_ge(s, at(value))

        def passed(eng):
            eng.sem_inc(waits_passed, 1)

        def steps(eng, step):
            step(-1, PER_B - 1)
            for q in range(PER_B):
                step(q, q)
            registers = [eng.alloc_register(f"count{i}") for i in range(5)]
            with eng.Fori(0, B - 2) as b:
                loop = Loop(eng, b, registers)
                for q in range(PER_B):
                    step(Count(loop, PER_B, PER_B + q), q)
            for q in range(PER_B):
                step(TILES - PER_B + q, q)
            step(TILES, 0)

        def known(k, test):
            return test(k) if isinstance(k, int) else True

        def has_next(k):
            return known(k, lambda i: i + 1 < TILES)

        def has_scan(k):
            return known(k, lambda i: 0 <= i < TILES)

        def has_prev(k):
            return known(k, lambda i: i >= 1)

        def heads(ap):
            return ap.rearrange("p (h d) -> p h d", h=NH)

        def per_head(ap):
            return ap.unsqueeze(2).to_broadcast([P, NH, HD])

        stage = [dmat[:, :, :].rearrange("p h t -> p (h t)"), yb[:, :, :].rearrange("p c n -> p (c n)")]
        scale_stage = [h1[:, :, :, :].rearrange("p a c n -> p (a c n)"),
                       res[:, :, :, :].rearrange("p a c n -> p (a c n)")]
        W1ROWS = tok_w1.rearrange("(c a b) n -> a c b n", a=2, b=2)
        LOADS = []
        LOADS += [("w1", k) for k in range(KM)] + [("w2", k) for k in range(2)]
        LOADS += [("win", k) for k in range(3)] + [("wout", 0)]
        LOADS += [("f1", k) for k in range(KM)] + [("f2", k) for k in range(2)]
        HALF = NT // 2

        def parts(kind, i):
            if kind == "w1":
                return [[w[:, i, :] for w in w1]]
            if kind == "w2":
                return [[w[:, i * HALF:(i + 1) * HALF, :].rearrange("p k n -> p (k n)") for w in w2]]
            if kind == "win":
                e0, e1 = i * 4 * P, min((i + 1) * 4 * P, E_ALL)
                return [[w[:, k, e0:e1] for w in win] for k in range(KM)]
            if kind == "wout":
                return [[w[:, k, :] for w in wout] for k in range(KI)]
            if kind == "f1":
                return [[w[:, i, :] for w in f1]]
            return [[w[:, i * HALF:(i + 1) * HALF, :].rearrange("p k n -> p (k n)") for w in f2]]

        FIRST_PART, n_parts = [], 0
        for kind, i in LOADS:
            FIRST_PART.append(n_parts)
            n_parts += len(parts(kind, i))
        FIRST_PART.append(n_parts)
        IN_FC = [n for n, (kind, _) in enumerate(LOADS) if kind in ("f1", "f2")]
        TURNED = [n for n, (kind, _) in enumerate(LOADS) if kind in ("win", "wout")]

        def part_source(n, p):
            kind, i = LOADS[n]
            if kind == "win":
                width = min(4 * P, E_ALL - i * 4 * P)
                return wide[p][:, 0:width]
            if kind == "wout":
                return wide[p % 2][:, (p // 2) * DM:(p // 2 + 1) * DM]
            return stage[n % 2]

        def load_count(n):
            return 16 * sum(2 if LOADS[m][0] == "w1" or LOADS[m] == ("win", 2) else 1 for m in range(n % 2, n + 1, 2))

        def part_scale(n, p):
            kind, i = LOADS[n]
            if kind == "wout":
                return nw[:, p:p + 1]
            if kind == "f1":
                return lng[:, i:i + 1]
            return 0.5 if kind == "f2" else 1.0

        block = ctx.enter_context(nc.Block())

        CONSTS = [
            (b1c[:, :], tok_b1.rearrange("(n p) -> p n", p=P)),
            (fcb_raw[:, :], fc1_bias.rearrange("(n p) -> p n", p=P)),
            (cw[:, :, :], conv_w.rearrange("(n p) o k -> p n (o k)", p=P)),
            (cb[:, :], conv_b.rearrange("(n p) -> p n", p=P)),
            (nw[:, :], norm_w.rearrange("(n p) -> p n", p=P)),
            (lng[:, :], ln_gamma.rearrange("(n p) -> p n", p=P)),
            (lnb[:, :], ln_beta.rearrange("(n p) -> p n", p=P)),
            (gam[:, :], tok_gamma.partition_broadcast(P)),
            (bet[:, :], tok_beta.partition_broadcast(P)),
            (b2r[:, :], tok_b2.partition_broadcast(P)),
            (fb2[:, :], fc2_bias.partition_broadcast(P)),
            (dpar[:, :], D_param.partition_broadcast(P)),
            (dtb[:, 0, :], dt_bias.partition_broadcast(P)),
            (dtb[:, 1, :], dt_bias.partition_broadcast(P)),
            (alog[:, 0, :], A_log.partition_broadcast(P)),
            (alog[:, 1, :], A_log.partition_broadcast(P)),
        ]
        x_rows = x.rearrange("i c (t r a) w -> a i t c r w", a=2, r=ROWS)
        out_rows = out.rearrange("i (t p) n -> (i t) p n", p=P)

        @block.sync
        def _(sp):
            def load_x(j, q):
                if not (isinstance(j, int) and j >= TILES):
                    wait(sp, xs_hi, j - 1)
                    wait(sp, xs_lo, j - 1)
                    if isinstance(j, int):
                        img = j // PER_B
                    else:
                        img = (j - q % PER_B) // PER_B
                    for a in range(2):
                        sp.dma_start(xin[q % 2][a * CIN:(a + 1) * CIN, :].rearrange("c (r w) -> c r w", w=WW),
                                     x_rows[a, img, q % PER_B]).then_inc(x_loaded[q % 2], 16)

            def step(k, q):
                if isinstance(k, int):
                    load_x(k + 4, q)
                else:
                    wait(sp, xs_hi, k + 3)
                    wait(sp, xs_lo, k + 3)
                    for a in range(2):
                        sp.dma_start(xin[q % 2][a * CIN:(a + 1) * CIN, :].rearrange("c (r w) -> c r w", w=WW),
                                     x_rows[a, bass.ds(k.loop.image + 2, 1), q][0]).then_inc(x_loaded[q % 2], 16)
                if has_prev(k):
                    for c in range(2):
                        g = 2 * (k - 1) + c
                        sp.wait_ge(out_ready, at(g + 1))
                        dst = out_rows[g] if isinstance(k, int) else out_rows[bass.ds(g.loop.image * g.per + g.extra, 1)][0]
                        sp.dma_start(dst, ob[:, c, :]).then_inc(out_stored[c], 16)

            for j in range(2):
                load_x(j, j)
            for n, (kind, i) in enumerate(LOADS):
                if n >= 2:
                    sp.wait_ge(w_lo, at(FIRST_PART[n - 1]))
                if n - 2 in IN_FC and LOADS[n - 2][0] == "f1":
                    sp.wait_ge(beta_product, at(IN_FC.index(n - 2) + 1))
                dst, s = stage[n % 2], w_loaded[n % 2]
                if kind == "w1":
                    for a in range(2):
                        sp.dma_start(dst[a * CIN:(a + 1) * CIN, :], W1ROWS[a, :, i, :]).then_inc(s, 16)
                elif kind == "w2":
                    sp.dma_start(dst.rearrange("p (k n) -> p k n", n=DM),
                                 tok_w2[i * HALF * P:(i + 1) * HALF * P, :].rearrange("(k p) n -> p k n", p=P)).then_inc(s, 16)
                elif kind == "win":
                    rows = min(4 * P, E_ALL - i * 4 * P)
                    full = rows // P
                    sp.dma_start(dst[:, 0:full * DM].rearrange("p (k n) -> p k n", n=DM),
                                 in_proj_w[i * 4 * P:(i * 4 + full) * P, :].rearrange("(k p) n -> p k n", p=P)).then_inc(s, 16)
                    if rows % P:
                        sp.dma_start(dst[0:NH, full * DM:(full + 1) * DM], in_proj_w[E_ALL - NH:E_ALL, :]).then_inc(s, 16)
                elif kind == "wout":
                    sp.dma_start(dst.rearrange("p (k n) -> p k n", n=DI),
                                 out_proj_w.rearrange("(k p) n -> p k n", p=P)).then_inc(s, 16)
                else:
                    o = IN_FC.index(n)
                    if o >= 2:
                        sp.wait_ge(dequant, at(o - 1))
                    sdst = scale_stage[o % 2]
                    if kind == "f1":
                        sp.dma_start(dst.bitcast(I32), fc1_q[i * P:(i + 1) * P, :]).then_inc(s, 16)
                        sp.dma_start(sdst, fc1_scales[i].partition_broadcast(P)).then_inc(scale_loaded[o % 2], 16)
                    else:
                        sp.dma_start(dst.bitcast(I32).rearrange("p (k n) -> p k n", n=DM),
                                     fc2_q[i * HALF * P:(i + 1) * HALF * P, :].rearrange("(k p) n -> p k n", p=P)).then_inc(s, 16)
                        sp.dma_start(sdst.rearrange("p (k n) -> p k n", n=DM),
                                     fc2_scales[i * HALF:(i + 1) * HALF, :].partition_broadcast(P)).then_inc(scale_loaded[o % 2], 16)
                if n == 0:
                    for dst, src in CONSTS:
                        sp.dma_start(dst, src, allow_slow_non_contiguous=True).then_inc(const_loaded, 16)
            load_x(2, 2)
            steps(sp, step)
            for c in range(2):
                sp.wait_ge(out_stored[c], at(16 * TILES))

        @block.gpsimd
        def _(pool):
            pool.memset(ident[:, :], 0.0).then_inc(ident_ready, 1)
            pool.memset(ident4[:, :, :], 0.0).then_inc(ident_ready, 1)
            pool.memset(notfirst[:, :], 1.0).then_inc(ident_ready, 1)
            pool.memset(zeros[:, :], 0.0).then_inc(ident_ready, 1)
            pool.memset(S[:, :], 0.0).then_inc(ident_ready, 1)
            pool.memset(mhalf[:, :], -0.5).then_inc(ident_ready, 1)
            pool.wait_ge(ident_ready, 6)
            pool.affine_select(out=ident[:, :], in_=ident[:, :], compare_op=ALU.not_equal, fill=1.0, base=0,
                               pattern=[[-1, P]], channel_multiplier=1).then_inc(ident_ready, 1)
            pool.affine_select(out=ident4[:, :, :], in_=ident4[:, :, :], compare_op=ALU.not_equal, fill=1.0,
                               base=0, pattern=[[0, 4], [-1, P]], channel_multiplier=1).then_inc(ident_ready, 1)
            pool.affine_select(out=notfirst[:, :], in_=notfirst[:, :], compare_op=ALU.not_equal, fill=0.0,
                               base=0, pattern=[[0, 1]], channel_multiplier=1).then_inc(ident_ready, 1)

            def scale_x(k, q, c):
                g, par = 2 * k + c, q % 2
                pool.wait_ge(xtm_done, at(g + 1))
                wait(pool, yintra_done, g)
                pool.tensor_tensor(heads(xdt[:, :]), heads(xtm[:, :]), per_head(dtt[:, par, c, :]),
                                   ALU.mult).then_inc(xdt_done, 1)

            def skip_x(k, c):
                g = 2 * k + c
                pool.wait_ge(xdt_done, at(g + 1))
                pool.tensor_tensor(heads(xtm[:, :]), heads(xtm[:, :]), per_head(dpar[:, :]),
                                   ALU.mult).then_inc(xd_done, 1)

            def decay_x(k, c):
                g = 2 * k + c
                pool.wait_ge(xdt_done, at(g + 1))
                pool.wait_ge(dlast_done, at(2 * g + 2))
                wait(pool, ds_done, g)
                pool.tensor_tensor(heads(xw[:, :]), heads(xdt[:, :]), per_head(dlast[:, :]),
                                   ALU.mult).then_inc(xw_done, 1)

            def decay_state(k, q, c):
                g, par = 2 * k + c, q % 2
                pool.wait_ge(yinter_done, at(g + 1))
                pool.wait_ge(pp_done, at(k + 1))
                wait(pool, s_done, g)
                pool.tensor_tensor(heads(S[:, :]), heads(S[:, :]), per_head(pp[:, par, 1, c, :]),
                                   ALU.mult).then_inc(s_decayed, 1)

            def gate(k, c):
                g = 2 * k + c
                pool.wait_ge(yb_done, at(g + 1))
                pool.wait_ge(xd_done, at(g + 1))
                pool.tensor_tensor(yb[:, c, :], yb[:, c, :], xtm[:, :], ALU.add).then_inc(y_steps, 1)
                pool.wait_ge(y_steps, at(2 * g + 1))
                pool.wait_ge(sz_done, at(g + 1))
                pool.tensor_tensor(yb[:, c, :], yb[:, c, :], sz[:, c, :], ALU.mult).then_inc(y_steps, 1)

            def inverse_rms(k, c):
                g = 2 * k + c
                pool.wait_ge(msq_done, at(g + 1))
                pool.tensor_tensor(yr[:, c:c + 1], msq[:, c:c + 1], mhalf[:, :], ALU.pow).then_inc(yr_done, 1)

            def inverse_std(which, c, stats, stats_count, powers, base):
                pool.wait_ge(stats, at(stats_count))
                pool.tensor_tensor(rstd[:, which, c:c + 1], veps[:, which, c:c + 1], mhalf[:, :],
                                   ALU.pow).then_inc(powers, 1)
                pool.wait_ge(powers, at(base + 1))
                pool.tensor_tensor(nb[:, which, c:c + 1], negm[:, which, c:c + 1], rstd[:, which, c:c + 1],
                                   ALU.mult).then_inc(powers, 1)

            def std_h2(k, c):
                g = 2 * k + c
                inverse_std(2, c, h2_stats, 5 * g + 5, pow_h2, 2 * g)

            def std_x3(k, c):
                g = 2 * k + c
                inverse_std(3, c, x3_stats, 4 * g + 4, pow_x3, 2 * g)

            def std_y(j, c):
                g = 2 * j + c
                inverse_std(0, c, y_stats, 5 * g + 5, pow_y, 2 * g)

            def std_h1(j, c):
                g = 2 * j + c
                inverse_std(1, c, h1_stats, 4 * g + 4, pow_h1, 2 * g)

            def residual(k, q, c):
                g, par = 2 * k + c, q % 2
                pool.wait_ge(x3_done, at(g + 1))
                wait(pool, out_ready, g - 3)
                pool.tensor_tensor(res[:, par, c, :], h2[:, c, :], x3[:, c, :], ALU.add).then_inc(res_steps, 1)
                pool.wait_ge(res_steps, at(2 * g + 1))
                pool.tensor_tensor(res[:, par, c, :], res[:, par, c, :], fb2[:, :], ALU.add).then_inc(res_steps, 1)

            def affine(j, q, c):
                g, par = 2 * j + c, q % 2
                pool.wait_ge(norm1_done, at(g + 1))
                wait(pool, h2_stats, 5 * (g - 4) + 1)
                pool.tensor_tensor(h1[:, par, c, :], ytok[:, c, :], gam[:, :], ALU.mult).then_inc(h1_steps, 1)
                pool.wait_ge(h1_steps, at(2 * g + 1))
                pool.tensor_tensor(h1[:, par, c, :], h1[:, par, c, :], bet[:, :], ALU.add).then_inc(h1_steps, 1)

            def halo(j, q):
                wait(pool, taps, 3 * NCV * j)
                passed(pool)
                if q % PER_B == 0:
                    pool.memset(raw[:, :, 0:HALO], 0.0).then_inc(halo_ready, 1)
                else:
                    pool.tensor_copy(raw[:, :, 0:HALO], raw[:, :, T:T + HALO]).then_inc(halo_ready, 1)

            def step(k, q):
                j, i = k + 1, k - 1
                if has_scan(k):
                    scale_x(k, q, 0)
                if has_prev(k):
                    std_x3(i, 1)
                if has_scan(k):
                    decay_x(k, 0)
                    skip_x(k, 0)
                if has_prev(k):
                    residual(i, q - 1, 1)
                if has_scan(k):
                    decay_state(k, q, 0)
                    gate(k, 0)
                if has_next(k):
                    halo(j, q + 1)
                    std_y(j, 0)
                    affine(j, q + 1, 0)
                if has_scan(k):
                    inverse_rms(k, 0)
                if has_next(k):
                    std_y(j, 1)
                if has_scan(k):
                    scale_x(k, q, 1)
                if has_next(k):
                    std_h1(j, 0)
                    affine(j, q + 1, 1)
                if has_scan(k):
                    std_h2(k, 0)
                if has_next(k):
                    std_h1(j, 1)
                if has_scan(k):
                    decay_x(k, 1)
                    skip_x(k, 1)
                    std_x3(k, 0)
                    decay_state(k, q, 1)
                    gate(k, 1)
                    residual(k, q, 0)
                    inverse_rms(k, 1)
                    std_h2(k, 1)

            pool.wait_ge(const_ready, at(1))
            pool.wait_ge(dequant, at(len(IN_FC)))
            steps(pool, step)

        @block.scalar
        def _(act):
            act.wait_ge(const_loaded, at(16 * len(CONSTS)))
            act.activation(expa[:, :, :], alog[:, :, :], ACT.Exp).then_inc(expa_ready, 1)
            for n, (kind, i) in enumerate(LOADS):
                for p, (hi, lo) in enumerate(parts(kind, i)):
                    if n in TURNED:
                        act.wait_ge(w_turned, at(TURNED.index(n) + 1))
                        if p >= 2:
                            act.wait_ge(w_lo, FIRST_PART[n] + p - 1)
                    elif n in IN_FC:
                        act.wait_ge(dequant, at(IN_FC.index(n) + 1))
                    else:
                        act.wait_ge(w_loaded[n % 2], at(load_count(n)))
                    act.activation(hi, part_source(n, p), ACT.Copy, scale=part_scale(n, p)).then_inc(w_hi, 1)

            def split_x(j, q):
                act.wait_ge(x_loaded[q % 2], at(32 * count_pairs(j, q)))
                wait(act, tok1_done, NT * j)
                act.activation(xs[0][:, :, :], xin[q % 2][:, :].rearrange("p (t b) -> p b t", b=2),
                               ACT.Copy).then_inc(xs_hi, 1)

            def x_and_b(k, c):
                g = 2 * k + c
                act.wait_ge(xT_done, at(g + 1))
                wait(act, y_steps, 2 * g - 1)
                act.activation(xtm[:, :], trb[:, :], ACT.Copy).then_inc(xtm_done, 1)
                act.wait_ge(bT_done, at(g + 1))
                wait(act, ds_done, g)
                act.activation(btm[:, :], yib[:, 0:NS], ACT.Copy).then_inc(btm_done, 1)

            def y_turned(k, c):
                g = 2 * k + c
                act.wait_ge(yT_done, at(g + 1))
                wait(act, outp_done, g)
                act.activation(yT[0][:, :, :], trb[:, :].rearrange("p (k t) -> p k t", t=P),
                               ACT.Copy).then_inc(yT_hi, 1)

            def normalise(dst, src, which, c):
                return act.activation(dst, src, ACT.Identity, scale=rstd[:, which, c:c + 1],
                                      bias=nb[:, which, c:c + 1])

            def norm_x3(k, c):
                g = 2 * k + c
                act.wait_ge(pow_h2, at(2 * g + 2))
                wait(act, res_steps, 2 * g - 3)
                normalise(x3[:, c, :], h2[:, c, :], 2, c).then_inc(x3_done, 1)

            def norm_f(k, c):
                g = 2 * k + c
                act.wait_ge(pow_x3, at(2 * g + 2))
                wait(act, fT_done, k)
                normalise(f[:, c, :], x3[:, c, :], 3, c).then_inc(f_done, 1)

            def norm_y(j, c):
                g = 2 * j + c
                act.wait_ge(pow_y, at(2 * g + 2))
                normalise(ytok[:, c, :], ytok[:, c, :], 0, c).then_inc(norm1_done, 1)

            def norm_u(j, q, c):
                g = 2 * j + c
                act.wait_ge(pow_h1, at(2 * g + 2))
                wait(act, uT_done, j)
                normalise(u[:, c, :], h1[:, q % 2, c, :], 1, c).then_inc(u_done, 1)

            def square(k, c):
                g = 2 * k + c
                act.wait_ge(y_steps, at(2 * g + 2))
                wait(act, sq_done, g)
                wait(act, msq_done, g - 1)
                act.activation(sq[:, :], yb[:, c, :], ACT.Square, accum_out=ssum[:, c:c + 1]).then_inc(sq_done, 1)

            def hidden(i, func, bias, done, full, full_done, hi_done, lo_done, hid_free, between):
                for n in range(NT + 1):
                    if n < NT:
                        act.wait_ge(done, at(NT * i + n + 1))
                        wait(act, lo_done, NT * i + n + 1 - RING)
                        act.activation(full[:, n % RING, :], wide[n % 2][:, 0:T], func,
                                       bias=bias[:, n:n + 1]).then_inc(full_done, 1)
                    if n >= 1:
                        if n == 1:
                            wait(act, *hid_free)
                        act.wait_ge(full_done, at(NT * i + n))
                        act.activation(hid[0][:, n - 1, :], full[:, (n - 1) % RING, :], ACT.Copy).then_inc(hi_done, 1)
                    between(n)

            def step(k, q):
                j, i = k + 1, k - 1

                def in_tok1(n):
                    if has_scan(k) and n == 1:
                        x_and_b(k, 0)
                    if has_prev(k) and n == 4:
                        norm_f(i, 1)

                def in_fc1(n):
                    if has_next(k) and n in (0, 4):
                        norm_u(j, q + 1, n // 4)
                    if has_scan(k) and n == 3:
                        norm_x3(k, 0)

                if has_next(k):
                    hidden(j, ACT.Gelu, b1c, tok1_done, hfull, gelu_done, tok_hi, tok_lo,
                           (fc2_done, 2 * (j - 2)), in_tok1)
                else:
                    for n in range(NT):
                        in_tok1(n)
                if has_scan(k):
                    square(k, 0)
                    y_turned(k, 0)
                if has_prev(k):
                    act.wait_ge(fT_done, at(i + 1))
                    wait(act, fc1_done, NT * i)
                    act.activation(fT[0][:, :, :], yxb[:, :].rearrange("p (k t) -> p k t", t=T),
                                   ACT.Copy).then_inc(fT_hi, 1)
                if has_next(k):
                    norm_y(j, 0)
                if has_scan(k):
                    x_and_b(k, 1)
                if has_next(k):
                    norm_y(j, 1)
                if known(k, lambda i: i + 2 < TILES):
                    split_x(k + 2, q + 2)
                if has_prev(k):
                    hidden(i, ACT.Silu, fcb, fc1_done, ffull, silu_done, fc_hi, fc_lo,
                           (tok2_done, 2 * j + 2) if has_next(k) else (fc2_done, 2 * i), in_fc1)
                else:
                    for n in range(NT):
                        in_fc1(n)
                if has_next(k):
                    act.wait_ge(uT_done, at(j + 1))
                    wait(act, dt_done, j)
                    act.activation(uT[0][:, :, :], trb[:, :].rearrange("p (k t) -> p k t", t=T),
                                   ACT.Copy).then_inc(uT_hi, 1)
                if has_scan(k):
                    square(k, 1)
                    norm_f(k, 0)
                    y_turned(k, 1)
                if has_next(k):
                    act.wait_ge(halo_ready, at(j + 1))
                    for n in range(NCV):
                        m = NCV * j + n
                        act.wait_ge(xbc_done, at(m + 1))
                        act.activation(raw[:, n, HALO:HALO + T], wide[n % 2][:, 0:T], ACT.Copy).then_inc(raw_done, 1)
                        wait(act, xc_done, m - 2)
                        act.activation(acc[:, n % 3, :], wide[n % 2][:, 0:T], ACT.Identity,
                                       scale=cw[:, n, HALO:TAPS], bias=cb[:, n:n + 1]).then_inc(tap0_done, 1)
                        if n >= 2:
                            conv_silu(k, j, n - 2)
                    for c in range(2):
                        act.wait_ge(z_done, at(2 * j + c + 1))
                        wait(act, y_steps, 4 * j - 2 + 2 * c)
                        act.activation(sz[:, c, :], wide[c][:, :], ACT.Silu).then_inc(sz_done, 1)
                if has_scan(k):
                    norm_x3(k, 1)
                if has_next(k):
                    for n in range(NCV - 2, NCV):
                        conv_silu(k, j, n)
                    act.preload_act_table_set("natural_log_exp_and_others")
                    act.wait_ge(dt_vec, at(4 * j + 1))
                    act.activation(dab[:, :, :], dtr[:, :, :], ACT.Abs).then_inc(dt_act, 1)
                    act.wait_ge(dt_act, at(4 * j + 1))
                    act.activation(dex[:, :, :], dab[:, :, :], ACT.Exp, scale=-1.0).then_inc(dt_act, 1)
                    act.wait_ge(dt_act, at(4 * j + 2))
                    act.activation(dln[:, :, :], dex[:, :, :], ACT.Ln, bias=1.0).then_inc(dt_act, 1)
                    act.wait_ge(dt_vec, at(4 * j + 3))
                    wait(act, decT_done, j)
                    act.activation(dec[:, :, :], da[:, :, :], ACT.Exp, scale=-1.0).then_inc(dt_act, 1)

            def conv_silu(k, j, n):
                act.wait_ge(taps, at(3 * (NCV * j + n - n % 2) + 2 * HALO - 1 + n % 2))
                if n == 0:
                    wait(act, xT_done, 2 * j)
                    wait(act, bT_done, 2 * j)
                    wait(act, yinter_done, 2 * j)
                act.activation(xc[:, n, :], acc[:, n % 3, :], ACT.Silu).then_inc(xc_done, 1)

            def count_pairs(j, q):
                return j // 2 + 1 if isinstance(j, int) else Count(j.loop, j.per // 2, j.extra // 2 + 1)

            split_x(0, 0)
            steps(act, step)

        @block.tensor
        def _(pe):
            def product(dst, pairs):
                n = len(pairs)
                for m, (lhs, rhs) in enumerate(pairs):
                    pe.matmul(dst, lhs[0], rhs[0], start=(m == 0), stop=False)
                    pe.matmul(dst, lhs[0], rhs[1], start=False, stop=False)
                    last = pe.matmul(dst, lhs[1], rhs[0], start=False, stop=(m == n - 1))
                return last

            pe.wait_ge(ident_ready, 9)
            for n, (kind, i) in enumerate(LOADS):
                if n in TURNED:
                    pe.wait_ge(w_loaded[n % 2], at(load_count(n)))
                    if TURNED.index(n):
                        pe.wait_ge(w_lo, at(FIRST_PART[n]))
                    if kind == "win":
                        rows = min(4 * P, E_ALL - i * 4 * P)
                        src = stage[n % 2].rearrange("p (k n) -> p k n", n=DM)
                        for kt in range(KM):
                            for t in range(0, rows, P):
                                h = min(P, rows - t)
                                last = pe.transpose(wide[kt][:, t:t + h], src[0:h, t // P, kt * P:(kt + 1) * P],
                                                    ident[0:h, 0:h])
                    else:
                        src = stage[n % 2].rearrange("p (k n) -> p k n", n=DI)
                        for kt in range(KI):
                            for t in range(KM):
                                o = (kt // 2) * DM + t * P
                                last = pe.transpose(wide[kt % 2][:, o:o + P], src[:, t, kt * P:(kt + 1) * P],
                                                    ident[:, :])
                    last.then_inc(w_turned, 1)
                elif kind == "f1":
                    pe.wait_ge(dequant, at(IN_FC.index(n) + 1))
                    for t in range(NT):
                        last = pe.matmul(tmb[:, i * NT + t:i * NT + t + 1], stage[n % 2][:, t * P:(t + 1) * P],
                                         lnb[:, i:i + 1], start=True, stop=True)
                    last.then_inc(beta_product, 1)

            def prepare(k, q, c):
                g, par, t = 2 * k + c, q % 2, slice(c * P, (c + 1) * P)
                if c == 1:
                    pe.wait_ge(yT_lo, at(g))
                else:
                    pe.wait_ge(xc_done, at(NCV * (k + 1)))
                    if has_prev(k):
                        pe.wait_ge(yT_lo, at(g))
                    else:
                        pe.wait_ge(uT_lo, 1)
                for n in range(KI):
                    last = pe.transpose(trb[:, n * P:(n + 1) * P], xc[:, n, t], ident[:, :])
                last.then_inc(xT_done, 1)
                wait(pe, yb_done, g)
                pe.transpose(yib[:, 0:NS], xc[:, KI, t], ident[:, :]).then_inc(bT_done, 1)
                wait(pe, s_done, g)
                pe.matmul(dsb[:, 0:P], xc[:, KI, t], xc[:, KI + 1, t], start=True, stop=True).then_inc(bc_done, 1)
                if c == 0:
                    pe.wait_ge(dt_vec, at(4 * k + 4))
                spread(k, q, c, 0)

            def spread(k, q, c, half):
                g, par = 2 * k + c, q % 2
                wait(pe, scan_done, 2 * g + half)
                for h in range(4):
                    col = decz[:, par, c, half * 4 + h:half * 4 + h + 1]
                    last = pe.transpose(bcb[:, h * P:(h + 1) * P], col.to_broadcast([P, P]), ident[:, :])
                last.then_inc(bcast_done, 1)

            def scan_products(k, c):
                g, t = 2 * k + c, slice(c * P, (c + 1) * P)
                wait(pe, s_done, g)
                if c == 1 and has_prev(k):
                    pe.wait_ge(fT_lo, at(k))
                else:
                    wait(pe, ya_done, g)
                pe.matmul(yxb[:, :], xc[:, KI + 1, t], S[:, :], start=True, stop=True).then_inc(yinter_done, 1)
                pe.wait_ge(xdt_done, at(g + 1))
                pe.wait_ge(btm_done, at(g + 1))
                for h in range(NH):
                    if h % 4 == 0:
                        pe.wait_ge(mask_done, at(2 * g + h // 4 + 1))
                    last = pe.matmul(yib[:, h * HD:(h + 1) * HD], dmat[:, h, :], xdt[:, h * HD:(h + 1) * HD],
                                     start=True, stop=True)
                last.then_inc(yintra_done, 1)
                pe.wait_ge(xw_done, at(g + 1))
                pe.matmul(dsb[:, :], btm[:, :], xw[:, :], start=True, stop=True).then_inc(ds_done, 1)

            def turn_y(k, c):
                g = 2 * k + c
                pe.wait_ge(y_steps, at(2 * g + 2))
                for n in range(KI):
                    last = pe.transpose(trb[:, n * P:(n + 1) * P], yb[:, c, n * P:(n + 1) * P], ident[:, :])
                last.then_inc(yT_done, 1)

            def out_proj(k, c):
                g = 2 * k + c
                pe.wait_ge(yT_lo, at(g + 1))
                product(tmb[:, 0:DM], [([w[:, n, :] for w in yT], [w[:, n, :] for w in wout])
                                       for n in range(KI)]).then_inc(outp_done, 1)

            def turn_decays(k):
                if known(k, lambda m: m >= 2):
                    pe.wait_ge(out_ready, at(2 * k - 2))
                else:
                    pe.wait_ge(h2_stats if k == 1 else y_stats, 6)
                pe.transpose(tmb[0:2 * NH, 0:P], dec[:, :, :].rearrange("p c h -> p (c h)"),
                             ident[:, :]).then_inc(decT_done, 1)

            def turn_products(k):
                pe.wait_ge(pT_done, at(k + 1))
                passed(pe)
                pe.transpose(tmb[:, P:P + 2 * NH], pT[:, :], ident[0:2 * NH, 0:2 * NH])
                pe.transpose(tmb[:, P + 2 * NH:P + 4 * NH], pT[:, P - 1:P].to_broadcast([2 * NH, P]),
                             ident[0:2 * NH, 0:2 * NH]).then_inc(ppT_done, 1)

            def tok2(j, c):
                for m in range(NT):
                    pe.wait_ge(tok_lo, at(NT * j + m + 1))
                    last = product_part(tmb[:, 0:DM], hid, w2, m, c)
                last.then_inc(tok2_done, 1)

            def fc2(i, c):
                for m in range(NT):
                    pe.wait_ge(fc_lo, at(NT * i + m + 1))
                    last = product_part(tmb[:, 0:DM], hid, f2, m, c)
                last.then_inc(fc2_done, 1)

            def product_part(dst, lhs, rhs, m, c):
                for o, (a, b) in enumerate(((0, 0), (0, 1), (1, 0))):
                    last = pe.matmul(dst, lhs[a][:, m, c * P:(c + 1) * P], rhs[b][:, m, :],
                                     start=(m == 0 and o == 0), stop=(m == NT - 1 and o == 2))
                return last

            def turn_pair(dst, src):
                for n in range(KM):
                    for c in range(2):
                        last = pe.transpose(dst[:, n * T + c * P:n * T + (c + 1) * P], src[:, c, n * P:(n + 1) * P],
                                            ident[:, :])
                return last

            def channels(k, j, n):
                if n >= 2:
                    pe.wait_ge(tap0_done, at(NCV * j + n - 1))
                elif has_prev(k):
                    pe.wait_ge(silu_done, at(NT * (k - 1) + NT + n - 1))
                else:
                    pe.wait_ge(gelu_done, at(NT * j + NT + n - 1))
                e = DI + n * P
                product(wide[n % 2][:, 0:T], [([w[:, m, e:e + P] for w in win], [v[:, m, :] for v in uT])
                                              for m in range(KM)]).then_inc(xbc_done, 1)

            def step(k, q):
                j, i = k + 1, k - 1
                if has_next(k):
                    pe.wait_ge(xs_lo, at(j + 1))
                for n in range(NT):
                    if has_next(k):
                        if n >= 2:
                            pe.wait_ge(gelu_done, at(NT * j + n - 1))
                        else:
                            wait(pe, sz_done, 2 * j + n - 1)
                        product(wide[n % 2][:, 0:T], [([w[:, m, n * P:(n + 1) * P] for w in w1], [v[:, m, :] for v in xs])
                                                      for m in range(KM)]).then_inc(tok1_done, 1)
                    if has_scan(k):
                        if n == 1:
                            prepare(k, q, 0)
                        if n == 3:
                            turn_decays(k)
                        if n == 4:
                            spread(k, q, 0, 1)
                        if n == 5:
                            turn_products(k)
                if has_scan(k):
                    scan_products(k, 0)
                if has_next(k):
                    if has_scan(k):
                        pe.wait_ge(pp_done, at(k + 1))
                    tok2(j, 0)
                if has_scan(k):
                    pe.wait_ge(xtm_done, at(2 * k + 1))
                    turn_y(k, 0)
                if has_prev(k):
                    pe.wait_ge(ya_done, at(2 * k + 1) if has_scan(k) else 2 * TILES)
                    pe.wait_ge(f_done, at(2 * i + 2))
                    turn_pair(yxb, f).then_inc(fT_done, 1)
                if has_next(k):
                    pe.wait_ge(y_stats, at(10 * j + 1))
                    tok2(j, 1)
                if has_scan(k):
                    prepare(k, q, 1)
                    if has_next(k):
                        pe.wait_ge(y_stats, at(10 * j + 6))
                    else:
                        pe.wait_ge(pp_done, k + 1)
                    out_proj(k, 0)
                if has_prev(k):
                    pe.wait_ge(fT_lo, at(i + 1))
                for n in range(NT):
                    if has_prev(k):
                        if n >= 2:
                            pe.wait_ge(silu_done, at(NT * i + n - 1))
                        elif has_next(k):
                            pe.wait_ge(gelu_done, at(NT * j + NT + n - 1))
                        elif has_scan(k):
                            pe.wait_ge(sz_done, 2 * k + n + 1)
                        else:
                            pe.wait_ge(silu_done, NT * i + n - 1)
                        product(wide[n % 2][:, 0:T], [([w[:, m, n * P:(n + 1) * P] for w in f1], [v[:, m, :] for v in fT])
                                                      for m in range(KM)]).then_inc(fc1_done, 1)
                    if has_scan(k) and n == 2:
                        spread(k, q, 1, 1)
                if has_scan(k):
                    scan_products(k, 1)
                if has_next(k):
                    pe.wait_ge(u_done, at(2 * j + 2))
                    if has_scan(k):
                        pe.wait_ge(xtm_done, at(2 * k + 2))
                    turn_pair(trb, u).then_inc(uT_done, 1)
                if has_prev(k):
                    if has_scan(k):
                        pe.wait_ge(h2_stats, at(10 * k + 1))
                    else:
                        pe.wait_ge(out_ready, 2 * i)
                    fc2(i, 0)
                if has_next(k):
                    pe.wait_ge(uT_lo, at(j + 1))
                    channels(k, j, 0)
                if has_scan(k):
                    if has_next(k):
                        pe.wait_ge(uT_lo, at(j + 1))
                    else:
                        pe.wait_ge(xtm_done, 2 * k + 2)
                    turn_y(k, 1)
                if has_next(k):
                    channels(k, j, 1)
                    channels(k, j, 2)
                if has_scan(k):
                    if has_prev(k):
                        pe.wait_ge(out_ready, at(2 * i + 1))
                    else:
                        pe.wait_ge(h2_stats, 1)
                    out_proj(k, 1)
                if has_next(k):
                    channels(k, j, 3)
                    wait(pe, scan_done, 4 * j)
                    for c in range(2):
                        last = product(bcb[:, c * NH:(c + 1) * NH],
                                       [([v[:, m, c * P:(c + 1) * P] for v in uT], [w[:, m, E_ALL - NH:E_ALL] for w in win])
                                        for m in range(KM)])
                    last.then_inc(dt_done, 1)
                    for n in range(4, NCV):
                        channels(k, j, n)
                    for c in range(2):
                        pe.wait_ge(tap0_done, at(NCV * j + NCV + c - 1))
                        product(wide[c][:, :], [([v[:, m, c * P:(c + 1) * P] for v in uT], [w[:, m, 0:DI] for w in win])
                                                for m in range(KM)]).then_inc(z_done, 1)
                if has_prev(k):
                    if has_scan(k):
                        pe.wait_ge(h2_stats, at(10 * k + 6))
                    else:
                        pe.wait_ge(out_ready, 2 * i + 1)
                    fc2(i, 1)

            pe.wait_ge(w_lo, at(FIRST_PART[-1]))
            pe.wait_ge(fcb_ready, at(2))
            steps(pe, step)

        @block.vector
        def _(dve):
            dve.wait_ge(const_loaded, at(16 * len(CONSTS)))
            dve.tensor_scalar(fb2[:, :], fb2[:, :], 0.5, None, ALU.mult).then_inc(const_ready, 1)
            dve.wait_ge(expa_ready, at(1))
            for n, (kind, i) in enumerate(LOADS):
                if n in IN_FC:
                    o = IN_FC.index(n)
                    dve.wait_ge(w_loaded[n % 2], at(load_count(n)))
                    dve.wait_ge(scale_loaded[o % 2], 16 * (o // 2 + 1))
                    dve.scalar_tensor_tensor(out=stage[n % 2], in0=stage[n % 2].bitcast(I32), scalar=-128.0,
                                             in1=scale_stage[o % 2], op0=ALU.add, op1=ALU.mult).then_inc(dequant, 1)
                for p, (hi, lo) in enumerate(parts(kind, i)):
                    dve.wait_ge(w_hi, at(FIRST_PART[n] + p + 1))
                    dve.scalar_tensor_tensor(out=lo, in0=part_source(n, p), scalar=part_scale(n, p), in1=hi,
                                             op0=ALU.mult, op1=ALU.subtract).then_inc(w_lo, 1)
            dve.wait_ge(beta_product, at(KM))
            dve.tensor_tensor(fcb_part[:, :], fcb_raw[:, :], tmb[:, 0:NT], ALU.add).then_inc(fcb_ready, 1)
            dve.wait_ge(fcb_ready, at(1))
            dve.tensor_tensor(fcb[:, :], fcb_part[:, :], tmb[:, NT:2 * NT], ALU.add).then_inc(fcb_ready, 1)

            def split_x(j, q):
                dve.wait_ge(xs_hi, at(j + 1))
                dve.tensor_tensor(xs[1][:, :, :], xin[q % 2][:, :].rearrange("p (t b) -> p b t", b=2),
                                  xs[0][:, :, :], ALU.subtract).then_inc(xs_lo, 1)

            def hidden_lo(j, n, full, hi_done, lo_done):
                dve.wait_ge(hi_done, at(NT * j + n + 1))
                dve.tensor_tensor(hid[1][:, n, :], full[:, n % RING, :], hid[0][:, n, :],
                                  ALU.subtract).then_inc(lo_done, 1)

            def scan(k, c, half):
                g, hs = 2 * k + c, slice(4 * half, 4 * half + 4)
                dve.wait_ge(bcast_done, at(2 * g + half + 1))
                if half == 0:
                    wait(dve, yintra_done, g)
                    wait(dve, xw_done, g)
                dve.tensor_tensor_scan(dmat[:, hs, :].rearrange("p h t -> p (h t)"), bcb[:, :],
                                       ident4[:, :, :].rearrange("p h t -> p (h t)"), 0.0,
                                       ALU.mult, ALU.add).then_inc(scan_done, 1)

            def mask(k, c, half):
                g, hs = 2 * k + c, slice(4 * half, 4 * half + 4)
                dve.wait_ge(scan_done, at(2 * g + half + 1))
                dve.tensor_copy(dlast[:, hs], dmat[:, hs, P - 1]).then_inc(dlast_done, 1)
                dve.wait_ge(dlast_done, at(2 * g + half + 1))
                dve.wait_ge(bc_done, at(g + 1))
                dve.tensor_tensor(dmat[:, hs, :], dmat[:, hs, :], dsb[:, 0:P].unsqueeze(1).to_broadcast([P, 4, P]),
                                  ALU.mult).then_inc(mask_done, 1)

            def y_lo(k, c):
                dve.wait_ge(yT_hi, at(2 * k + c + 1))
                dve.tensor_tensor(yT[1][:, :, :], trb[:, :].rearrange("p (k t) -> p k t", t=P), yT[0][:, :, :],
                                  ALU.subtract).then_inc(yT_lo, 1)

            def gather_y(k, q, c):
                g, par = 2 * k + c, q % 2
                dve.wait_ge(yinter_done, at(g + 1))
                dve.wait_ge(pp_done, at(k + 1))
                wait(dve, yT_done, g - 1)
                wait(dve, sq_done, g - 1)
                dve.tensor_tensor(heads(yb[:, c, :]), heads(yxb[:, :]), per_head(pp[:, par, 0, c, :]),
                                  ALU.mult).then_inc(ya_done, 1)
                dve.wait_ge(ya_done, at(g + 1))
                dve.wait_ge(yintra_done, at(g + 1))
                dve.tensor_tensor(yb[:, c, :], yb[:, c, :], yib[:, :], ALU.add).then_inc(yb_done, 1)

            def state(k, q, c):
                g = 2 * k + c
                dve.wait_ge(s_decayed, at(g + 1))
                dve.wait_ge(ds_done, at(g + 1))
                if q == PER_B - 1 and c == 1:
                    dve.memset(S[:, :], 0.0).then_inc(s_done, 1)
                else:
                    dve.tensor_tensor(S[:, :], S[:, :], dsb[:, :], ALU.add).then_inc(s_done, 1)

            def moments(src, which, c, s, base):
                dve.bn_stats(st[:, which, :], src).then_inc(s, 1)
                dve.wait_ge(s, at(base + 1))
                passed(dve)
                dve.bn_aggr(mv[:, which, c, :], st[:, which, :]).then_inc(s, 1)
                dve.wait_ge(s, at(base + 2))
                dve.tensor_scalar(veps[:, which, c:c + 1], mv[:, which, c, 1:2], EPS, None, ALU.add).then_inc(s, 1)
                dve.tensor_scalar(negm[:, which, c:c + 1], mv[:, which, c, 0:1], -1.0, None, ALU.mult).then_inc(s, 1)

            def mean_square(k, c):
                g = 2 * k + c
                dve.wait_ge(sq_done, at(g + 1))
                dve.tensor_scalar(msq[:, c:c + 1], ssum[:, c:c + 1], 1.0 / DI, EPS, ALU.mult, ALU.add).then_inc(msq_done, 1)

            def stats_h2(k, q, c):
                g, par = 2 * k + c, q % 2
                dve.wait_ge(yr_done, at(g + 1))
                dve.wait_ge(outp_done, at(g + 1))
                wait(dve, res_steps, 2 * g - 3)
                dve.scalar_tensor_tensor(out=h2[:, c, :], in0=tmb[:, 0:DM], scalar=yr[:, c:c + 1],
                                         in1=h1[:, par, c, :], op0=ALU.mult, op1=ALU.add).then_inc(h2_stats, 1)
                dve.wait_ge(h2_stats, at(5 * g + 1))
                moments(h2[:, c, :], 2, c, h2_stats, 5 * g + 1)

            def stats_x3(k, c):
                g = 2 * k + c
                dve.wait_ge(x3_done, at(g + 1))
                moments(x3[:, c, :], 3, c, x3_stats, 4 * g)

            def stats_y(j, c):
                g = 2 * j + c
                dve.wait_ge(tok2_done, at(g + 1))
                wait(dve, h1_steps, 2 * g - 3)
                dve.tensor_tensor(ytok[:, c, :], tmb[:, 0:DM], b2r[:, :], ALU.add).then_inc(y_stats, 1)
                dve.wait_ge(y_stats, at(5 * g + 1))
                moments(ytok[:, c, :], 0, c, y_stats, 5 * g + 1)

            def stats_h1(j, q, c):
                g, par = 2 * j + c, q % 2
                dve.wait_ge(h1_steps, at(2 * g + 2))
                moments(h1[:, par, c, :], 1, c, h1_stats, 4 * g)

            def step(k, q):
                j, i = k + 1, k - 1
                if has_prev(k):
                    stats_x3(i, 1)
                for n in range(NT):
                    if has_next(k):
                        hidden_lo(j, n, hfull, tok_hi, tok_lo)
                    if has_scan(k):
                        if n == 0:
                            scan(k, 0, 0)
                            mask(k, 0, 0)
                        if n == 3:
                            multiply_up(k)
                        if n == 4:
                            scan(k, 0, 1)
                            mask(k, 0, 1)
                        if n == 6:
                            keep_products(k, q)
                if has_scan(k):
                    gather_y(k, q, 0)
                    state(k, q, 0)
                if has_next(k):
                    stats_y(j, 0)
                if has_scan(k):
                    mean_square(k, 0)
                    y_lo(k, 0)
                if has_prev(k):
                    dve.wait_ge(fT_hi, at(i + 1))
                    dve.tensor_tensor(fT[1][:, :, :], yxb[:, :].rearrange("p (k t) -> p k t", t=T), fT[0][:, :, :],
                                      ALU.subtract).then_inc(fT_lo, 1)
                if has_next(k):
                    stats_y(j, 1)
                    stats_h1(j, q + 1, 0)
                if has_scan(k):
                    scan(k, 1, 0)
                    mask(k, 1, 0)
                    stats_h2(k, q, 0)
                if known(k, lambda m: m + 2 < TILES):
                    split_x(k + 2, q + 2)
                for n in range(NT):
                    if has_prev(k):
                        hidden_lo(i, n, ffull, fc_hi, fc_lo)
                    if has_next(k) and n == 2:
                        stats_h1(j, q + 1, 1)
                    if has_scan(k) and n == 3:
                        scan(k, 1, 1)
                        mask(k, 1, 1)
                    if has_scan(k) and n == 5:
                        stats_x3(k, 0)
                if has_scan(k):
                    gather_y(k, q, 1)
                if has_next(k):
                    dve.wait_ge(uT_hi, at(j + 1))
                    dve.tensor_tensor(uT[1][:, :, :], trb[:, :].rearrange("p (k t) -> p k t", t=T), uT[0][:, :, :],
                                      ALU.subtract).then_inc(uT_lo, 1)
                if has_scan(k):
                    state(k, q, 1)
                if has_prev(k):
                    output(i, q - 1, 0)
                if has_scan(k):
                    mean_square(k, 1)
                    y_lo(k, 1)
                if has_next(k):
                    convolve(j, 0)
                if has_scan(k):
                    stats_h2(k, q, 1)
                if has_next(k):
                    convolve(j, 2)
                    step_bias(j)
                    convolve(j, 4)
                    time_steps(j, q + 1)
                if has_prev(k):
                    output(i, q - 1, 1)

            def output(i, q, c):
                dve.wait_ge(fc2_done, at(2 * i + c + 1))
                dve.wait_ge(res_steps, at(4 * i + 2 * c + 2))
                wait(dve, out_stored[c], 16 * i)
                dve.tensor_tensor(ob[:, c, :], tmb[:, 0:DM], res[:, q % 2, c, :], ALU.add).then_inc(out_ready, 1)

            def convolve(j, n):
                seq = 3 * (NCV * j + n)
                for t in range(1, TAPS):
                    for m in (n, n + 1):
                        if t == 1:
                            dve.wait_ge(tap0_done, at(NCV * j + m + 1))
                            dve.wait_ge(raw_done, at(NCV * j + m + 1))
                        else:
                            dve.wait_ge(taps, at(seq + 2 * (t - 2) + (m - n) + 1))
                        o = HALO - t
                        dve.scalar_tensor_tensor(out=acc[:, m % 3, :], in0=raw[:, m, o:o + T],
                                                 scalar=cw[:, m, HALO - t:HALO - t + 1], in1=acc[:, m % 3, :],
                                                 op0=ALU.mult, op1=ALU.add).then_inc(taps, 1)

            def step_bias(j):
                dve.wait_ge(dt_done, at(j + 1))
                dve.tensor_tensor(dtr[:, :, :], bcb[:, 0:2 * NH].rearrange("p (c h) -> p c h", c=2), dtb[:, :, :],
                                  ALU.add).then_inc(dt_vec, 1)

            def time_steps(j, q):
                par = q % 2
                dve.wait_ge(dt_vec, at(4 * j + 1))
                dve.wait_ge(dt_act, at(4 * j + 3))
                dve.scalar_tensor_tensor(out=dtt[:, par, :, :], in0=dtr[:, :, :], scalar=0.0, in1=dln[:, :, :],
                                         op0=ALU.max, op1=ALU.add).then_inc(dt_vec, 1)
                dve.wait_ge(dt_vec, at(4 * j + 2))
                dve.tensor_tensor(da[:, :, :], dtt[:, par, :, :], expa[:, :, :], ALU.mult).then_inc(dt_vec, 1)
                dve.wait_ge(dt_act, at(4 * j + 4))
                dve.tensor_scalar(decz[:, par, :, :], dec[:, :, :], notfirst[:, 0:1], None,
                                  ALU.mult).then_inc(dt_vec, 1)

            def multiply_up(k):
                dve.wait_ge(decT_done, at(k + 1))
                dve.tensor_tensor_scan(pT[:, :], tmb[0:2 * NH, 0:P], zeros[0:2 * NH, :], 1.0, ALU.mult,
                                       ALU.add).then_inc(pT_done, 1)

            def keep_products(k, q):
                dve.wait_ge(ppT_done, at(k + 1))
                dve.tensor_copy(pp[:, q % 2, :, :, :].rearrange("p a c h -> p (a c h)"),
                                tmb[:, P:P + 4 * NH]).then_inc(pp_done, 1)

            split_x(0, 0)
            steps(dve, step)


_INS = ['x', 'L0_tok_w1', 'L0_tok_b1', 'L0_tok_w2', 'L0_tok_b2', 'L0_tok_gamma', 'L0_tok_beta',
        'L0_attn_in_proj_w', 'L0_attn_conv_w', 'L0_attn_conv_b', 'L0_attn_norm_w', 'L0_attn_out_proj_w',
        'L0_attn_dt_bias', 'L0_attn_A_log', 'L0_attn_D_param', 'L0_ffn_ln_gamma', 'L0_ffn_ln_beta',
        'L0_ffn_fc1_q', 'L0_ffn_fc1_scales', 'L0_ffn_fc1_bias', 'L0_ffn_fc2_q', 'L0_ffn_fc2_scales',
        'L0_ffn_fc2_bias']
_OUTS = [((8, 1024, 256), 'float32')]


def kernel(**inputs):
    import numpy as _np
    import concourse.bacc as _bacc
    from concourse import mybir as _mybir
    from concourse.bass_utils import run_bass_kernel_spmd as _run

    nc = _bacc.Bacc("TRN2", target_bir_lowering=False, num_devices=1)
    arrays, args = {}, []
    for name in _INS:
        a = _np.ascontiguousarray(inputs[name])
        arrays[f"in_{name}_dram"] = a
        args.append(nc.dram_tensor(f"in_{name}_dram", a.shape, _mybir.dt.from_np(a.dtype), kind="ExternalInput").ap())
    for i, (shape, dtype) in enumerate(_OUTS):
        dt = _mybir.dt.from_np(_np.dtype(dtype))
        args.append(nc.dram_tensor(f"out_{i}_dram", shape, dt, kind="ExternalOutput").ap())
    vit_tower(nc, *args)
    r = _run(nc, [arrays], core_ids=[0])
    got = tuple(r.results[0][f"out_{i}_dram"] for i in range(len(_OUTS)))
    return got[0]
```

```python
from contextlib import ExitStack

import concourse.bass as bass
from concourse import mybir

ALU = mybir.AluOpType
ACT = mybir.ActivationFunctionType
F32 = mybir.dt.float32
F32R = mybir.dt.float32r
I32 = mybir.dt.int32

P = 128
EPS = 1e-5


class Count:

    def __init__(self, loop, per, extra):
        self.loop, self.per, self.extra = loop, per, extra

    def __add__(self, n):
        return Count(self.loop, self.per, self.extra + n)

    def __sub__(self, n):
        return Count(self.loop, self.per, self.extra - n)

    def __mul__(self, n):
        return Count(self.loop, self.per * n, self.extra * n)

    __radd__, __rmul__ = __add__, __mul__


class Loop:

    def __init__(self, eng, image, registers):
        self.eng, self.image, self.used = eng, image, 0
        self.product, *self.registers = registers

    def register(self, count):
        r = self.registers[self.used % len(self.registers)]
        self.used += 1
        self.eng.reg_mul(self.product, self.image, count.per)
        self.eng.reg_add(r, self.product, count.extra)
        return r


def at(value):
    return value.loop.register(value) if isinstance(value, Count) else value


def vit_tower(nc, x, tok_w1, tok_b1, tok_w2, tok_b2, tok_gamma, tok_beta, in_proj_w, conv_w, conv_b,
              norm_w, out_proj_w, dt_bias, A_log, D_param, ln_gamma, ln_beta, fc1_q, fc1_scales,
              fc1_bias, fc2_q, fc2_scales, fc2_bias, out):
    B, CIN, HH, WW = x.shape
    HR, WR = HH // 2, WW // 2
    L = HR * WR
    HID = tok_w1.shape[1]
    DM = tok_w2.shape[1]
    NH = dt_bias.shape[0]
    DI = out_proj_w.shape[1]
    HD = DI // NH
    NS = (conv_w.shape[0] - DI) // 2
    TAPS = conv_w.shape[2]
    HALO = TAPS - 1
    E_ALL = in_proj_w.shape[0]
    T = 2 * P
    TILES = B * L // T
    PER_B = L // T
    ROWS = T // WR
    NT = HID // P
    KM = DM // P
    KI = DI // P
    NCV = conv_w.shape[0] // P
    RING = 4
    assert CIN * 4 == 2 * P and KM == 2 and NS == P and PER_B == 4 and fc1_q.shape[1] == HID

    ctx = ExitStack()
    with ctx:
        def sb(name, shape, dt=F32):
            return ctx.enter_context(nc.sbuf_tensor(name, shape, dt))

        def sem(name):
            return ctx.enter_context(nc.semaphore(name))

        w1 = [sb(f"w1_{p}", [P, KM, HID], F32R) for p in ("hi", "lo")]
        w2 = [sb(f"w2_{p}", [P, NT, DM], F32R) for p in ("hi", "lo")]
        win = [sb(f"win_{p}", [P, KM, E_ALL], F32R) for p in ("hi", "lo")]
        wout = [sb(f"wout_{p}", [P, KI, DM], F32R) for p in ("hi", "lo")]
        f1 = [sb(f"f1_{p}", [P, KM, HID], F32R) for p in ("hi", "lo")]
        f2 = [sb(f"f2_{p}", [P, NT, DM], F32R) for p in ("hi", "lo")]
        ident = sb("ident", [P, P])
        ident4 = sb("ident4", [P, 4, P])
        zeros = sb("zeros", [P, P])
        notfirst = sb("notfirst", [P, 1])
        b1c = sb("b1c", [P, NT])
        fcb = sb("fcb", [P, NT])
        fcb_raw = sb("fcb_raw", [P, NT])
        fcb_part = sb("fcb_part", [P, NT])
        cw = sb("cw", [P, NCV, TAPS])
        cb = sb("cb", [P, NCV])
        nw = sb("nw", [P, KI])
        lng = sb("lng", [P, KM])
        lnb = sb("lnb", [P, KM])
        gam = sb("gam", [P, DM])
        bet = sb("bet", [P, DM])
        b2r = sb("b2r", [P, DM])
        fb2 = sb("fb2", [P, DM])
        dpar = sb("dpar", [P, NH])
        dtb = sb("dtb", [NH, 1])
        alog = sb("alog", [P, 2, NH])
        expa = sb("expa", [P, 2, NH])
        xin = [sb(f"xin{i}", [P, ROWS * WW]) for i in range(2)]
        xs = [sb(f"xs_{p}", [P, 2, T], F32R) for p in ("hi", "lo")]
        hfull = sb("hfull", [P, RING, T])
        ffull = sb("ffull", [P, RING, T])
        hid = [sb(f"hid_{p}", [P, NT, T], F32R) for p in ("hi", "lo")]
        ytok = sb("ytok", [P, 2, DM])
        h1 = sb("h1", [P, 2, 2, DM])
        u = sb("u", [P, 2, DM])
        uT = [sb(f"uT_{p}", [P, KM, T], F32R) for p in ("hi", "lo")]
        raw = sb("raw", [P, NCV, HALO + T])
        acc = sb("acc", [P, NCV, T])
        xc = sb("xc", [P, NCV, T])
        sz = sb("sz", [P, 2, DI])
        dtr = sb("dtr", [NH, T])
        dab = sb("dab", [P, 2, NH])
        dex = sb("dex", [P, 2, NH])
        dln = sb("dln", [P, 2, NH])
        dtt = sb("dtt", [P, 2, 2, NH])
        da = sb("da", [P, 2, NH])
        dec = sb("dec", [P, 2, NH])
        decz = sb("decz", [P, 2, 2, NH])
        pT = sb("pT", [2 * NH, P])
        pp = sb("pp", [P, 2, 2, 2, NH])
        xtm = sb("xtm", [P, DI])
        xdt = sb("xdt", [P, DI])
        xw = sb("xw", [P, DI])
        btm = sb("btm", [P, NS])
        dmat = sb("dmat", [P, NH, P])
        dlast = sb("dlast", [P, NH])
        S = sb("S", [P, DI])
        yb = sb("yb", [P, 2, DI])
        sq = sb("sq", [P, DI])
        ssum = sb("ssum", [P, 2])
        yr = sb("yr", [P, 2])
        yT = [sb(f"yT_{p}", [P, KI, P], F32R) for p in ("hi", "lo")]
        h2 = sb("h2", [P, 2, DM])
        x3 = sb("x3", [P, 2, DM])
        res = sb("res", [P, 2, 2, DM])
        f = sb("f", [P, 2, DM])
        fT = [sb(f"fT_{p}", [P, KM, T], F32R) for p in ("hi", "lo")]
        ob = sb("ob", [P, 2, DM])
        st = sb("st", [P, 4, 6])
        mv = sb("mv", [P, 4, 2, 2])
        veps = sb("veps", [P, 4, 2])
        mhalf = sb("mhalf", [P, 1])
        msq = sb("msq", [P, 2])
        rstd = sb("rstd", [P, 4, 2])

        def bank(name):
            return ctx.enter_context(nc.psum_tensor(name, [P, 512], F32))

        wide = [bank("wide0"), bank("wide1")]
        tmb = bank("tmb")
        trb = bank("trb")
        bcb = bank("bcb")
        yib = bank("yib")
        yxb = bank("yxb")
        dsb = bank("dsb")

        waits_passed = sem("waits_passed")
        x_loaded = [sem("x_loaded0"), sem("x_loaded1")]
        tok_const_loaded = sem("tok_const_loaded")
        const_loaded = sem("const_loaded")
        w_loaded = [sem(f"w_loaded{n}") for n in range(8)]
        fc_loaded = [sem(f"fc_loaded{n}") for n in range(3)]
        scale_loaded = [sem(f"scale_loaded{n}") for n in range(3)]
        ident_ready = sem("ident_ready")
        const_ready = sem("const_ready")
        expa_ready = sem("expa_ready")
        dequant = sem("dequant")
        w_turned = sem("w_turned")
        w_hi = sem("w_hi")
        w_lo = sem("w_lo")
        beta_product = sem("beta_product")
        fcb_ready = sem("fcb_ready")
        xs_hi = sem("xs_hi")
        xs_lo = sem("xs_lo")
        tok1_done = sem("tok1_done")
        gelu_done = sem("gelu_done")
        tok_hi = sem("tok_hi")
        tok_lo = sem("tok_lo")
        tok2_done = sem("tok2_done")
        y_stats = sem("y_stats")
        h1_stats = sem("h1_stats")
        h1_done = sem("h1_done")
        u_done = sem("u_done")
        uT_done = sem("uT_done")
        uT_hi = sem("uT_hi")
        uT_lo = sem("uT_lo")
        xbc_done = sem("xbc_done")
        halo_ready = sem("halo_ready")
        raw_done = sem("raw_done")
        tap0_done = sem("tap0_done")
        taps = sem("taps")
        xc_done = sem("xc_done")
        z_done = sem("z_done")
        sz_done = sem("sz_done")
        dt_done = sem("dt_done")
        dtT_done = sem("dtT_done")
        dt_act = sem("dt_act")
        dt_vec = sem("dt_vec")
        decT_done = sem("decT_done")
        pT_done = sem("pT_done")
        ppT_done = sem("ppT_done")
        pp_done = sem("pp_done")
        xT_done = sem("xT_done")
        bT_done = sem("bT_done")
        bc_done = sem("bc_done")
        bcast_done = sem("bcast_done")
        xtm_done = sem("xtm_done")
        btm_done = sem("btm_done")
        scan_done = sem("scan_done")
        dlast_done = sem("dlast_done")
        mask_done = sem("mask_done")
        xdt_done = sem("xdt_done")
        xd_done = sem("xd_done")
        xw_done = sem("xw_done")
        yinter_done = sem("yinter_done")
        yintra_done = sem("yintra_done")
        ds_done = sem("ds_done")
        s_decayed = sem("s_decayed")
        s_done = sem("s_done")
        ya_done = sem("ya_done")
        skip_added = sem("skip_added")
        yb_done = sem("yb_done")
        gated = sem("gated")
        sq_done = sem("sq_done")
        msq_done = sem("msq_done")
        yr_done = sem("yr_done")
        pow_y = sem("pow_y")
        pow_h1 = sem("pow_h1")
        pow_h2 = sem("pow_h2")
        pow_x3 = sem("pow_x3")
        yT_done = sem("yT_done")
        yT_hi = sem("yT_hi")
        yT_lo = sem("yT_lo")
        outp_done = sem("outp_done")
        h2_stats = sem("h2_stats")
        x3_stats = sem("x3_stats")
        x3_done = sem("x3_done")
        f_done = sem("f_done")
        res_steps = sem("res_steps")
        fT_done = sem("fT_done")
        fT_hi = sem("fT_hi")
        fT_lo = sem("fT_lo")
        fc1_done = sem("fc1_done")
        silu_done = sem("silu_done")
        fc_hi = sem("fc_hi")
        fc_lo = sem("fc_lo")
        fc2_done = sem("fc2_done")
        out_ready = sem("out_ready")
        out_stored = [sem("out_stored0"), sem("out_stored1")]

        def wait(eng, s, value):
            if not (isinstance(value, int) and value <= 0):
                eng.wait_ge(s, at(value))

        def passed(eng):
            eng.sem_inc(waits_passed, 1)

        def steps(eng, step):
            step(-1, PER_B - 1)
            for q in range(PER_B):
                step(q, q)
            registers = [eng.alloc_register(f"count{i}") for i in range(5)]
            with eng.Fori(0, B - 2) as b:
                loop = Loop(eng, b, registers)
                for q in range(PER_B):
                    step(Count(loop, PER_B, PER_B + q), q)
            for q in range(PER_B):
                step(TILES - PER_B + q, q)
            step(TILES, 0)

        def known(k, test):
            return test(k) if isinstance(k, int) else True

        def has_next(k):
            return known(k, lambda i: i + 1 < TILES)

        def has_scan(k):
            return known(k, lambda i: 0 <= i < TILES)

        def has_prev(k):
            return known(k, lambda i: i >= 1)

        def has_older(k):
            return known(k, lambda i: i >= 2)

        def heads(ap):
            return ap.rearrange("p (h d) -> p h d", h=NH)

        def per_head(ap):
            return ap.unsqueeze(2).to_broadcast([P, NH, HD])

        W1ROWS = tok_w1.rearrange("(c a b) n -> a c b n", a=2, b=2)
        LOADS = []
        LOADS += [("w1", k) for k in range(KM)] + [("w2", k) for k in range(2)]
        LOADS += [("win", k) for k in range(3)] + [("wout", 0)]
        LOADS += [("f1", k) for k in range(4)] + [("f2", k) for k in range(4)]
        HALF = NT // 2

        def parts(kind, i):
            if kind == "w1":
                return [[w[:, i, :] for w in w1]]
            if kind == "w2":
                return [[w[:, i * HALF:(i + 1) * HALF, :].rearrange("p k n -> p (k n)") for w in w2]]
            if kind == "win":
                e0, e1 = i * 4 * P, min((i + 1) * 4 * P, E_ALL)
                return [[w[:, k, e0:e1] for w in win] for k in range(KM)]
            if kind == "wout":
                return [[w[:, k, :] for w in wout] for k in range(KI)]
            if kind == "f1":
                return [[w[:, i // 2, (i % 2) * 4 * P:(i % 2 + 1) * 4 * P] for w in f1]]
            return [[w[:, 2 * i:2 * i + 2, :].rearrange("p k n -> p (k n)") for w in f2]]

        FIRST_PART, n_parts = [], 0
        for kind, i in LOADS:
            FIRST_PART.append(n_parts)
            n_parts += len(parts(kind, i))
        FIRST_PART.append(n_parts)
        IN_FC = [n for n, (kind, _) in enumerate(LOADS) if kind in ("f1", "f2")]
        TURNED = [n for n, (kind, _) in enumerate(LOADS) if kind in ("win", "wout")]

        flat2, flat3 = "p a b -> p (a b)", "p a b c -> p (a b c)"
        stage = [raw[:, :, :].rearrange(flat2)[:, 0:HID], h1[:, :, :, :].rearrange(flat3),
                 ffull[:, :, :].rearrange(flat2), res[:, :, :, :].rearrange(flat3),
                 dmat[:, :, :].rearrange(flat2), yb[:, :, :].rearrange(flat2),
                 xc[:, 0:3, :].rearrange(flat2), sz[:, :, :].rearrange(flat2)]
        FC_SLOTS = 3
        for n in range(len(IN_FC)):
            stage.append([stage[2][:, 0:2 * DM], stage[2][:, 2 * DM:4 * DM],
                          f[:, :, :].rearrange(flat2)][n % FC_SLOTS])
        scale_stage = [stage[3][:, 0:2 * DM], stage[3][:, 2 * DM:4 * DM], ob[:, :, :].rearrange(flat2)]
        turn_banks = [[yxb, yib], [bcb, dsb]]

        def part_source(n, p):
            kind, i = LOADS[n]
            if n in TURNED:
                banks = turn_banks[TURNED.index(n) % 2]
                if kind == "win":
                    return banks[p][:, 0:min(4 * P, E_ALL - i * 4 * P)]
                return banks[p % 2][:, (p // 2) * DM:(p // 2 + 1) * DM]
            return stage[n]

        def load_count(n):
            if n in IN_FC:
                o = IN_FC.index(n)
                return fc_loaded[o % FC_SLOTS], 16 * (o // FC_SLOTS + 1)
            return w_loaded[n], 32 if LOADS[n][0] == "w1" or LOADS[n] == ("win", 2) else 16

        def part_scale(n, p):
            kind, i = LOADS[n]
            if kind == "wout":
                return nw[:, p:p + 1]
            if kind == "f1":
                return lng[:, i // 2:i // 2 + 1]
            return 0.5 if kind == "f2" else 1.0

        turned_dt = bcb[:, T:T + 2 * NH].rearrange("p (c h) -> p c h", c=2)

        block = ctx.enter_context(nc.Block())

        TOK_CONSTS = [
            (b1c[:, :], tok_b1.rearrange("(n p) -> p n", p=P)),
            (b2r[:, :], tok_b2.partition_broadcast(P)),
            (gam[:, :], tok_gamma.partition_broadcast(P)),
            (bet[:, :], tok_beta.partition_broadcast(P)),
        ]
        CONSTS = [
            (cw[:, :, :], conv_w.rearrange("(n p) o k -> p n (o k)", p=P)),
            (cb[:, :], conv_b.rearrange("(n p) -> p n", p=P)),
            (dtb[:, :], dt_bias.rearrange("(h o) -> h o", o=1)),
            (alog[:, 0, :], A_log.partition_broadcast(P)),
            (alog[:, 1, :], A_log.partition_broadcast(P)),
            (nw[:, :], norm_w.rearrange("(n p) -> p n", p=P)),
            (dpar[:, :], D_param.partition_broadcast(P)),
            (lng[:, :], ln_gamma.rearrange("(n p) -> p n", p=P)),
            (lnb[:, :], ln_beta.rearrange("(n p) -> p n", p=P)),
            (fcb_raw[:, :], fc1_bias.rearrange("(n p) -> p n", p=P)),
            (fb2[:, :], fc2_bias.partition_broadcast(P)),
        ]
        x_rows = x.rearrange("i c (t r a) w -> a i t c r w", a=2, r=ROWS)
        out_rows = out.rearrange("i (t p) n -> (i t) p n", p=P)

        @block.sync
        def _(sp):
            def load_x(j, q):
                if not (isinstance(j, int) and j >= TILES):
                    wait(sp, xs_hi, j - 1)
                    wait(sp, xs_lo, j - 1)
                    if isinstance(j, int):
                        img = j // PER_B
                    else:
                        img = (j - q % PER_B) // PER_B
                    for a in range(2):
                        sp.dma_start(xin[q % 2][a * CIN:(a + 1) * CIN, :].rearrange("c (r w) -> c r w", w=WW),
                                     x_rows[a, img, q % PER_B]).then_inc(x_loaded[q % 2], 16)

            def step(k, q):
                if isinstance(k, int):
                    if k == 0:
                        for o in range(2 * FC_SLOTS, len(IN_FC)):
                            load_fc(o)
                    load_x(k + 4, q)
                    if k == -1:
                        for o in range(FC_SLOTS, 2 * FC_SLOTS):
                            load_fc(o)
                else:
                    wait(sp, xs_hi, k + 3)
                    wait(sp, xs_lo, k + 3)
                    for a in range(2):
                        sp.dma_start(xin[q % 2][a * CIN:(a + 1) * CIN, :].rearrange("c (r w) -> c r w", w=WW),
                                     x_rows[a, bass.ds(k.loop.image + 2, 1), q][0]).then_inc(x_loaded[q % 2], 16)
                if has_prev(k):
                    for c in range(2):
                        g = 2 * (k - 1) + c
                        sp.wait_ge(out_ready, at(g + 1))
                        dst = out_rows[g] if isinstance(k, int) else out_rows[bass.ds(g.loop.image * g.per + g.extra, 1)][0]
                        sp.dma_start(dst, ob[:, c, :]).then_inc(out_stored[c], 16)

            def load_fc(o):
                n, slot = IN_FC[o], o % FC_SLOTS
                kind, i = LOADS[n]
                if o >= FC_SLOTS:
                    sp.wait_ge(w_lo, FIRST_PART[n - FC_SLOTS + 1])
                    if o - FC_SLOTS < 4:
                        sp.wait_ge(beta_product, o - FC_SLOTS + 1)
                dst, s, sdst = stage[n].bitcast(I32), fc_loaded[slot], scale_stage[slot]
                if kind == "f1":
                    rows, cols = slice((i // 2) * P, (i // 2 + 1) * P), slice((i % 2) * 4 * P, (i % 2 + 1) * 4 * P)
                    sp.dma_start(dst, fc1_q[rows, cols]).then_inc(s, 16)
                    sp.dma_start(sdst, fc1_scales[i // 2][cols].partition_broadcast(P)).then_inc(scale_loaded[slot], 16)
                else:
                    sp.dma_start(dst.rearrange("p (k n) -> p k n", n=DM),
                                 fc2_q[2 * i * P:2 * (i + 1) * P, :].rearrange("(k p) n -> p k n", p=P)).then_inc(s, 16)
                    sp.dma_start(sdst.rearrange("p (k n) -> p k n", n=DM),
                                 fc2_scales[2 * i:2 * (i + 1), :].partition_broadcast(P)).then_inc(scale_loaded[slot], 16)

            load_x(0, 0)
            for n, (kind, i) in enumerate(LOADS[:IN_FC[0]]):
                dst, s = stage[n], w_loaded[n]
                if kind == "w1":
                    for a in range(2):
                        sp.dma_start(dst[a * CIN:(a + 1) * CIN, :], W1ROWS[a, :, i, :]).then_inc(s, 16)
                elif kind == "w2":
                    sp.dma_start(dst.rearrange("p (k n) -> p k n", n=DM),
                                 tok_w2[i * HALF * P:(i + 1) * HALF * P, :].rearrange("(k p) n -> p k n", p=P)).then_inc(s, 16)
                elif kind == "win":
                    rows = min(4 * P, E_ALL - i * 4 * P)
                    full = rows // P
                    sp.dma_start(dst[:, 0:full * DM].rearrange("p (k n) -> p k n", n=DM),
                                 in_proj_w[i * 4 * P:(i * 4 + full) * P, :].rearrange("(k p) n -> p k n", p=P)).then_inc(s, 16)
                    if rows % P:
                        sp.dma_start(dst[0:NH, full * DM:(full + 1) * DM], in_proj_w[E_ALL - NH:E_ALL, :]).then_inc(s, 16)
                else:
                    sp.dma_start(dst.rearrange("p (k n) -> p k n", n=DI),
                                 out_proj_w.rearrange("(k p) n -> p k n", p=P)).then_inc(s, 16)
                if n == 3:
                    for dst, src in TOK_CONSTS:
                        sp.dma_start(dst, src, allow_slow_non_contiguous=True).then_inc(tok_const_loaded, 16)
                if n == 6:
                    for dst, src in CONSTS:
                        sp.dma_start(dst, src, allow_slow_non_contiguous=True).then_inc(const_loaded, 16)
                if n == 7:
                    load_x(1, 1)
            load_x(2, 2)
            sp.wait_ge(w_lo, FIRST_PART[4])
            for o in range(FC_SLOTS):
                load_fc(o)
            steps(sp, step)
            for c in range(2):
                sp.wait_ge(out_stored[c], at(16 * TILES))

        @block.gpsimd
        def _(pool):
            pool.memset(ident[:, :], 0.0).then_inc(ident_ready, 1)
            pool.memset(ident4[:, :, :], 0.0).then_inc(ident_ready, 1)
            pool.memset(notfirst[:, :], 1.0).then_inc(ident_ready, 1)
            pool.memset(zeros[:, :], 0.0).then_inc(ident_ready, 1)
            pool.memset(S[:, :], 0.0).then_inc(ident_ready, 1)
            pool.memset(mhalf[:, :], -0.5).then_inc(ident_ready, 1)
            pool.wait_ge(ident_ready, 6)
            pool.affine_select(out=ident[:, :], in_=ident[:, :], compare_op=ALU.not_equal, fill=1.0, base=0,
                               pattern=[[-1, P]], channel_multiplier=1).then_inc(ident_ready, 1)
            pool.affine_select(out=ident4[:, :, :], in_=ident4[:, :, :], compare_op=ALU.not_equal, fill=1.0,
                               base=0, pattern=[[0, 4], [-1, P]], channel_multiplier=1).then_inc(ident_ready, 1)
            pool.affine_select(out=notfirst[:, :], in_=notfirst[:, :], compare_op=ALU.not_equal, fill=0.0,
                               base=0, pattern=[[0, 1]], channel_multiplier=1).then_inc(ident_ready, 1)

            def scale_x(k, q, c):
                g, par = 2 * k + c, q % 2
                pool.wait_ge(xtm_done, at(g + 1))
                wait(pool, yintra_done, g)
                pool.tensor_tensor(heads(xdt[:, :]), heads(xtm[:, :]), per_head(dtt[:, par, c, :]),
                                   ALU.mult).then_inc(xdt_done, 1)

            def skip_x(k, c):
                g = 2 * k + c
                pool.wait_ge(xdt_done, at(g + 1))
                pool.tensor_tensor(heads(xtm[:, :]), heads(xtm[:, :]), per_head(dpar[:, :]),
                                   ALU.mult).then_inc(xd_done, 1)

            def decay_x(k, c):
                g = 2 * k + c
                pool.wait_ge(xdt_done, at(g + 1))
                pool.wait_ge(dlast_done, at(2 * g + 2))
                wait(pool, ds_done, g)
                pool.tensor_tensor(heads(xw[:, :]), heads(xdt[:, :]), per_head(dlast[:, :]),
                                   ALU.mult).then_inc(xw_done, 1)

            def decay_state(k, q, c):
                g, par = 2 * k + c, q % 2
                pool.wait_ge(yinter_done, at(g + 1))
                pool.wait_ge(pp_done, at(k + 1))
                wait(pool, s_done, g)
                pool.tensor_tensor(heads(S[:, :]), heads(S[:, :]), per_head(pp[:, par, 1, c, :]),
                                   ALU.mult).then_inc(s_decayed, 1)

            def split_x(j, q):
                pool.wait_ge(xs_hi, at(j + 1))
                pool.tensor_tensor(xs[1][:, :, :], xin[q % 2][:, :].rearrange("p (t b) -> p b t", b=2),
                                   xs[0][:, :, :], ALU.subtract).then_inc(xs_lo, 1)

            def add_skip(k, c):
                g = 2 * k + c
                pool.wait_ge(ya_done, at(g + 1))
                pool.wait_ge(xd_done, at(g + 1))
                pool.tensor_tensor(yb[:, c, :], yb[:, c, :], xtm[:, :], ALU.add).then_inc(skip_added, 1)

            def inverse_rms(k, c):
                g = 2 * k + c
                pool.wait_ge(msq_done, at(g + 1))
                pool.tensor_tensor(yr[:, c:c + 1], msq[:, c:c + 1], mhalf[:, :], ALU.pow).then_inc(yr_done, 1)

            def inverse_std(which, c, stats, stats_count, powers):
                pool.wait_ge(stats, at(stats_count))
                pool.tensor_tensor(rstd[:, which, c:c + 1], veps[:, which, c:c + 1], mhalf[:, :],
                                   ALU.pow).then_inc(powers, 1)

            def std_y(j, c):
                inverse_std(0, c, y_stats, 5 * (2 * j + c) + 4, pow_y)

            def std_h1(j, c):
                inverse_std(1, c, h1_stats, 3 * (2 * j + c) + 3, pow_h1)

            def std_h2(k, c):
                inverse_std(2, c, h2_stats, 4 * (2 * k + c) + 4, pow_h2)

            def std_x3(k, c):
                inverse_std(3, c, x3_stats, 3 * (2 * k + c) + 3, pow_x3)

            def residual(k, q, c):
                g, par = 2 * k + c, q % 2
                pool.wait_ge(x3_done, at(g + 1))
                wait(pool, out_ready, g - 3)
                pool.tensor_tensor(res[:, par, c, :], h2[:, c, :], x3[:, c, :], ALU.add).then_inc(res_steps, 1)
                pool.wait_ge(res_steps, at(2 * g + 1))
                pool.tensor_tensor(res[:, par, c, :], res[:, par, c, :], fb2[:, :], ALU.add).then_inc(res_steps, 1)

            def halo(j, q):
                wait(pool, taps, 3 * NCV * j)
                passed(pool)
                if q % PER_B == 0:
                    pool.memset(raw[:, :, 0:HALO], 0.0).then_inc(halo_ready, 1)
                else:
                    pool.tensor_copy(raw[:, :, 0:HALO], raw[:, :, T:T + HALO]).then_inc(halo_ready, 1)

            def step(k, q):
                j = k + 1
                if k == 0:
                    pool.wait_ge(const_loaded, 16 * len(CONSTS))
                if has_scan(k):
                    scale_x(k, q, 0)
                    skip_x(k, 0)
                    decay_x(k, 0)
                    add_skip(k, 0)
                    decay_state(k, q, 0)
                if has_next(k):
                    halo(j, q + 1)
                    std_y(j, 0)
                if has_scan(k):
                    inverse_rms(k, 0)
                if has_next(k):
                    std_h1(j, 0)
                    std_y(j, 1)
                if has_scan(k):
                    scale_x(k, q, 1)
                    std_h2(k, 0)
                if has_next(k):
                    std_h1(j, 1)
                if known(k, lambda m: m + 2 < TILES):
                    split_x(k + 2, q + 2)
                if has_scan(k):
                    decay_x(k, 1)
                    skip_x(k, 1)
                    std_x3(k, 0)
                    add_skip(k, 1)
                    decay_state(k, q, 1)
                    inverse_rms(k, 1)
                    if k == 0:
                        pool.wait_ge(dequant, len(IN_FC))
                        pool.wait_ge(const_ready, 1)
                    residual(k, q, 0)
                    std_h2(k, 1)
                    std_x3(k, 1)
                    residual(k, q, 1)

            split_x(0, 0)
            pool.wait_ge(w_lo, FIRST_PART[1])
            steps(pool, step)

        @block.scalar
        def _(act):
            def split_load(n):
                kind, i = LOADS[n]
                for p, (hi, lo) in enumerate(parts(kind, i)):
                    if n in TURNED:
                        act.wait_ge(w_turned, TURNED.index(n) + 1)
                    elif n in IN_FC:
                        act.wait_ge(dequant, IN_FC.index(n) + 1)
                    else:
                        act.wait_ge(*load_count(n))
                    if kind == "wout" and p >= 2:
                        act.wait_ge(w_lo, FIRST_PART[n] + p - 1)
                    act.activation(hi, part_source(n, p), ACT.Copy, scale=part_scale(n, p)).then_inc(w_hi, 1)

            def split_x(j, q):
                act.wait_ge(x_loaded[q % 2], at(32 * count_pairs(j, q)))
                wait(act, tok1_done, NT * j)
                act.activation(xs[0][:, :, :], xin[q % 2][:, :].rearrange("p (t b) -> p b t", b=2),
                               ACT.Copy).then_inc(xs_hi, 1)

            def x_and_b(k, c):
                g = 2 * k + c
                act.wait_ge(xT_done, at(g + 1))
                wait(act, skip_added, g)
                act.activation(xtm[:, :], trb[:, :], ACT.Copy).then_inc(xtm_done, 1)
                act.wait_ge(bT_done, at(g + 1))
                wait(act, ds_done, g)
                act.activation(btm[:, :], yib[:, 0:NS], ACT.Copy).then_inc(btm_done, 1)

            def y_turned(k, c):
                g = 2 * k + c
                act.wait_ge(yT_done, at(g + 1))
                wait(act, outp_done, g)
                act.activation(yT[0][:, :, :], trb[:, :].rearrange("p (k t) -> p k t", t=P),
                               ACT.Copy).then_inc(yT_hi, 1)

            def square(k, c):
                g = 2 * k + c
                act.wait_ge(gated, at(g + 1))
                wait(act, sq_done, g)
                wait(act, msq_done, g - 1)
                act.activation(sq[:, :], yb[:, c, :], ACT.Square, accum_out=ssum[:, c:c + 1]).then_inc(sq_done, 1)

            def hidden(i, func, bias, done, full, full_done, hi_done, lo_done, hid_free, between):
                for n in range(NT + 1):
                    if n < NT:
                        act.wait_ge(done, at(NT * i + n + 1))
                        wait(act, lo_done, NT * i + n + 1 - RING)
                        act.activation(full[:, n % RING, :], wide[n % 2][:, 0:T], func,
                                       bias=bias[:, n:n + 1]).then_inc(full_done, 1)
                    if n >= 1:
                        if n == 1:
                            wait(act, *hid_free)
                        act.wait_ge(full_done, at(NT * i + n))
                        act.activation(hid[0][:, n - 1, :], full[:, (n - 1) % RING, :], ACT.Copy).then_inc(hi_done, 1)
                    between(n)

            def step(k, q):
                j, i = k + 1, k - 1

                def in_tok1(n):
                    if k == -1 and n in (3, 6):
                        split_load(1 + n // 3)
                    if k == 0 and n in (2, 5, 6):
                        split_load(IN_FC[{2: 3, 5: 4, 6: 5}[n]])
                    if has_scan(k) and n == 1:
                        x_and_b(k, 0)
                    if n == NT - 1:
                        act.preload_act_table_set("silu_and_others")

                if k == -1:
                    act.wait_ge(tok_const_loaded, 16 * len(TOK_CONSTS))
                if has_next(k):
                    hidden(j, ACT.Gelu, b1c, tok1_done, hfull, gelu_done, tok_hi, tok_lo,
                           (fc2_done, 2 * (j - 2)), in_tok1)
                else:
                    for n in range(NT):
                        in_tok1(n)
                if has_scan(k):
                    square(k, 0)
                    y_turned(k, 0)
                if has_prev(k):
                    act.wait_ge(fT_done, at(i + 1))
                    wait(act, fc1_done, NT * i)
                    act.activation(fT[0][:, :, :], yxb[:, :].rearrange("p (k t) -> p k t", t=T),
                                   ACT.Copy).then_inc(fT_hi, 1)
                if has_scan(k):
                    x_and_b(k, 1)
                if k == -1:
                    for n in TURNED:
                        if n == TURNED[-1]:
                            act.wait_ge(const_loaded, 16 * len(CONSTS))
                        split_load(n)
                if known(k, lambda i: i + 2 < TILES):
                    split_x(k + 2, q + 2)
                if k == 0:
                    for n in IN_FC[6:]:
                        split_load(n)
                if has_prev(k):
                    hidden(i, ACT.Silu, fcb, fc1_done, ffull, silu_done, fc_hi, fc_lo,
                           (tok2_done, 2 * j + 2) if has_next(k) else (fc2_done, 2 * i), lambda n: None)
                if has_next(k):
                    act.wait_ge(uT_done, at(j + 1))
                    wait(act, dt_done, j)
                    act.activation(uT[0][:, :, :], trb[:, :].rearrange("p (k t) -> p k t", t=T),
                                   ACT.Copy).then_inc(uT_hi, 1)
                if has_scan(k) and not has_next(k):
                    square(k, 1)
                    y_turned(k, 1)
                if has_next(k):
                    act.wait_ge(halo_ready, at(j + 1))
                    for n in range(NCV):
                        m = NCV * j + n
                        act.wait_ge(xbc_done, at(m + 1))
                        act.activation(raw[:, n, HALO:HALO + T], wide[n % 2][:, 0:T], ACT.Copy).then_inc(raw_done, 1)
                        act.activation(acc[:, n, :], wide[n % 2][:, 0:T], ACT.Identity,
                                       scale=cw[:, n, HALO:TAPS], bias=cb[:, n:n + 1]).then_inc(tap0_done, 1)
                        if n == 0 and has_scan(k):
                            square(k, 1)
                        if n == 1 and has_scan(k):
                            y_turned(k, 1)
                        if k == -1 and n in (1, 3):
                            split_load(IN_FC[n // 2])
                        if n >= 3:
                            conv_silu(k, j, n - 3)
                    for c in range(2):
                        act.wait_ge(z_done, at(2 * j + c + 1))
                        wait(act, gated, 2 * j - 1 + c)
                        act.activation(sz[:, c, :], wide[c][:, :], ACT.Silu).then_inc(sz_done, 1)
                        if c == 0:
                            conv_silu(k, j, 3)
                            act.wait_ge(dtT_done, at(j + 1))
                            act.activation(dab[:, :, :], turned_dt, ACT.Abs).then_inc(dt_act, 1)
                    if k == -1:
                        split_load(IN_FC[2])
                    for n in range(NCV - 2, NCV):
                        conv_silu(k, j, n)
                    act.preload_act_table_set("natural_log_exp_and_others")
                    if k == -1:
                        act.activation(expa[:, :, :], alog[:, :, :], ACT.Exp).then_inc(expa_ready, 1)
                    act.wait_ge(dt_act, at(4 * j + 1))
                    act.activation(dex[:, :, :], dab[:, :, :], ACT.Exp, scale=-1.0).then_inc(dt_act, 1)
                    act.wait_ge(dt_act, at(4 * j + 2))
                    act.activation(dln[:, :, :], dex[:, :, :], ACT.Ln, bias=1.0).then_inc(dt_act, 1)
                    act.wait_ge(dt_vec, at(4 * j + 3))
                    wait(act, decT_done, j)
                    act.activation(dec[:, :, :], da[:, :, :], ACT.Exp, scale=-1.0).then_inc(dt_act, 1)
                    act.preload_act_table_set("gelu_and_others")

            def conv_silu(k, j, n):
                act.wait_ge(taps, at(3 * (NCV * j + n - n % 2) + 2 * HALO - 1 + n % 2))
                if n == 0:
                    wait(act, xT_done, 2 * j)
                    wait(act, bT_done, 2 * j)
                    wait(act, yinter_done, 2 * j)
                act.activation(xc[:, n, :], acc[:, n, :], ACT.Silu).then_inc(xc_done, 1)

            def count_pairs(j, q):
                return j // 2 + 1 if isinstance(j, int) else Count(j.loop, j.per // 2, j.extra // 2 + 1)

            split_load(0)
            split_load(1)
            split_x(0, 0)
            steps(act, step)

        @block.tensor
        def _(pe):
            def product(dst, pairs):
                n = len(pairs)
                for m, (lhs, rhs) in enumerate(pairs):
                    pe.matmul(dst, lhs[0], rhs[0], start=(m == 0), stop=False)
                    pe.matmul(dst, lhs[0], rhs[1], start=False, stop=False)
                    last = pe.matmul(dst, lhs[1], rhs[0], start=False, stop=(m == n - 1))
                return last

            def turn_load(n):
                kind, i = LOADS[n]
                banks = turn_banks[TURNED.index(n) % 2]
                pe.wait_ge(*load_count(n))
                if TURNED.index(n) >= 2:
                    pe.wait_ge(w_lo, FIRST_PART[n - 1])
                if kind == "win":
                    rows = min(4 * P, E_ALL - i * 4 * P)
                    src = stage[n].rearrange("p (k n) -> p k n", n=DM)
                    for kt in range(KM):
                        for t in range(0, rows, P):
                            h = min(P, rows - t)
                            last = pe.transpose(banks[kt][:, t:t + h], src[0:h, t // P, kt * P:(kt + 1) * P],
                                                ident[0:h, 0:h])
                else:
                    src = stage[n].rearrange("p (k n) -> p k n", n=DI)
                    for kt in range(KI):
                        for t in range(KM):
                            o = (kt // 2) * DM + t * P
                            last = pe.transpose(banks[kt % 2][:, o:o + P], src[:, t, kt * P:(kt + 1) * P],
                                                ident[:, :])
                last.then_inc(w_turned, 1)

            def beta_share(i):
                pe.wait_ge(const_loaded, 16 * len(CONSTS))
                pe.wait_ge(dequant, i + 1)
                for t in range(4):
                    o = (i // 2) * NT + (i % 2) * 4 + t
                    last = pe.matmul(yxb[:, o:o + 1], stage[IN_FC[i]][:, t * P:(t + 1) * P],
                                     lnb[:, i // 2:i // 2 + 1], start=True, stop=True)
                last.then_inc(beta_product, 1)

            def prepare(k, q, c):
                g, par, t = 2 * k + c, q % 2, slice(c * P, (c + 1) * P)
                if c == 1:
                    pe.wait_ge(yT_lo, at(g))
                else:
                    pe.wait_ge(xc_done, at(NCV * (k + 1)))
                    if has_prev(k):
                        pe.wait_ge(yT_lo, at(g))
                    else:
                        pe.wait_ge(uT_lo, 1)
                for n in range(KI):
                    last = pe.transpose(trb[:, n * P:(n + 1) * P], xc[:, n, t], ident[:, :])
                last.then_inc(xT_done, 1)
                wait(pe, yb_done, g)
                pe.transpose(yib[:, 0:NS], xc[:, KI, t], ident[:, :]).then_inc(bT_done, 1)
                wait(pe, s_done, g)
                pe.matmul(dsb[:, 0:P], xc[:, KI, t], xc[:, KI + 1, t], start=True, stop=True).then_inc(bc_done, 1)
                if c == 0:
                    pe.wait_ge(dt_vec, at(4 * k + 4))
                spread(k, q, c, 0)

            def spread(k, q, c, half):
                g, par = 2 * k + c, q % 2
                wait(pe, scan_done, 2 * g + half)
                for h in range(4):
                    col = decz[:, par, c, half * 4 + h:half * 4 + h + 1]
                    last = pe.transpose(bcb[:, h * P:(h + 1) * P], col.to_broadcast([P, P]), ident[:, :])
                last.then_inc(bcast_done, 1)

            def scan_products(k, c):
                g, t = 2 * k + c, slice(c * P, (c + 1) * P)
                wait(pe, s_done, g)
                if c == 1 and has_prev(k):
                    pe.wait_ge(fT_lo, at(k))
                else:
                    wait(pe, ya_done, g)
                pe.matmul(yxb[:, :], xc[:, KI + 1, t], S[:, :], start=True, stop=True).then_inc(yinter_done, 1)
                pe.wait_ge(xdt_done, at(g + 1))
                pe.wait_ge(btm_done, at(g + 1))
                for h in range(NH):
                    if h % 4 == 0:
                        pe.wait_ge(mask_done, at(2 * g + h // 4 + 1))
                    last = pe.matmul(yib[:, h * HD:(h + 1) * HD], dmat[:, h, :], xdt[:, h * HD:(h + 1) * HD],
                                     start=True, stop=True)
                last.then_inc(yintra_done, 1)

            def state_product(k, c):
                g = 2 * k + c
                pe.wait_ge(mask_done, at(2 * g + 2))
                pe.wait_ge(xw_done, at(g + 1))
                pe.matmul(dsb[:, :], btm[:, :], xw[:, :], start=True, stop=True).then_inc(ds_done, 1)

            def turn_y(k, c):
                g = 2 * k + c
                pe.wait_ge(gated, at(g + 1))
                for n in range(KI):
                    last = pe.transpose(trb[:, n * P:(n + 1) * P], yb[:, c, n * P:(n + 1) * P], ident[:, :])
                last.then_inc(yT_done, 1)

            def out_proj(k, c):
                g = 2 * k + c
                pe.wait_ge(yT_lo, at(g + 1))
                product(tmb[:, 0:DM], [([w[:, n, :] for w in yT], [w[:, n, :] for w in wout])
                                       for n in range(KI)]).then_inc(outp_done, 1)

            def turn_decays(k):
                if known(k, lambda m: m >= 2):
                    pe.wait_ge(out_ready, at(2 * k - 2))
                else:
                    pe.wait_ge(*((h2_stats, 5) if k == 1 else (y_stats, 6)))
                pe.transpose(tmb[0:2 * NH, 0:P], dec[:, :, :].rearrange("p c h -> p (c h)"),
                             ident[:, :]).then_inc(decT_done, 1)

            def turn_products(k):
                pe.wait_ge(pT_done, at(k + 1))
                passed(pe)
                pe.transpose(tmb[:, P:P + 2 * NH], pT[:, :], ident[0:2 * NH, 0:2 * NH])
                pe.transpose(tmb[:, P + 2 * NH:P + 4 * NH], pT[:, P - 1:P].to_broadcast([2 * NH, P]),
                             ident[0:2 * NH, 0:2 * NH]).then_inc(ppT_done, 1)

            def tok2(j, c):
                for m in range(NT):
                    pe.wait_ge(tok_lo, at(NT * j + m + 1))
                    last = product_part(tmb[:, 0:DM], hid, w2, m, c)
                last.then_inc(tok2_done, 1)

            def fc2(i, c, tiles=range(NT)):
                for m in tiles:
                    pe.wait_ge(fc_lo, at(NT * i + m + 1))
                    last = product_part(tmb[:, 0:DM], hid, f2, m, c)
                if m == NT - 1:
                    last.then_inc(fc2_done, 1)

            def product_part(dst, lhs, rhs, m, c):
                for o, (a, b) in enumerate(((0, 0), (0, 1), (1, 0))):
                    last = pe.matmul(dst, lhs[a][:, m, c * P:(c + 1) * P], rhs[b][:, m, :],
                                     start=(m == 0 and o == 0), stop=(m == NT - 1 and o == 2))
                return last

            def turn_pair(dst, src):
                for n in range(KM):
                    for c in range(2):
                        last = pe.transpose(dst[:, n * T + c * P:n * T + (c + 1) * P], src[:, c, n * P:(n + 1) * P],
                                            ident[:, :])
                return last

            def channels(k, j, n):
                if n >= 2:
                    pe.wait_ge(tap0_done, at(NCV * j + n - 1))
                elif has_prev(k):
                    pe.wait_ge(silu_done, at(NT * (k - 1) + NT + n - 1))
                else:
                    pe.wait_ge(gelu_done, at(NT * j + NT + n - 1))
                e = DI + n * P
                product(wide[n % 2][:, 0:T], [([w[:, m, e:e + P] for w in win], [v[:, m, :] for v in uT])
                                              for m in range(KM)]).then_inc(xbc_done, 1)

            def step(k, q):
                j, i = k + 1, k - 1
                if has_next(k):
                    pe.wait_ge(xs_lo, at(j + 1))
                for n in range(NT):
                    if has_next(k):
                        if n >= 2:
                            pe.wait_ge(gelu_done, at(NT * j + n - 1))
                        else:
                            wait(pe, sz_done, 2 * j + n - 1)
                        product(wide[n % 2][:, 0:T], [([w[:, m, n * P:(n + 1) * P] for w in w1], [v[:, m, :] for v in xs])
                                                      for m in range(KM)]).then_inc(tok1_done, 1)
                    if n == 1 and has_older(k):
                        pe.wait_ge(h2_stats, at(8 * k - 3))
                        fc2(k - 2, 1)
                    if has_scan(k):
                        if n == 1:
                            prepare(k, q, 0)
                        if k == 0 and n == 3:
                            beta_share(3)
                        if n == 2:
                            turn_decays(k)
                        if n == 3:
                            spread(k, q, 0, 1)
                        if n == 6:
                            turn_products(k)
                if k == 0:
                    pe.wait_ge(fcb_ready, 2)
                if has_scan(k):
                    scan_products(k, 0)
                    state_product(k, 0)
                if k == -1:
                    turn_load(TURNED[0])
                    pe.wait_ge(w_lo, FIRST_PART[4])
                if has_next(k):
                    if has_scan(k):
                        pe.wait_ge(pp_done, at(k + 1))
                    tok2(j, 0)
                if k == -1:
                    turn_load(TURNED[1])
                if has_scan(k):
                    pe.wait_ge(xtm_done, at(2 * k + 1))
                    turn_y(k, 0)
                if has_prev(k):
                    pe.wait_ge(ya_done, at(2 * k + 1) if has_scan(k) else 2 * TILES)
                    pe.wait_ge(f_done, at(2 * i + 2))
                    turn_pair(yxb, f).then_inc(fT_done, 1)
                if has_next(k):
                    pe.wait_ge(y_stats, at(10 * j + 1))
                    tok2(j, 1)
                if k == -1:
                    turn_load(TURNED[2])
                    turn_load(TURNED[3])
                if has_scan(k):
                    prepare(k, q, 1)
                    if has_next(k):
                        pe.wait_ge(y_stats, at(10 * j + 6))
                    else:
                        pe.wait_ge(pp_done, k + 1)
                    out_proj(k, 0)
                if k == 1:
                    pe.wait_ge(w_lo, FIRST_PART[-1])
                if has_prev(k):
                    pe.wait_ge(fT_lo, at(i + 1))
                for n in range(NT):
                    if has_prev(k):
                        if n >= 2:
                            pe.wait_ge(silu_done, at(NT * i + n - 1))
                        elif has_next(k):
                            pe.wait_ge(gelu_done, at(NT * j + NT + n - 1))
                        elif has_scan(k):
                            pe.wait_ge(sz_done, 2 * k + n + 1)
                        else:
                            pe.wait_ge(silu_done, NT * i + n - 1)
                        product(wide[n % 2][:, 0:T], [([w[:, m, n * P:(n + 1) * P] for w in f1], [v[:, m, :] for v in fT])
                                                      for m in range(KM)]).then_inc(fc1_done, 1)
                    if has_scan(k) and n == 2:
                        spread(k, q, 1, 1)
                if has_scan(k):
                    scan_products(k, 1)
                if has_next(k):
                    pe.wait_ge(u_done, at(2 * j + 2))
                    if has_scan(k):
                        pe.wait_ge(xtm_done, at(2 * k + 2))
                    turn_pair(trb, u).then_inc(uT_done, 1)
                if has_scan(k):
                    state_product(k, 1)
                if has_prev(k):
                    if has_scan(k):
                        pe.wait_ge(h2_stats, at(8 * k + 1))
                    else:
                        pe.wait_ge(out_ready, 2 * i)
                    fc2(i, 0, range(HALF))
                if has_next(k):
                    if k == -1:
                        pe.wait_ge(w_lo, FIRST_PART[7])
                    pe.wait_ge(uT_lo, at(j + 1))
                    channels(k, j, 0)
                    channels(k, j, 1)
                if has_scan(k):
                    if has_next(k):
                        pe.wait_ge(uT_lo, at(j + 1))
                    else:
                        pe.wait_ge(xtm_done, 2 * k + 2)
                    turn_y(k, 1)
                if has_next(k):
                    if k == -1:
                        pe.wait_ge(w_lo, FIRST_PART[8])
                    wait(pe, scan_done, 4 * j)
                    product(bcb[0:NH, 0:T], [([w[:, m, E_ALL - NH:E_ALL] for w in win], [v[:, m, :] for v in uT])
                                             for m in range(KM)]).then_inc(dt_done, 1)
                    if k == -1:
                        beta_share(0)
                        beta_share(1)
                    channels(k, j, 2)
                    channels(k, j, 3)
                if has_prev(k):
                    fc2(i, 0, range(HALF, NT))
                if has_next(k):
                    channels(k, j, 4)
                    channels(k, j, 5)
                    pe.wait_ge(dt_vec, at(4 * j + 1))
                    passed(pe)
                    for c in range(2):
                        last = pe.transpose(bcb[:, T + c * NH:T + (c + 1) * NH], dtr[:, c * P:(c + 1) * P],
                                            ident[0:NH, 0:NH])
                    last.then_inc(dtT_done, 1)
                    for c in range(2):
                        pe.wait_ge(tap0_done, at(NCV * j + NCV + c - 1))
                        product(wide[c][:, :], [([v[:, m, c * P:(c + 1) * P] for v in uT], [w[:, m, 0:DI] for w in win])
                                                for m in range(KM)]).then_inc(z_done, 1)
                    if k == -1:
                        beta_share(2)
                if has_scan(k):
                    if has_prev(k):
                        pe.wait_ge(out_ready, at(2 * i + 1))
                    else:
                        pe.wait_ge(h2_stats, 1)
                    out_proj(k, 1)
                if k == TILES:
                    pe.wait_ge(out_ready, 2 * i + 1)
                    fc2(i, 1)

            pe.wait_ge(ident_ready, 9)
            pe.wait_ge(w_lo, FIRST_PART[2])
            steps(pe, step)

        @block.vector
        def _(dve):
            def dequantise(n):
                o = IN_FC.index(n)
                dve.wait_ge(*load_count(n))
                dve.wait_ge(scale_loaded[o % FC_SLOTS], 16 * (o // FC_SLOTS + 1))
                dve.scalar_tensor_tensor(out=stage[n], in0=stage[n].bitcast(I32), scalar=-128.0,
                                         in1=scale_stage[o % FC_SLOTS], op0=ALU.add, op1=ALU.mult).then_inc(dequant, 1)

            def split_load(n):
                kind, i = LOADS[n]
                for p, (hi, lo) in enumerate(parts(kind, i)):
                    dve.wait_ge(w_hi, FIRST_PART[n] + p + 1)
                    dve.scalar_tensor_tensor(out=lo, in0=part_source(n, p), scalar=part_scale(n, p), in1=hi,
                                             op0=ALU.mult, op1=ALU.subtract).then_inc(w_lo, 1)

            def fc1_bias_sum():
                dve.wait_ge(beta_product, 4)
                dve.tensor_tensor(fcb_part[:, :], fcb_raw[:, :], yxb[:, 0:NT], ALU.add).then_inc(fcb_ready, 1)
                dve.wait_ge(fcb_ready, 1)
                dve.tensor_tensor(fcb[:, :], fcb_part[:, :], yxb[:, NT:2 * NT], ALU.add).then_inc(fcb_ready, 1)

            def hidden_lo(j, n, full, hi_done, lo_done):
                dve.wait_ge(hi_done, at(NT * j + n + 1))
                dve.tensor_tensor(hid[1][:, n, :], full[:, n % RING, :], hid[0][:, n, :],
                                  ALU.subtract).then_inc(lo_done, 1)

            def scan(k, c, half):
                g, hs = 2 * k + c, slice(4 * half, 4 * half + 4)
                dve.wait_ge(bcast_done, at(2 * g + half + 1))
                if half == 0:
                    wait(dve, yintra_done, g)
                    wait(dve, xw_done, g)
                dve.tensor_tensor_scan(dmat[:, hs, :].rearrange("p h t -> p (h t)"), bcb[:, :],
                                       ident4[:, :, :].rearrange("p h t -> p (h t)"), 0.0,
                                       ALU.mult, ALU.add).then_inc(scan_done, 1)

            def keep_last(k, c, half):
                g, hs = 2 * k + c, slice(4 * half, 4 * half + 4)
                dve.wait_ge(scan_done, at(2 * g + half + 1))
                dve.tensor_copy(dlast[:, hs], dmat[:, hs, P - 1]).then_inc(dlast_done, 1)

            def mask(k, c, half):
                g, hs = 2 * k + c, slice(4 * half, 4 * half + 4)
                dve.wait_ge(dlast_done, at(2 * g + half + 1))
                dve.wait_ge(bc_done, at(g + 1))
                dve.tensor_tensor(dmat[:, hs, :], dmat[:, hs, :], dsb[:, 0:P].unsqueeze(1).to_broadcast([P, 4, P]),
                                  ALU.mult).then_inc(mask_done, 1)

            def y_lo(k, c):
                dve.wait_ge(yT_hi, at(2 * k + c + 1))
                dve.tensor_tensor(yT[1][:, :, :], trb[:, :].rearrange("p (k t) -> p k t", t=P), yT[0][:, :, :],
                                  ALU.subtract).then_inc(yT_lo, 1)

            def from_state(k, q, c):
                g, par = 2 * k + c, q % 2
                dve.wait_ge(yinter_done, at(g + 1))
                dve.wait_ge(pp_done, at(k + 1))
                wait(dve, yT_done, g - 1)
                wait(dve, sq_done, g - 1)
                dve.tensor_tensor(heads(yb[:, c, :]), heads(yxb[:, :]), per_head(pp[:, par, 0, c, :]),
                                  ALU.mult).then_inc(ya_done, 1)

            def own_part(k, c):
                g = 2 * k + c
                dve.wait_ge(skip_added, at(g + 1))
                dve.wait_ge(yintra_done, at(g + 1))
                dve.tensor_tensor(yb[:, c, :], yb[:, c, :], yib[:, :], ALU.add).then_inc(yb_done, 1)

            def gate(k, c):
                g = 2 * k + c
                dve.wait_ge(yb_done, at(g + 1))
                dve.wait_ge(sz_done, at(g + 1))
                dve.tensor_tensor(yb[:, c, :], yb[:, c, :], sz[:, c, :], ALU.mult).then_inc(gated, 1)

            def state(k, q, c):
                g = 2 * k + c
                dve.wait_ge(s_decayed, at(g + 1))
                dve.wait_ge(ds_done, at(g + 1))
                if q == PER_B - 1 and c == 1:
                    dve.memset(S[:, :], 0.0).then_inc(s_done, 1)
                else:
                    dve.tensor_tensor(S[:, :], S[:, :], dsb[:, :], ALU.add).then_inc(s_done, 1)

            def moments(*rows):
                for src, which, c, s, base in rows:
                    if which in (0, 2):
                        dve.wait_ge(s, at(base))
                    dve.bn_stats(st[:, which, :], src).then_inc(s, 1)
                for src, which, c, s, base in rows:
                    dve.wait_ge(s, at(base + 1))
                    passed(dve)
                    dve.bn_aggr(mv[:, which, c, :], st[:, which, :]).then_inc(s, 1)
                for src, which, c, s, base in rows:
                    dve.wait_ge(s, at(base + 2))
                    dve.tensor_scalar(veps[:, which, c:c + 1], mv[:, which, c, 1:2], EPS, None, ALU.add).then_inc(s, 1)

            def normalise(dst, src, which, c):
                return dve.tensor_scalar(dst, src, mv[:, which, c, 0:1], rstd[:, which, c:c + 1],
                                         ALU.subtract, ALU.mult)

            def mean_square(k, c):
                g = 2 * k + c
                dve.wait_ge(sq_done, at(g + 1))
                dve.tensor_scalar(msq[:, c:c + 1], ssum[:, c:c + 1], 1.0 / DI, EPS, ALU.mult, ALU.add).then_inc(msq_done, 1)

            def make_h2(k, q, c):
                g = 2 * k + c
                dve.wait_ge(yr_done, at(g + 1))
                dve.wait_ge(outp_done, at(g + 1))
                wait(dve, res_steps, 2 * g - 3)
                dve.scalar_tensor_tensor(out=h2[:, c, :], in0=tmb[:, 0:DM], scalar=yr[:, c:c + 1],
                                         in1=h1[:, q % 2, c, :], op0=ALU.mult, op1=ALU.add).then_inc(h2_stats, 1)

            def rows_h2(k, c):
                return h2[:, c, :], 2, c, h2_stats, 4 * (2 * k + c) + 1

            def make_x3(k, c):
                g = 2 * k + c
                dve.wait_ge(pow_h2, at(g + 1))
                wait(dve, res_steps, 2 * g - 3)
                normalise(x3[:, c, :], h2[:, c, :], 2, c).then_inc(x3_done, 1)

            def rows_x3(k, c):
                dve.wait_ge(x3_done, at(2 * k + c + 1))
                return x3[:, c, :], 3, c, x3_stats, 3 * (2 * k + c)

            def norm_f(k, c):
                g = 2 * k + c
                dve.wait_ge(pow_x3, at(g + 1))
                wait(dve, fT_done, k)
                normalise(f[:, c, :], x3[:, c, :], 3, c).then_inc(f_done, 1)

            def make_y(j, c):
                g = 2 * j + c
                dve.wait_ge(tok2_done, at(g + 1))
                wait(dve, h1_done, g - 1)
                dve.tensor_tensor(ytok[:, c, :], tmb[:, 0:DM], b2r[:, :], ALU.add).then_inc(y_stats, 1)

            def rows_y(j, c):
                return ytok[:, c, :], 0, c, y_stats, 5 * (2 * j + c) + 1

            def centre_y(j, c):
                dve.scalar_tensor_tensor(out=ytok[:, c, :], in0=ytok[:, c, :], scalar=mv[:, 0, c, 0:1],
                                         in1=gam[:, :], op0=ALU.subtract, op1=ALU.mult).then_inc(y_stats, 1)

            def make_h1(j, q, c):
                g = 2 * j + c
                dve.wait_ge(y_stats, at(5 * g + 5))
                dve.wait_ge(pow_y, at(g + 1))
                wait(dve, h2_stats, 4 * (g - 4) + 1)
                dve.scalar_tensor_tensor(out=h1[:, q % 2, c, :], in0=ytok[:, c, :], scalar=rstd[:, 0, c:c + 1],
                                         in1=bet[:, :], op0=ALU.mult, op1=ALU.add).then_inc(h1_done, 1)

            def rows_h1(j, q, c):
                dve.wait_ge(h1_done, at(2 * j + c + 1))
                return h1[:, q % 2, c, :], 1, c, h1_stats, 3 * (2 * j + c)

            def norm_u(j, q, c):
                g = 2 * j + c
                dve.wait_ge(pow_h1, at(g + 1))
                wait(dve, uT_done, j)
                normalise(u[:, c, :], h1[:, q % 2, c, :], 1, c).then_inc(u_done, 1)

            def step(k, q):
                j, i = k + 1, k - 1
                for n in range(NT):
                    if has_scan(k) and n == NT - 1:
                        from_state(k, q, 0)
                    if has_older(k) and n == 0:
                        output(k - 2, q - 2, 1)
                    if has_scan(k) and n == 0:
                        scan(k, 0, 0)
                        keep_last(k, 0, 0)
                    if has_next(k):
                        hidden_lo(j, n, hfull, tok_hi, tok_lo)
                    if has_scan(k):
                        if n == 1:
                            mask(k, 0, 0)
                        if n == 2:
                            multiply_up(k)
                        if n == 3:
                            scan(k, 0, 1)
                            keep_last(k, 0, 1)
                        if n == 4:
                            mask(k, 0, 1)
                        if n == 6:
                            keep_products(k, q)
                    if has_prev(k) and n == 5:
                        norm_f(i, 1)
                    if k == -1 and n in (3, 6):
                        split_load(1 + n // 3)
                    if k == 0 and n in (1, 4, 5):
                        dequantise(IN_FC[{1: 3, 4: 4, 5: 5}[n]])
                    if k == 0 and n in (3, 6, 7):
                        split_load(IN_FC[{3: 3, 6: 4, 7: 5}[n]])
                    if k == 0 and n == 4:
                        fc1_bias_sum()
                if k == -1:
                    split_load(TURNED[0])
                    dve.wait_ge(tok_const_loaded, 16 * len(TOK_CONSTS))
                if has_scan(k):
                    own_part(k, 0)
                    gate(k, 0)
                    state(k, q, 0)
                if has_next(k):
                    make_y(j, 0)
                    moments(rows_y(j, 0))
                    centre_y(j, 0)
                if k == -1:
                    split_load(TURNED[1])
                if has_scan(k):
                    mean_square(k, 0)
                    y_lo(k, 0)
                if has_prev(k):
                    dve.wait_ge(fT_hi, at(i + 1))
                    dve.tensor_tensor(fT[1][:, :, :], yxb[:, :].rearrange("p (k t) -> p k t", t=T), fT[0][:, :, :],
                                      ALU.subtract).then_inc(fT_lo, 1)
                if has_next(k):
                    make_h1(j, q + 1, 0)
                    make_y(j, 1)
                    moments(rows_h1(j, q + 1, 0), rows_y(j, 1))
                    centre_y(j, 1)
                if k == -1:
                    split_load(TURNED[2])
                if has_scan(k):
                    scan(k, 1, 0)
                    keep_last(k, 1, 0)
                if has_next(k):
                    make_h1(j, q + 1, 1)
                if has_scan(k):
                    mask(k, 1, 0)
                    make_h2(k, q, 0)
                rows = []
                if has_next(k):
                    rows.append(rows_h1(j, q + 1, 1))
                if has_scan(k):
                    rows.append(rows_h2(k, 0))
                moments(*rows)
                if k == -1:
                    dve.wait_ge(const_loaded, 16 * len(CONSTS))
                    split_load(TURNED[3])
                if k == 0:
                    dve.tensor_scalar(fb2[:, :], fb2[:, :], 0.5, None, ALU.mult).then_inc(const_ready, 1)
                for n in range(NT):
                    if has_scan(k) and n == NT - 1:
                        from_state(k, q, 1)
                    if has_prev(k):
                        hidden_lo(i, n, ffull, fc_hi, fc_lo)
                    if has_next(k) and n in (1, 4):
                        norm_u(j, q + 1, n // 4)
                    if has_scan(k) and n == 2:
                        scan(k, 1, 1)
                        keep_last(k, 1, 1)
                    if has_scan(k) and n == 3:
                        mask(k, 1, 1)
                    if k == 0 and n == 4:
                        for m in IN_FC[6:]:
                            dequantise(m)
                        for m in IN_FC[6:]:
                            split_load(m)
                    if has_scan(k) and n == 5:
                        make_x3(k, 0)
                        moments(rows_x3(k, 0))
                if has_next(k):
                    dve.wait_ge(uT_hi, at(j + 1))
                    dve.tensor_tensor(uT[1][:, :, :], trb[:, :].rearrange("p (k t) -> p k t", t=T), uT[0][:, :, :],
                                      ALU.subtract).then_inc(uT_lo, 1)
                if has_scan(k):
                    own_part(k, 1)
                    gate(k, 1)
                    state(k, q, 1)
                    norm_f(k, 0)
                if k == -1:
                    dequantise(IN_FC[0])
                    dequantise(IN_FC[1])
                if has_next(k):
                    convolve(j, 0)
                    if k == -1:
                        split_load(IN_FC[0])
                if has_scan(k):
                    mean_square(k, 1)
                if has_next(k):
                    step_bias(j)
                    convolve(j, 2)
                if has_scan(k):
                    y_lo(k, 1)
                if has_prev(k):
                    output(i, q - 1, 0)
                if k == -1:
                    split_load(IN_FC[1])
                    dequantise(IN_FC[2])
                if has_next(k):
                    convolve(j, 4)
                if has_scan(k):
                    make_h2(k, q, 1)
                    moments(rows_h2(k, 1))
                if k == -1:
                    split_load(IN_FC[2])
                if has_next(k):
                    time_steps(j, q + 1)
                if k == TILES:
                    output(i, q - 1, 1)
                if has_next(k):
                    decays(j, q + 1)
                if has_scan(k):
                    make_x3(k, 1)
                    moments(rows_x3(k, 1))

            def output(i, q, c):
                dve.wait_ge(fc2_done, at(2 * i + c + 1))
                dve.wait_ge(res_steps, at(4 * i + 2 * c + 2))
                wait(dve, out_stored[c], 16 * i)
                dve.tensor_tensor(ob[:, c, :], tmb[:, 0:DM], res[:, q % 2, c, :], ALU.add).then_inc(out_ready, 1)

            def convolve(j, n):
                seq = 3 * (NCV * j + n)
                for t in range(1, TAPS):
                    for m in (n, n + 1):
                        if t == 1:
                            dve.wait_ge(tap0_done, at(NCV * j + m + 1))
                            dve.wait_ge(raw_done, at(NCV * j + m + 1))
                        else:
                            dve.wait_ge(taps, at(seq + 2 * (t - 2) + (m - n) + 1))
                        o = HALO - t
                        dve.scalar_tensor_tensor(out=acc[:, m, :], in0=raw[:, m, o:o + T],
                                                 scalar=cw[:, m, HALO - t:HALO - t + 1], in1=acc[:, m, :],
                                                 op0=ALU.mult, op1=ALU.add).then_inc(taps, 1)

            def step_bias(j):
                dve.wait_ge(dt_done, at(j + 1))
                dve.tensor_scalar(dtr[:, :], bcb[0:NH, 0:T], dtb[:, 0:1], None, ALU.add).then_inc(dt_vec, 1)

            def time_steps(j, q):
                par = q % 2
                dve.wait_ge(dtT_done, at(j + 1))
                dve.wait_ge(dt_act, at(4 * j + 3))
                dve.scalar_tensor_tensor(out=dtt[:, par, :, :], in0=turned_dt, scalar=0.0, in1=dln[:, :, :],
                                         op0=ALU.max, op1=ALU.add).then_inc(dt_vec, 1)
                if j == 0:
                    dve.wait_ge(expa_ready, 1)
                dve.wait_ge(dt_vec, at(4 * j + 2))
                dve.tensor_tensor(da[:, :, :], dtt[:, par, :, :], expa[:, :, :], ALU.mult).then_inc(dt_vec, 1)

            def decays(j, q):
                par = q % 2
                dve.wait_ge(dt_act, at(4 * j + 4))
                dve.tensor_scalar(decz[:, par, :, :], dec[:, :, :], notfirst[:, 0:1], None,
                                  ALU.mult).then_inc(dt_vec, 1)

            def multiply_up(k):
                dve.wait_ge(decT_done, at(k + 1))
                dve.tensor_tensor_scan(pT[:, :], tmb[0:2 * NH, 0:P], zeros[0:2 * NH, :], 1.0, ALU.mult,
                                       ALU.add).then_inc(pT_done, 1)

            def keep_products(k, q):
                dve.wait_ge(ppT_done, at(k + 1))
                dve.tensor_copy(pp[:, q % 2, :, :, :].rearrange("p a c h -> p (a c h)"),
                                tmb[:, P:P + 4 * NH]).then_inc(pp_done, 1)

            split_load(0)
            split_load(1)
            steps(dve, step)


_INS = ['x', 'L0_tok_w1', 'L0_tok_b1', 'L0_tok_w2', 'L0_tok_b2', 'L0_tok_gamma', 'L0_tok_beta',
        'L0_attn_in_proj_w', 'L0_attn_conv_w', 'L0_attn_conv_b', 'L0_attn_norm_w', 'L0_attn_out_proj_w',
        'L0_attn_dt_bias', 'L0_attn_A_log', 'L0_attn_D_param', 'L0_ffn_ln_gamma', 'L0_ffn_ln_beta',
        'L0_ffn_fc1_q', 'L0_ffn_fc1_scales', 'L0_ffn_fc1_bias', 'L0_ffn_fc2_q', 'L0_ffn_fc2_scales',
        'L0_ffn_fc2_bias']
_OUTS = [((8, 1024, 256), 'float32')]


def kernel(**inputs):
    import numpy as _np
    import concourse.bacc as _bacc
    from concourse import mybir as _mybir
    from concourse.bass_utils import run_bass_kernel_spmd as _run

    nc = _bacc.Bacc("TRN2", target_bir_lowering=False, num_devices=1)
    arrays, args = {}, []
    for name in _INS:
        a = _np.ascontiguousarray(inputs[name])
        arrays[f"in_{name}_dram"] = a
        args.append(nc.dram_tensor(f"in_{name}_dram", a.shape, _mybir.dt.from_np(a.dtype), kind="ExternalInput").ap())
    for i, (shape, dtype) in enumerate(_OUTS):
        dt = _mybir.dt.from_np(_np.dtype(dtype))
        args.append(nc.dram_tensor(f"out_{i}_dram", shape, dt, kind="ExternalOutput").ap())
    vit_tower(nc, *args)
    r = _run(nc, [arrays], core_ids=[0])
    got = tuple(r.results[0][f"out_{i}_dram"] for i in range(len(_OUTS)))
    return got[0]
```
